# Optimizing a Trainium2 kernel written in Bass

```python
import numpy as np
import jax
import jax.numpy as jnp

def _softmax(x, axis=-1):
    return jax.nn.softmax(x, axis=axis)

def _gelu(x):
    return jax.nn.gelu(x, approximate=True)

def _silu(x):
    return jax.nn.silu(x)

def _sigmoid(x):
    return jax.nn.sigmoid(x)

def _layernorm(x, axis=-1, eps=1e-05):
    m = jnp.mean(x, axis=axis, keepdims=True)
    v = jnp.var(x, axis=axis, keepdims=True)
    return (x - m) / jnp.sqrt(v + eps)

def _scatter_add(tgt, idx, src, axis=0):
    return tgt.at[idx].add(src)

def _segment_sum(src, seg, n):
    return jax.ops.segment_sum(src, seg, n)
kernel_name = 'mk_seq_preln_d2_jaxref_r8_ac3727'

def setup_inputs(seed: int=0):
    np.random.seed(seed)
    _w = jnp.asarray

    def _L0_attn_setup():
        import jax, jax.numpy as jnp
        import numpy as np
        D_MODEL = 128
        N_HEADS = 16
        LATENT_HEADS = 8
        LATENT_DIM = 64
        N_LATENTS = 64
        WINDOW = 32
        HEAD_DIM = D_MODEL // N_HEADS
        LAT_HD = LATENT_DIM // LATENT_HEADS
        B, S = (2, 512)

        def _pool_to_latents(x):
            Bx, Sx, C = x.shape
            chunk = max(1, Sx // N_LATENTS)
            return x.reshape(Bx, N_LATENTS, chunk, C).mean(axis=2)

        def _local_window_attn(Q, K, V):
            Bx, H, Sx, D = Q.shape
            W = WINDOW
            nb = Sx // W
            Qb = Q.reshape(Bx, H, nb, W, D)
            Kp = jnp.pad(K, ((0, 0), (0, 0), (W, 0), (0, 0))).reshape(Bx, H, nb + 1, W, D)
            Vp = jnp.pad(V, ((0, 0), (0, 0), (W, 0), (0, 0))).reshape(Bx, H, nb + 1, W, D)
            Kw = jnp.concatenate([Kp[:, :, :-1], Kp[:, :, 1:]], axis=3)
            Vw = jnp.concatenate([Vp[:, :, :-1], Vp[:, :, 1:]], axis=3)
            i = jnp.arange(W)[:, None]
            j = jnp.arange(2 * W)[None, :]
            base = (j > i) & (j <= i + W)
            blk0 = (jnp.arange(nb) > 0)[:, None, None] | (j >= W)[None, :, :]
            mask = base[None, :, :] & blk0
            sc = jnp.einsum('bhnid,bhnjd->bhnij', Qb, Kw) / np.sqrt(D).astype(np.float32)
            sc = jnp.where(mask[None, None], sc, -jnp.inf)
            p = jax.nn.softmax(sc, axis=-1)
            out = jnp.einsum('bhnij,bhnjd->bhnid', p, Vw)
            return out.reshape(Bx, H, Sx, D)
        key = jax.random.key(seed)
        ks = jax.random.split(key, 11)
        std = 0.02
        w = lambda k, shp: jax.random.normal(k, shp, jnp.float32) * std
        return {'x': jax.random.normal(ks[0], (B, S, D_MODEL), jnp.float32), 'wq': w(ks[1], (D_MODEL, D_MODEL)), 'wk': w(ks[2], (D_MODEL, D_MODEL)), 'wv': w(ks[3], (D_MODEL, D_MODEL)), 'wgq': w(ks[4], (D_MODEL, LATENT_DIM)), 'wgk': w(ks[5], (D_MODEL, LATENT_DIM)), 'wgv': w(ks[6], (D_MODEL, LATENT_DIM)), 'r_out_w': w(ks[7], (LATENT_DIM, D_MODEL)), 'gate_local_w': w(ks[8], (N_HEADS, HEAD_DIM)), 'gate_remote_w': w(ks[9], (N_HEADS, HEAD_DIM)), 'w_out': w(ks[10], (D_MODEL, D_MODEL))}
    _L0_attn_in = _L0_attn_setup()

    def _L0_ffn_setup():
        import jax, jax.numpy as jnp
        import numpy as np
        FEATURES = 128
        D_IN = 128

        def fp8_gemm_optimized(x, input_scale, kernel, kernel_scale):
            s_in = input_scale[0]
            s_k = kernel_scale[0]
            x_q = (x.astype(jnp.float32) / s_in).astype(jnp.float8_e4m3fn)
            k_q = (kernel.astype(jnp.float32) / s_k).astype(jnp.float8_e4m3fn)
            y = jnp.dot(x_q.astype(jnp.float32), k_q.astype(jnp.float32), preferred_element_type=jnp.float32)
            return y * (s_in * s_k)
        key = jax.random.key(seed)
        kx, kk, kb = jax.random.split(key, 3)
        x = jax.random.normal(kx, (4, 1024, D_IN), dtype=jnp.float32)
        limit = np.sqrt(6.0 / (D_IN + FEATURES)).astype(np.float32)
        kernel = jax.random.uniform(kk, (D_IN, FEATURES), dtype=jnp.float32, minval=-limit, maxval=limit).astype(jnp.bfloat16)
        input_scale = jnp.ones((1,), dtype=jnp.float32)
        kernel_scale = jnp.ones((1,), dtype=jnp.float32)
        bias = jnp.zeros((FEATURES,), dtype=jnp.bfloat16)
        return {'x': x, 'kernel': kernel, 'input_scale': input_scale, 'kernel_scale': kernel_scale, 'bias': bias}
    _L0_ffn_in = _L0_ffn_setup()

    def _L1_attn_setup():
        import jax, jax.numpy as jnp
        import numpy as np
        DIM = 128
        key = jax.random.key(seed)
        ks = jax.random.split(key, 10)
        d = DIM
        return {'x': jax.random.normal(ks[0], (8, 512, d), dtype=jnp.float32), 'A': jax.random.normal(ks[1], (d, d), dtype=jnp.float32) * 0.1, 'B': jax.random.normal(ks[2], (d, d), dtype=jnp.float32) * 0.1, 'W_in': jax.random.normal(ks[3], (d, d), dtype=jnp.float32) * (1.0 / np.sqrt(d)), 'b_in': jax.random.normal(ks[4], (d,), dtype=jnp.float32) * 0.01, 'W_gate': jax.random.normal(ks[5], (d, d), dtype=jnp.float32) * (1.0 / np.sqrt(d)), 'b_gate': jax.random.normal(ks[6], (d,), dtype=jnp.float32) * 0.01, 'W_out': jax.random.normal(ks[7], (d, d), dtype=jnp.float32) * (1.0 / np.sqrt(d)), 'b_out': jax.random.normal(ks[8], (d,), dtype=jnp.float32) * 0.01}
    _L1_attn_in = _L1_attn_setup()

    def _L1_ffn_setup():
        import jax, jax.numpy as jnp
        import numpy as np
        E, D, DFF = (8, 128, 512)
        key = jax.random.key(seed)
        ks = jax.random.split(key, 10)
        s = 0.02
        return {'x': jax.random.normal(ks[0], (4, 256, D), dtype=jnp.float32), 'Wr': jax.random.normal(ks[1], (D, E), dtype=jnp.float32) * s, 'br': jnp.zeros((E,), dtype=jnp.float32), 'W1': jax.random.normal(ks[2], (E, D, DFF), dtype=jnp.float32) * s, 'b1': jnp.zeros((E, DFF), dtype=jnp.float32), 'W2': jax.random.normal(ks[3], (E, D, DFF), dtype=jnp.float32) * s, 'b2': jnp.zeros((E, DFF), dtype=jnp.float32), 'W3': jax.random.normal(ks[4], (E, DFF, D), dtype=jnp.float32) * s, 'b3': jnp.zeros((E, D), dtype=jnp.float32)}
    _L1_ffn_in = _L1_ffn_setup()
    _d = {'L0_attn_x': _L0_attn_in['x'], 'L0_attn_wq': _L0_attn_in['wq'], 'L0_attn_wk': _L0_attn_in['wk'], 'L0_attn_wv': _L0_attn_in['wv'], 'L0_attn_wgq': _L0_attn_in['wgq'], 'L0_attn_wgk': _L0_attn_in['wgk'], 'L0_attn_wgv': _L0_attn_in['wgv'], 'L0_attn_r_out_w': _L0_attn_in['r_out_w'], 'L0_attn_gate_local_w': _L0_attn_in['gate_local_w'], 'L0_attn_gate_remote_w': _L0_attn_in['gate_remote_w'], 'L0_attn_w_out': _L0_attn_in['w_out'], 'L0_ffn_kernel': _L0_ffn_in['kernel'], 'L0_ffn_input_scale': _L0_ffn_in['input_scale'], 'L0_ffn_kernel_scale': _L0_ffn_in['kernel_scale'], 'L0_ffn_bias': _L0_ffn_in['bias'], 'L1_attn_A': _L1_attn_in['A'], 'L1_attn_B': _L1_attn_in['B'], 'L1_attn_W_in': _L1_attn_in['W_in'], 'L1_attn_b_in': _L1_attn_in['b_in'], 'L1_attn_W_gate': _L1_attn_in['W_gate'], 'L1_attn_b_gate': _L1_attn_in['b_gate'], 'L1_attn_W_out': _L1_attn_in['W_out'], 'L1_attn_b_out': _L1_attn_in['b_out'], 'L1_ffn_Wr': _L1_ffn_in['Wr'], 'L1_ffn_br': _L1_ffn_in['br'], 'L1_ffn_W1': _L1_ffn_in['W1'], 'L1_ffn_b1': _L1_ffn_in['b1'], 'L1_ffn_W2': _L1_ffn_in['W2'], 'L1_ffn_b2': _L1_ffn_in['b2'], 'L1_ffn_W3': _L1_ffn_in['W3'], 'L1_ffn_b3': _L1_ffn_in['b3']}
    _x0 = _d['L0_attn_x']
    _d['L0_attn_x'] = jax.random.normal(jax.random.fold_in(jax.random.key(seed), 1), (8, 1024, 128), dtype=_x0.dtype)
    del _x0
    return _d

def reference(L0_attn_x, L0_attn_wq, L0_attn_wk, L0_attn_wv, L0_attn_wgq, L0_attn_wgk, L0_attn_wgv, L0_attn_r_out_w, L0_attn_gate_local_w, L0_attn_gate_remote_w, L0_attn_w_out, L0_ffn_kernel, L0_ffn_input_scale, L0_ffn_kernel_scale, L0_ffn_bias, L1_attn_A, L1_attn_B, L1_attn_W_in, L1_attn_b_in, L1_attn_W_gate, L1_attn_b_gate, L1_attn_W_out, L1_attn_b_out, L1_ffn_Wr, L1_ffn_br, L1_ffn_W1, L1_ffn_b1, L1_ffn_W2, L1_ffn_b2, L1_ffn_W3, L1_ffn_b3):

    def _L0_attn_ref(x, wq, wk, wv, wgq, wgk, wgv, r_out_w, gate_local_w, gate_remote_w, w_out):
        import jax, jax.numpy as jnp
        import numpy as np
        D_MODEL = 128
        N_HEADS = 16
        LATENT_HEADS = 8
        LATENT_DIM = 64
        N_LATENTS = 64
        WINDOW = 32
        HEAD_DIM = D_MODEL // N_HEADS
        LAT_HD = LATENT_DIM // LATENT_HEADS
        B, S = (2, 512)

        def _pool_to_latents(x):
            Bx, Sx, C = x.shape
            chunk = max(1, Sx // N_LATENTS)
            return x.reshape(Bx, N_LATENTS, chunk, C).mean(axis=2)

        def _local_window_attn(Q, K, V):
            Bx, H, Sx, D = Q.shape
            W = WINDOW
            nb = Sx // W
            Qb = Q.reshape(Bx, H, nb, W, D)
            Kp = jnp.pad(K, ((0, 0), (0, 0), (W, 0), (0, 0))).reshape(Bx, H, nb + 1, W, D)
            Vp = jnp.pad(V, ((0, 0), (0, 0), (W, 0), (0, 0))).reshape(Bx, H, nb + 1, W, D)
            Kw = jnp.concatenate([Kp[:, :, :-1], Kp[:, :, 1:]], axis=3)
            Vw = jnp.concatenate([Vp[:, :, :-1], Vp[:, :, 1:]], axis=3)
            i = jnp.arange(W)[:, None]
            j = jnp.arange(2 * W)[None, :]
            base = (j > i) & (j <= i + W)
            blk0 = (jnp.arange(nb) > 0)[:, None, None] | (j >= W)[None, :, :]
            mask = base[None, :, :] & blk0
            sc = jnp.einsum('bhnid,bhnjd->bhnij', Qb, Kw) / np.sqrt(D).astype(np.float32)
            sc = jnp.where(mask[None, None], sc, -jnp.inf)
            p = jax.nn.softmax(sc, axis=-1)
            out = jnp.einsum('bhnij,bhnjd->bhnid', p, Vw)
            return out.reshape(Bx, H, Sx, D)
        Bx, Sx, _ = x.shape
        chunk = max(1, Sx // N_LATENTS)
        Q = (x @ wq).reshape(Bx, Sx, N_HEADS, HEAD_DIM).transpose(0, 2, 1, 3)
        K = (x @ wk).reshape(Bx, Sx, N_HEADS, HEAD_DIM).transpose(0, 2, 1, 3)
        V = (x @ wv).reshape(Bx, Sx, N_HEADS, HEAD_DIM).transpose(0, 2, 1, 3)
        local = _local_window_attn(Q, K, V)
        GQ = (x @ wgq).reshape(Bx, Sx, LATENT_HEADS, LAT_HD).transpose(0, 2, 1, 3)
        GK = _pool_to_latents(x @ wgk).reshape(Bx, N_LATENTS, LATENT_HEADS, LAT_HD).transpose(0, 2, 1, 3)
        GV = _pool_to_latents(x @ wgv).reshape(Bx, N_LATENTS, LATENT_HEADS, LAT_HD).transpose(0, 2, 1, 3)
        lsc = jnp.einsum('bhsd,bhnd->bhsn', GQ, GK) / np.sqrt(LAT_HD).astype(np.float32)
        lmask = jnp.arange(N_LATENTS)[None, :] <= (jnp.arange(Sx) // chunk)[:, None]
        lsc = jnp.where(lmask[None, None], lsc, -jnp.inf)
        lp = jax.nn.softmax(lsc, axis=-1)
        rem = jnp.einsum('bhsn,bhnd->bhsd', lp, GV)
        rem = rem.transpose(0, 2, 1, 3).reshape(Bx, Sx, LATENT_DIM) @ r_out_w
        rem = rem.reshape(Bx, Sx, N_HEADS, HEAD_DIM).transpose(0, 2, 1, 3)
        gl = jax.nn.sigmoid(jnp.einsum('bhsd,hd->bhs', Q, gate_local_w))[..., None]
        gr = jax.nn.sigmoid(jnp.einsum('bhsd,hd->bhs', Q, gate_remote_w))[..., None]
        out = gl * local + gr * rem
        out = out.transpose(0, 2, 1, 3).reshape(Bx, Sx, D_MODEL)
        return out @ w_out

    def _L0_ffn_ref(x, kernel, input_scale, kernel_scale, bias):
        import jax, jax.numpy as jnp
        import numpy as np
        FEATURES = 128
        D_IN = 128

        def fp8_gemm_optimized(x, input_scale, kernel, kernel_scale):
            s_in = input_scale[0]
            s_k = kernel_scale[0]
            x_q = (x.astype(jnp.float32) / s_in).astype(jnp.float8_e4m3fn)
            k_q = (kernel.astype(jnp.float32) / s_k).astype(jnp.float8_e4m3fn)
            y = jnp.dot(x_q.astype(jnp.float32), k_q.astype(jnp.float32), preferred_element_type=jnp.float32)
            return y * (s_in * s_k)
        dtype = jnp.bfloat16
        x = x.astype(dtype)
        orig_shape = x.shape
        x2 = x.reshape(-1, x.shape[-1])
        y = fp8_gemm_optimized(x2, input_scale, kernel, kernel_scale)
        y = y.astype(dtype) + bias
        return y.reshape(orig_shape[:-1] + (FEATURES,))

    def _L1_attn_ref(x, A, B, W_in, b_in, W_gate, b_gate, W_out, b_out):
        import jax, jax.numpy as jnp
        import numpy as np
        DIM = 128
        batch, seq, dim = x.shape
        inp = jnp.einsum('bsd,ed->bse', x, W_in) + b_in
        gate = jax.nn.sigmoid(jnp.einsum('bsd,ed->bse', inp, W_gate) + b_gate)
        u = jnp.einsum('bsd,ed->bse', inp, B)

        def step(state, t):
            inp_t, gate_t, u_t = t
            s = jnp.tanh(state @ A.T + u_t)
            s = gate_t * s + (1.0 - gate_t) * inp_t
            return (s, s)
        init = jnp.zeros((batch, dim), dtype=x.dtype)
        xs = (jnp.swapaxes(inp, 0, 1), jnp.swapaxes(gate, 0, 1), jnp.swapaxes(u, 0, 1))
        _, states = jax.lax.scan(step, init, xs)
        out = jnp.einsum('sbd,ed->sbe', states, W_out) + b_out
        return jnp.swapaxes(out, 0, 1)

    def _L1_ffn_ref(x, Wr, br, W1, b1, W2, b2, W3, b3):
        import jax, jax.numpy as jnp
        import numpy as np
        E, D, DFF = (8, 128, 512)
        b, s, d = x.shape
        xt = x.reshape(b * s, d)
        logits = xt @ Wr + br
        pr, idx = jax.lax.top_k(logits, 2)
        w = jax.nn.softmax(pr, axis=-1)
        onehot = jax.nn.one_hot(idx, W1.shape[0], dtype=x.dtype)
        cw = jnp.einsum('tk,tke->te', w, onehot)
        y = jnp.zeros_like(xt)
        for e in range(W1.shape[0]):
            h = jax.nn.silu(xt @ W1[e] + b1[e]) * (xt @ W2[e] + b2[e])
            y = y + (h @ W3[e] + b3[e]) * cw[:, e:e + 1]
        return y.reshape(b, s, d)
    x = L0_attn_x
    x = x + _L0_attn_ref(_layernorm(x, axis=-1), L0_attn_wq, L0_attn_wk, L0_attn_wv, L0_attn_wgq, L0_attn_wgk, L0_attn_wgv, L0_attn_r_out_w, L0_attn_gate_local_w, L0_attn_gate_remote_w, L0_attn_w_out)
    x = x + _L0_ffn_ref(_layernorm(x, axis=-1), L0_ffn_kernel, L0_ffn_input_scale, L0_ffn_kernel_scale, L0_ffn_bias)
    x = x + _L1_attn_ref(_layernorm(x, axis=-1), L1_attn_A, L1_attn_B, L1_attn_W_in, L1_attn_b_in, L1_attn_W_gate, L1_attn_b_gate, L1_attn_W_out, L1_attn_b_out)
    x = x + _L1_ffn_ref(_layernorm(x, axis=-1), L1_ffn_Wr, L1_ffn_br, L1_ffn_W1, L1_ffn_b1, L1_ffn_W2, L1_ffn_b2, L1_ffn_W3, L1_ffn_b3)
    return x

_drawn_inputs = setup_inputs


def setup_inputs(seed=0):
    import zlib

    import numpy as np

    out = dict(_drawn_inputs(seed))
    spreads = {'L0_ffn_bias': (0.0, 0.1),
     'L1_ffn_br': (0.0, 0.316),
     'L1_ffn_b1': (0.0, 0.8),
     'L1_ffn_b2': (0.0, 0.8),
     'L1_ffn_b3': (0.0, 0.791)}
    factors = {'L0_attn_wq': 8.0,
     'L0_attn_wk': 8.0,
     'L0_attn_wv': 5.052,
     'L0_attn_wgq': 8.0,
     'L0_attn_wgk': 8.0,
     'L0_attn_wgv': 8.0,
     'L0_attn_r_out_w': 8.0,
     'L0_attn_gate_local_w': 8.0,
     'L0_attn_gate_remote_w': 8.0,
     'L0_attn_w_out': 5.107,
     'L1_attn_b_in': 8.0,
     'L1_attn_b_gate': 8.0,
     'L1_attn_b_out': 8.0,
     'L1_ffn_W1': 8.0,
     'L1_ffn_W2': 8.0,
     'L1_ffn_W3': 8.0}
    for name, (base, spread) in spreads.items():
        noise = np.random.default_rng([zlib.crc32(name.encode()), seed]).standard_normal(out[name].shape)
        drawn = base * np.exp(spread * noise) if base else spread * noise
        out[name] = jnp.asarray(drawn.astype(out[name].dtype))
    for name, factor in factors.items():
        out[name] = (out[name] * factor).astype(out[name].dtype)
    return out
```

```python
from contextlib import ExitStack

import concourse.bass as bass
from concourse import mybir

F32 = mybir.dt.float32
BF16 = mybir.dt.bfloat16
F16 = mybir.dt.float16
U32 = mybir.dt.uint32
ALU = mybir.AluOpType
ACT = mybir.ActivationFunctionType
AX = mybir.AxisListType

P = 128
B, S, D = 8, 1024, 128
NJ = S // P
NU = NJ * B
H, HD = 16, 8
HG, HH = 4, 4
WIN = 32
NB = P // WIN
KW = 2 * WIN
XW = P + WIN
LH, LD, NL = 8, 64, 64
CHUNK = S // NL
E, DFF = 8, 512
NC4 = DFF // P
EPS = 1e-5
NEG = -1.0e30
ISQ = float(1.0 / (8.0 ** 0.5))
STEPS = 8
HALF = 4
N5 = HALF * P



WORK = 14592


class Cut:

    def __init__(self, area):
        self.area, self.at = area, 0

    def take(self, n, dt=F32):
        words = n if dt == F32 else (n + 1) // 2
        words += words % 2
        v = self.area[:, self.at:self.at + words]
        self.at += words
        assert self.at <= WORK, self.at
        return v if dt == F32 else v.bitcast(dt)


class Memory:
    pass


class Arrays:

    def __init__(self, aps):
        (self.x, self.wq, self.wk, self.wv, self.wgq, self.wgk, self.wgv, self.r_out_w, self.gate_local_w,
         self.gate_remote_w, self.w_out, self.f_kernel, self.f_sin, self.f_sk, self.f_bias, self.A, self.B,
         self.W_in, self.b_in, self.W_gate, self.b_gate, self.W_out, self.b_out, self.Wr, self.br, self.W1, self.b1,
         self.W2, self.b2, self.W3, self.b3) = aps


def lay_out(nc, ctx):
    def sb(name, shape, dt=F32):
        return ctx.enter_context(nc.sbuf_tensor(name, shape, dt))

    m = Memory()
    m.X = sb("X", [P, NU, D])
    m.xnT = sb("xnT", [P, NU + B, XW])
    m.mix = sb("mix", [P, NU, D])
    m.work = sb("work", [P, WORK])
    wflat = m.xnT[:, :, :].rearrange("p u x -> p (u x)").bitcast(F16)
    ef = E * DFF
    m.W1h, m.W1l, m.W2h, m.W2l = [wflat[:, n * ef:(n + 1) * ef].rearrange("p (e f) -> p e f", e=E) for n in range(4)]
    mflat = m.mix[:, :, :].rearrange("p u x -> p (u x)")
    m.Wst = mflat[:, 0:ef]
    m.W3s = mflat[:, ef:2 * ef].rearrange("p (e n) -> p e n", e=E)
    m.stats = sb("stats", [P, NU, 6])
    m.mv = sb("mv", [P, NU, 2])
    m.rstd = sb("rstd", [P, NU])
    m.nhalf = sb("nhalf", [P, NU])
    m.ident = sb("ident", [P, P])
    m.identb = sb("identb", [P, P], BF16)
    m.hm = sb("hm", [P, HH])
    m.par = sb("par", [P, 2])
    m.lhm = sb("lhm", [P, LH])
    m.m16 = sb("m16", [P, H])
    m.cmask = sb("cmask", [P, 2, NB, KW])
    m.wq = sb("wq", [P, D])
    m.wk = sb("wk", [P, D])
    m.wv = sb("wv", [P, D])
    m.wgq = sb("wgq", [P, LD])
    m.wgk = sb("wgk", [P, LD])
    m.wgv = sb("wgv", [P, LD])
    m.wout = sb("wout", [P, D])
    m.wr = sb("wr", [P, E])
    m.gbd = sb("gbd", [P, 2 * H])
    m.wg = sb("wg", [P, 2 * H])
    m.gcol = sb("gcol", [P, 2])
    m.bcol = sb("bcol", [P, 3])
    m.bout = sb("bout", [P, D])
    m.fsc = sb("fsc", [P, 5])
    m.br = sb("br", [P, E])
    m.iota8 = sb("iota8", [P, E])
    m.routp = sb("routp", [LD, D])
    m.w5T = sb("w5T", [P, 6, D])
    m.fk = sb("fk", [P, D], BF16)
    m.fkq = sb("fkq", [P, D], BF16)
    m.fbias = sb("fbias", [P, D], BF16)
    m.b12 = sb("b12", [P, 2, NC4, E])
    m.st4 = sb("st4", [P, B, 6])
    m.mv4 = sb("mv4", [P, B, 2])
    m.tick = sb("tick", [P, 2])
    m.rstd4 = sb("rstd4", [P, B])[:, :]
    m.gkbd = sb("gkbd", [LD, B, LH, NL])
    m.b3bd = m.gkbd[:, 0:2, :, :].rearrange("p b h n -> p (b h n)")
    m.gvx = sb("gvx", [P, B * NC4, 2, 9])
    m.glr = sb("glr", [P, NU, 2 * H])
    m.psum = ctx.enter_context(nc.psum_tensor("psum", [P, 8 * 512], F32))
    m.ps = [m.psum[:, 512 * n:512 * (n + 1)] for n in range(8)]
    return m


def setup(nc, ctx, m, a):
    s_w = ctx.enter_context(nc.semaphore("s_w"))
    s_const = ctx.enter_context(nc.semaphore("s_const"))
    s_dve = ctx.enter_context(nc.semaphore("s_setup_dve"))
    s_pe = ctx.enter_context(nc.semaphore("s_setup_pe"))
    m.s_x = [ctx.enter_context(nc.semaphore(f"s_x{j}")) for j in range(NJ)]
    loads = []
    c = Cut(m.work)
    m.raw5 = c.take(5 * D).rearrange("p (n d) -> p n d", n=5)
    m.b12r = c.take(2 * DFF)[0:E].rearrange("p (n d) -> p n d", n=2)
    m.rout = c.take(D)[0:LD]

    def ld(dst, src):
        loads.append((dst, src))

    def rowb(v):
        return v.rearrange("(o n) -> o n", o=1).broadcast_to([P, v.shape[0]])

    for dst, src in ((m.wq, a.wq), (m.wk, a.wk), (m.wv, a.wv), (m.wgq, a.wgq), (m.wgk, a.wgk), (m.wgv, a.wgv),
                     (m.rout, a.r_out_w), (m.fk, a.f_kernel), (m.wr, a.Wr)):
        ld(dst[:, :], src)
    wo_v = a.w_out.rearrange("(r g h d) n -> r h g d n", r=2, g=2, h=HH)
    for r in range(2):
        for h in range(HH):
            for g in range(2):
                at = 64 * r + 16 * h + 8 * g
                ld(m.wout[at:at + 8, :], wo_v[r, h, g])
    ld(m.gcol[:, 0:1], a.gate_local_w.rearrange("h (d o) -> (h d) o", o=1))
    ld(m.gcol[:, 1:2], a.gate_remote_w.rearrange("h (d o) -> (h d) o", o=1))
    for n, w in enumerate((a.A, a.B, a.W_in, a.W_gate, a.W_out)):
        ld(m.raw5[:, n, :], w)
    ld(m.bcol[:, 0:1], a.b_in.rearrange("(d o) -> d o", o=1))
    ld(m.bcol[:, 1:2], a.b_gate.rearrange("(d o) -> d o", o=1))
    ld(m.bout[:, :], rowb(a.b_out))
    ld(m.fbias[:, :], rowb(a.f_bias))
    ld(m.fsc[:, 0:1], rowb(a.f_sin))
    ld(m.fsc[:, 1:2], rowb(a.f_sk))
    ld(m.br[:, :], rowb(a.br))
    for n, b in enumerate((a.b1, a.b2)):
        ld(m.b12r[:, n, :], b)

    with nc.Block() as block:
        @block.sync
        def _(sp):
            for j in range(NJ):
                sp.dma_start(m.X[:, B * j:B * (j + 1), :],
                             a.x[:, P * j:P * (j + 1), :].rearrange("b p f -> p b f")).then_inc(m.s_x[j], 16)

        @block.scalar
        def _(act):
            for dst, src in loads:
                act.dma_start(dst, src).then_inc(s_w, 16)

        @block.gpsimd
        def _(e):
            done = [0]

            def step(ins):
                ins.then_inc(s_const, 1)
                done[0] += 1
                e.wait_ge(s_const, done[0])

            step(e.memset(m.ident[:, :], 0.0))
            step(e.affine_select(out=m.ident[:, :], in_=m.ident[:, :], compare_op=ALU.not_equal, fill=1.0, base=0,
                                 pattern=[[-1, P]], channel_multiplier=1))
            step(e.memset(m.gvx[:, :, :, :], 1.0))
            m.const_ident = done[0]
            step(e.memset(m.nhalf[:, :], -0.5))
            step(e.memset(m.xnT[:, 0:B, 0:WIN], 0.0))
            step(e.iota(m.iota8[:, :], pattern=[[1, E]], base=0, channel_multiplier=0,
                        allow_small_or_imprecise_dtypes=True))
            step(e.memset(m.cmask[:, :, :, :], 0.0))
            for q in range(HH):
                v = m.cmask[WIN * q:WIN * (q + 1), :, :, :].rearrange("p v b k -> p (v b) k")
                step(e.affine_select(out=v, in_=v, compare_op=ALU.is_ge, fill=NEG, base=-1,
                                     pattern=[[0, 2 * NB], [1, KW]], channel_multiplier=-1))
                step(e.affine_select(out=v, in_=v, compare_op=ALU.is_ge, fill=NEG, base=WIN,
                                     pattern=[[0, 2 * NB], [-1, KW]], channel_multiplier=1))
            step(e.affine_select(out=m.cmask[:, 1, 0, :], in_=m.cmask[:, 1, 0, :], compare_op=ALU.is_ge, fill=NEG,
                                 base=-WIN, pattern=[[1, KW]], channel_multiplier=0))

        @block.vector
        def _(e):
            done = [0]

            def step(ins):
                ins.then_inc(s_dve, 1)
                done[0] += 1
                e.wait_ge(s_dve, done[0])

            e.wait_ge(s_const, m.const_ident)
            step(e.tensor_reduce(m.hm[:, :], m.ident[:, :].rearrange("p (a h d) -> p h a d", a=HG, h=HH), axis=AX.XY, op=ALU.add))
            step(e.tensor_scalar(m.hm[:, :], m.hm[:, :], ISQ, None, ALU.mult))
            step(e.tensor_reduce(m.par[:, :], m.ident[:, :].rearrange("p (r k) -> p r k", r=2), axis=AX.X, op=ALU.add))
            step(e.tensor_reduce(m.lhm[:, :], m.ident[:, 0:LD].rearrange("p (h d) -> p h d", h=LH), axis=AX.X, op=ALU.add))
            step(e.tensor_scalar(m.lhm[:, :], m.lhm[:, :], 1.0 / CHUNK, None, ALU.mult))
            for r in range(2):
                for g in range(2):
                    step(e.tensor_reduce(m.m16[:, 8 * r + g:8 * r + 8:2],
                                         m.ident[:, 64 * r + 32 * g:64 * r + 32 * g + 32].rearrange("p (h d) -> p h d", h=HH),
                                         axis=AX.X, op=ALU.add))
            step(e.tensor_copy(m.identb[:, :], m.ident[:, :]))
            for g in range(2):
                step(e.tensor_scalar(m.gvx[:, :, g, 8], m.gvx[:, :, g, 8], m.par[:, g:g + 1], None, ALU.mult))
            e.wait_ge(s_w, 16 * len(loads))
            for n in range(2):
                step(e.tensor_scalar(m.gbd[:, H * n:H * (n + 1)], m.m16[:, :], m.gcol[:, n:n + 1], None, ALU.mult))
            step(e.tensor_scalar(m.wout[:, :], m.wout[:, :], 0.5, None, ALU.mult))
            step(e.tensor_scalar(m.bcol[:, 2:3], m.bcol[:, 1:2], 0.5, None, ALU.mult))
            for r in range(2):
                for g in range(2):
                    step(e.tensor_copy(m.routp[:, 64 * r:64 * r + 64].rearrange("p (h g d) -> p h g d", h=HH, g=2)[:, :, g, :],
                                       m.rout[:, 64 * r + 32 * g:64 * r + 32 * g + 32].rearrange("p (h d) -> p h d", h=HH)))
            step(e.reciprocal(m.fsc[:, 2:4], m.fsc[:, 0:2]))
            step(e.tensor_tensor(m.fsc[:, 4:5], m.fsc[:, 0:1], m.fsc[:, 1:2], ALU.mult))
            t, q, w = c.take(D), c.take(D), c.take(D)
            step(e.tensor_scalar(t, m.fk[:, :], m.fsc[:, 3:4], None, ALU.mult))
            round_e4m3fn(e, step, t, q, w)
            step(e.tensor_copy(m.fkq[:, :], q))
            e.wait_ge(s_pe, 1)
            step(e.tensor_copy(m.w5T[:, 0:4, :].rearrange("p n d -> p (n d)"), m.ps[0][:, :]))
            step(e.tensor_copy(m.w5T[:, 4:6, :].rearrange("p n d -> p (n d)"), m.ps[1][:, 0:256]))
            step(e.tensor_copy(m.b12[:, :, :, :].rearrange("p n j e -> p (n j e)"), m.ps[1][:, 256:256 + 2 * NC4 * E]))
            e.wait_ge(s_pe, 2)
            step(e.tensor_copy(m.wg[:, :], m.ps[2][:, 0:2 * H]))
            m.setup_steps = done[0]

        @block.tensor
        def _(e):
            e.wait_ge(s_const, m.const_ident)
            e.wait_ge(s_w, 16 * len(loads))
            for n in range(6):
                src = m.raw5[:, n, :] if n < 5 else m.wq[:, :]
                last = e.transpose(m.ps[n // 4][:, D * (n % 4):D * (n % 4) + D], src, m.ident[:, :])
            for n in range(2):
                for j in range(NC4):
                    last = e.transpose(m.ps[1][:, 256 + E * (NC4 * n + j):256 + E * (NC4 * n + j + 1)],
                                       m.b12r[:, n, P * j:P * (j + 1)], m.ident[0:E, 0:E])
            last.then_inc(s_pe, 1)
            e.wait_ge(s_dve, m.setup_steps - 1)
            e.matmul(m.ps[2][:, 0:2 * H], m.w5T[:, 5, :], m.gbd[:, :], start=True, stop=True).then_inc(s_pe, 1)


def round_e4m3fn(e, step, t, q, w):
    step(e.tensor_scalar(w.bitcast(U32), t.bitcast(U32), 0x7F800000, None, ALU.bitwise_and))
    step(e.tensor_scalar(w, w, 2.0 ** -6, 1.5 * 2.0 ** 20, ALU.max, ALU.mult))
    step(e.tensor_tensor(q, t, w, ALU.add))
    step(e.tensor_tensor(q, q, w, ALU.subtract))
    step(e.tensor_scalar(w.bitcast(U32), q.bitcast(U32), 0x7FFFFFFF, None, ALU.bitwise_and))
    step(e.tensor_scalar(w, w, 448.0, 448.0, ALU.max, ALU.subtract))
    step(e.tensor_scalar(w, w, 3.0e38, 0.0, ALU.mult, ALU.mult))
    step(e.tensor_tensor(q, q, w, ALU.add))


MOMENTS = 6


def moments(e, s_step, before, st, mean, ve):
    n = [0]

    def step(ins):
        ins.then_inc(s_step, 1)
        n[0] += 1
        e.wait_ge(s_step, before + n[0])

    m1, q1, m2, q2 = (st[:, :, k] for k in (1, 2, 4, 5))
    step(e.tensor_tensor(mean, m1, m2, ALU.subtract))
    step(e.scalar_tensor_tensor(ve, mean, 0.25, mean, ALU.mult, ALU.mult))
    step(e.tensor_tensor(q1, q1, q2, ALU.add))
    step(e.scalar_tensor_tensor(ve, q1, 1.0 / D, ve, ALU.mult, ALU.add))
    step(e.tensor_tensor(mean, m1, m2, ALU.add))
    e.tensor_scalar(mean, mean, 0.5, None, ALU.mult)
    step(e.tensor_scalar(ve, ve, EPS, None, ALU.add))
    assert n[0] == MOMENTS


def norm_all(nc, ctx, m, a):
    def sem(name):
        return ctx.enter_context(nc.semaphore(name))
    s_st, s_var, s_rs = sem("ln1_stats"), sem("ln1_var"), sem("ln1_rstd")
    s_xn, s_tr, s_cp, s_tail, s_pool = sem("ln1_normed"), sem("ln1_turned"), sem("ln1_stored"), sem("ln1_tails"), sem("ln1_pooled")
    s_lat, s_gk = sem("latents_made"), sem("latents_kept")
    c = Cut(m.work)
    xn = [c.take(B * D).rearrange("p (b d) -> p b d", b=B) for _ in range(2)]
    m.pool = c.take(B * NL).rearrange("p (b n) -> p b n", b=B)
    pool2 = c.take(B * 2 * NL).rearrange("p (b o n) -> p b o n", b=B, o=2)

    with nc.Block() as block:
        @block.vector
        def _(e):
            for j in range(NJ):
                e.wait_ge(m.s_x[j], 16)
                with e.Fori(B * j, B * (j + 1)) as u:
                    e.bn_stats(m.stats[:, u, :], m.X[:, u, :]).then_inc(s_st, 1)
            e.wait_ge(s_st, NU)
            moments(e, s_var, 0, m.stats[:, :, :], m.mv[:, :, 0], m.mv[:, :, 1])
            e.wait_ge(s_rs, 1)

            def norm(j, k):
                for b in range(B):
                    last = e.tensor_scalar(xn[k][:, b, :], m.X[:, B * j + b, :], m.mv[:, B * j + b, 0:1],
                                           m.rstd[:, bass.ds(B * j + b, 1)], ALU.subtract, ALU.mult)
                last.then_inc(s_xn, 1)

            def pooled(j):
                e.wait_ge(s_cp, 2 * j + 2)
                e.tensor_reduce(m.pool[:, :, bass.ds(8 * j, 8)],
                                m.xnT[:, bass.ds(B * j, B), WIN:XW].rearrange("p b (n t) -> p b n t", t=CHUNK), axis=AX.X, op=ALU.add).then_inc(s_pool, 1)

            norm(0, 0)
            norm(1, 1)
            with e.Fori(0, NJ // 2 - 1) as jj:
                for k in range(2):
                    j = 2 * jj
                    e.wait_ge(s_tr, 2 * (j + k) + 2)
                    norm(j + k + 2, k)
                    pooled(j + k)
            pooled(NJ - 2)
            pooled(NJ - 1)
            e.wait_ge(s_lat, 1)
            for b in range(B):
                e.tensor_tensor(m.gkbd[:, b, :, :],
                                m.ps[4][0:LD, NL * b:NL * (b + 1)].rearrange("p (o n) -> p o n", o=1).broadcast_to([LD, LH, NL]),
                                m.lhm[0:LD, :].rearrange("p (h o) -> p h o", o=1).broadcast_to([LD, LH, NL]), ALU.mult)
            for g in range(2):
                last = e.tensor_scalar(m.gvx[:, :, g, 0:8], m.ps[5][:, :].rearrange("p (k g d) -> p k g d", g=2, d=8)[:, :, g, :],
                                       m.par[:, g:g + 1], 1.0 / CHUNK, ALU.mult, ALU.mult)
            last.then_inc(s_gk, 1)

        @block.gpsimd
        def _(e):
            e.wait_ge(s_var, MOMENTS)
            e.tensor_tensor(m.rstd[:, :], m.mv[:, :, 1], m.nhalf[:, :], ALU.pow).then_inc(s_rs, 1)
            with e.Fori(0, NJ) as j:
                e.wait_ge(s_cp, 2 * j + 2)
                e.tensor_copy(m.xnT[:, bass.ds(B * j + B, B), 0:WIN], m.xnT[:, bass.ds(B * j, B), P:XW]).then_inc(s_tail, 1)
            e.wait_ge(s_pool, NJ)
            e.tensor_copy(pool2[:, :, :, :], m.pool[:, :, :].rearrange("p b (o n) -> p b o n", o=1).broadcast_to([P, B, 2, NL])).then_inc(s_pool, 1)

        @block.tensor
        def _(e):
            def turn(j, k):
                e.wait_ge(s_xn, j + 1)
                for h in range(2):
                    if not isinstance(j, int) or j >= 2:
                        e.wait_ge(s_cp, 2 * (j - 2) + h + 1)
                    for b in range(HALF):
                        last = e.transpose(m.ps[2 * k + h][:, D * b:D * (b + 1)], xn[k][:, HALF * h + b, :], m.ident[:, :])
                    last.then_inc(s_tr, 1)

            turn(0, 0)
            turn(1, 1)
            with e.Fori(1, NJ // 2) as jj:
                for k in range(2):
                    turn(2 * jj + k, k)
            e.wait_ge(s_pool, NJ + 1)
            e.matmul(m.ps[4][0:LD, :], m.wgk[:, :], m.pool[:, :, :].rearrange("p b n -> p (b n)"), start=True, stop=True)
            for b in range(B):
                last = e.matmul(m.ps[5][:, LD * b:LD * (b + 1)],
                                pool2[:, b, :, :].rearrange("p o n -> p (o n)"),
                                m.wgv[:, :], start=True, stop=True)
            last.then_inc(s_lat, 1)

        @block.scalar
        def _(e):
            def store(j, k):
                for h in range(2):
                    e.wait_ge(s_tr, 2 * j + h + 1)
                    e.copy(m.xnT[:, bass.ds(B * j + HALF * h, HALF), WIN:XW], m.ps[2 * k + h][:, :].rearrange("p (b t) -> p b t", b=HALF)).then_inc(s_cp, 1)
            with e.Fori(0, NJ // 2) as jj:
                for k in range(2):
                    store(2 * jj + k, k)


def wait(e, semaphore, value):
    if not isinstance(value, int) or value > 0:
        e.wait_ge(semaphore, value)


def skewed(e, front, back, n, peeled=1):
    def body(t):
        front(2 * t + 1, 1)
        back(2 * t, 0)
        front(2 * t + 2, 0)
        back(2 * t + 1, 1)

    front(0, 0)
    for t in range(peeled):
        body(t)
    with e.Fori(peeled, n // 2 - 1) as t:
        body(t)
    front(n - 1, 1)
    back(n - 2, 0)
    back(n - 1, 1)


def local_attention(nc, ctx, m, a):
    def sem(name):
        return ctx.enter_context(nc.semaphore("local_" + name))
    s_xd, s_qkg, s_kt, s_gt, s_qx, s_v, s_vx, s_ones = (sem(n) for n in ("windows", "qkg", "k", "gates", "q", "v", "v_kept", "ones"))
    s_sc, s_sm, s_mx, s_sub, s_exp = (sem(n) for n in ("scores", "masked", "max", "shifted", "exp"))
    s_t, s_ptd, s_pta, s_pv, s_rec, s_o = (sem(n) for n in ("turned", "turned_dve", "turned_act", "pv", "norm", "out"))
    NP = NU // 2
    NG = 4
    c = Cut(m.work)
    xd = [c.take(NB * 2 * KW).rearrange("p (b o k) -> p b o k", b=NB, o=2) for _ in range(2)]
    qx = [c.take(NB * P).rearrange("p (b h q) -> p b h q", b=NB, h=HH) for _ in range(2)]
    kx = [c.take(HG * XW).rearrange("p (g t) -> p g t", g=HG) for _ in range(2)]
    vx = c.take(4 * 576).rearrange("p (n g c) -> p n g c", g=2, c=9)
    Sc = [c.take(4 * 2 * HG * KW).rearrange("p (n u k) -> p n u k", n=4, u=2 * HG) for _ in range(2)]
    Pr = c.take(2 * NB * HG * KW).rearrange("p (u g k) -> p u g k", u=2 * NB, g=HG)
    PT = c.take(NG * NB * P).rearrange("p (n b c) -> p n b c", n=NG, b=NB)
    mx = c.take(2 * 4 * 2 * HG).rearrange("p (v n u) -> p v n u", v=2, n=4)
    rec = c.take(2 * H).rearrange("p (u s) -> p u s", u=2)
    bank_s, bank_t, bank_q, bank_v = m.ps[0:4], m.ps[4:6], m.ps[6], m.ps[7]

    def vbuf(v, k):
        return vx[:, 32 * (2 * v + k):32 * (2 * v + k) + 32, :, :]

    with nc.Block() as block:
        @block.gpsimd
        def _(e):
            def windows(i):
                for k in range(2):
                    wait(e, s_v, 2 * i + k - 1)
                    for h in range(2):
                        e.tensor_copy(xd[k][:, :, :, WIN * h:WIN * h + WIN],
                                      m.xnT[:, 2 * i + k, WIN * h:WIN * h + P].rearrange("p (b o k) -> p b o k", b=NB, o=1)
                                      .broadcast_to([P, NB, 2, WIN])).then_inc(s_xd, 1)

            def front(i, v):
                if not (isinstance(i, int) and i == NP - 1):
                    windows(i + 1)
                for n in range(4):
                    e.wait_ge(s_mx, 4 * i + n + 1)
                    e.tensor_tensor(Sc[v][:, n, :, :], Sc[v][:, n, :, :],
                                    mx[:, v, n, :].rearrange("p (u o) -> p u o", o=1).broadcast_to([P, 2 * HG, KW]),
                                    ALU.subtract).then_inc(s_sub, 1)

            windows(0)
            skewed(e, front, lambda i, v: None, NP)

        @block.tensor
        def _(e):
            def turn(i, k):
                e.wait_ge(s_exp, 2 * i + k + 1)
                for r in range(2):
                    if k == 0:
                        wait(e, s_pta if r else s_ptd, 2 * i)
                    else:
                        e.wait_ge(s_pta if r else s_ptd, 2 * i + 1)
                    for b in range(NB):
                        last = e.transpose(bank_t[r][:, P * b:P * b + P],
                                           Pr[:, NB * k + b, 2 * r:2 * r + 2, :].rearrange("p g k -> p (g k)"), m.ident[:, :])
                    last.then_inc(s_t, 1)

            def front(i, v):
                for k in range(2):
                    if not (isinstance(i, int) and i == 0):
                        turn(i - 1, k)
                    u = 2 * i + k
                    wait(e, s_qx, u)
                    e.wait_ge(s_xd, 2 * u + 2)
                    e.matmul(bank_q[:, 0:P], m.wq[:, :], m.xnT[:, u, WIN:XW], start=True, stop=True)
                    e.matmul(bank_q[:, P:P + XW], m.wk[:, :], m.xnT[:, u, :], start=True, stop=True)
                    for b in range(NB):
                        last = e.matmul(bank_q[WIN * b:WIN * b + WIN, P + XW:P + XW + 2 * H], xd[k][:, b, 0, WIN:KW],
                                        m.wg[:, :], start=True, stop=True)
                    last.then_inc(s_qkg, 1)
                    if k == 0:
                        wait(e, s_o, i - 1)
                    wait(e, s_vx, u)
                    for b in range(NB):
                        last = e.matmul(bank_v[:, D * b:D * b + D], xd[k][:, b, :, :].rearrange("p o k -> p (o k)"),
                                        m.wv[:, :], start=True, stop=True)
                    last.then_inc(s_v, 1)
                e.wait_ge(s_kt, 2 * i + 2)
                e.wait_ge(s_qx, 2 * i + 2)
                for n in range(4):
                    wait(e, s_sm, 4 * (i - 1) + n + 1)
                    k = n // 2
                    for t in range(2):
                        b = 2 * (n % 2) + t
                        last = e.matmul(bank_s[n][:, HG * KW * t:HG * KW * (t + 1)], qx[k][:, b, :, :].rearrange("p h q -> p (h q)"),
                                        kx[k][:, :, WIN * b:WIN * b + KW], start=True, stop=True)
                    last.then_inc(s_sc, 1)

            def back(i, v):
                if isinstance(i, int) and i == NP - 1:
                    for k in range(2):
                        turn(i, k)
                e.wait_ge(s_vx, 2 * i + 2)
                wait(e, s_v, 2 * i + 2)
                for n in range(NG):
                    k, r = n // 2, n % 2
                    e.wait_ge(s_ptd if n % 2 == 0 else s_pta, 2 * i + n // 2 + 1)
                    for b in range(NB):
                        for h in range(HH):
                            at = 144 * k + 18 * (HH * r + h)
                            last = e.matmul(bank_v[WIN * b:WIN * b + WIN, at:at + 18], PT[:, n, b, WIN * h:WIN * h + WIN],
                                            vbuf(v, k)[:, 8 * b + 4 * r + h, :, :].rearrange("p g c -> p (g c)"),
                                            start=True, stop=True)
                last.then_inc(s_pv, 1)

            def back_after(i, v):
                wait(e, s_vx, 2 * i + 4) if not (isinstance(i, int) and i == NP - 1) else None
                back(i, v)
            skewed(e, front, back_after, NP)

        @block.vector
        def _(e):
            e.memset(vx[:, :, :, :], 1.0).then_inc(s_ones, 1)
            e.wait_ge(s_ones, 1)
            for g in range(2):
                last = e.tensor_scalar(vx[:, :, g, 8], vx[:, :, g, 8], m.par[:, g:g + 1], None, ALU.mult)
            last.then_inc(s_ones, 1)
            for k in range(2):
                e.memset(kx[k], 0.0).then_inc(s_ones, 1)

            def keep(i, k):
                wait(e, s_pv, i)
                e.wait_ge(s_t, 4 * i + 2 * k + 1)
                e.tensor_copy(PT[:, 2 * k, :, :].rearrange("p b c -> p (b c)"), bank_t[0][:, :]).then_inc(s_ptd, 1)

            def front(i, v, var):
                for k in range(2):
                    if not (isinstance(i, int) and i == 0):
                        keep(i - 1, k)
                    u = 2 * i + k
                    e.wait_ge(s_gt, u + 1)
                    wait(e, s_sc, 4 * i)
                    e.tensor_tensor(qx[k].rearrange("p b h q -> p h b q"),
                                    bank_q[:, 0:P].rearrange("p (o b q) -> p o b q", o=1, b=NB).broadcast_to([P, HH, NB, WIN]),
                                    m.hm[:, :].rearrange("p (h o w) -> p h o w", o=1, w=1).broadcast_to([P, HH, NB, WIN]),
                                    ALU.mult).then_inc(s_qx, 1)
                for n in range(4):
                    e.wait_ge(s_sc, 4 * i + n + 1)
                    wait(e, s_exp, 2 * (i - 1))
                    half = slice(2 * (n % 2), 2 * (n % 2) + 2)
                    e.tensor_tensor(Sc[v][:, n, :, :].rearrange("p (b g) k -> p b g k", b=2),
                                    bank_s[n][:, :].rearrange("p (b g k) -> p b g k", b=2, g=HG),
                                    m.cmask[:, var, half, :].rearrange("p b (o k) -> p b o k", o=1).broadcast_to([P, 2, HG, KW]),
                                    ALU.add).then_inc(s_sm, 1)
                    e.wait_ge(s_sm, 4 * i + n + 1)
                    e.tensor_reduce(mx[:, v, n, :], Sc[v][:, n, :, :], axis=AX.X, op=ALU.max).then_inc(s_mx, 1)

            def back(i, v):
                if isinstance(i, int) and i == NP - 1:
                    for k in range(2):
                        keep(i, k)
                e.wait_ge(s_pv, i + 1)
                o = bank_v[:, 0:288].rearrange("p (u s c) -> p u s c", u=2, c=9)
                e.reciprocal(rec, o[:, :, :, 8]).then_inc(s_rec, 1)
                e.wait_ge(s_rec, 2 * i + 1)
                e.scalar_tensor_tensor(rec, m.glr[:, bass.ds(2 * i, 2), 0:H], 1.0, rec, ALU.add, ALU.mult).then_inc(s_rec, 1)
                e.wait_ge(s_rec, 2 * i + 2)
                e.tensor_tensor(m.mix[:, bass.ds(2 * i, 2), :].rearrange("p u (s d) -> p u s d", d=HD), o[:, :, :, 0:8],
                                rec.rearrange("p u (s o) -> p u s o", o=1).broadcast_to([P, 2, H, HD]), ALU.mult).then_inc(s_o, 1)

            def front_by_span(i, v):
                front(i, v, 1 if isinstance(i, int) and i < B // 2 else 0)
            skewed(e, front_by_span, back, NP, 2)

        @block.scalar
        def _(e):
            def keep(i, k):
                wait(e, s_pv, i)
                e.wait_ge(s_t, 4 * i + 2 * k + 2)
                e.copy(PT[:, 2 * k + 1, :, :].rearrange("p b c -> p (b c)"), bank_t[1][:, :]).then_inc(s_pta, 1)

            def exps(i, v):
                wait(e, s_t, 4 * i)
                for h in range(2):
                    e.wait_ge(s_sub, 4 * i + 2 * h + 2)
                    e.activation(Pr[:, NB * h:NB * h + NB, :, :].rearrange("p b g k -> p (b g k)"),
                                 Sc[v][:, 2 * h:2 * h + 2, :, :].rearrange("p n u k -> p (n u k)"), ACT.Exp).then_inc(s_exp, 1)

            def front(i, v):
                for k in range(2):
                    if not (isinstance(i, int) and i == 0):
                        keep(i - 1, k)
                    u = 2 * i + k
                    wait(e, s_sc, 4 * i)
                    e.wait_ge(s_qkg, u + 1)
                    if isinstance(i, int) and i == 0:
                        e.wait_ge(s_ones, 4)
                    for g in range(HG):
                        rows = slice(WIN * g, WIN * g + WIN)
                        last = e.copy(kx[k][rows, g, :], bank_q[rows, P:P + XW])
                    last.then_inc(s_kt, 1)
                    e.activation(m.glr[:, u, :], bank_q[:, P + XW:P + XW + 2 * H], ACT.Tanh, scale=0.5).then_inc(s_gt, 1)
                    e.wait_ge(s_v, u + 1)
                    if k == 0:
                        wait(e, s_pv, i - 1)
                    for g in range(2):
                        for r in range(2):
                            o = vbuf(v, k)[:, :, g, 0:8].rearrange("p (b r h) d -> p r b h d", b=NB, r=2)[:, r]
                            x = bank_v[:, :].rearrange("p (b r g h d) -> p r g b h d", b=NB, r=2, g=2, h=HH)[:, r, g]
                            last = e.activation(o, x, ACT.Copy, scale=m.par[:, g:g + 1])
                    last.then_inc(s_vx, 1)
                exps(i, v)

            def back(i, v):
                if isinstance(i, int) and i == NP - 1:
                    for k in range(2):
                        keep(i, k)

            skewed(e, front, back, NP)


def pipeline(e, stages, n, width, first):
    stages = sorted(stages, key=lambda x: -x[0])
    for r in range(first):
        for lag, f in stages:
            if r - lag >= 0:
                f(r - lag, (r - lag) % width, (r - lag) // width)
    with e.Fori(first // width, n // width) as t:
        for r in range(width):
            for lag, f in stages:
                f(width * t + (r - lag), (r - lag) % width, t + (r - lag) // width)
    for r in range(n, n + stages[0][0]):
        for lag, f in stages:
            if r - lag < n:
                f(r - lag, (r - lag) % width, (r - lag) // width)


def latent_attention(nc, ctx, m, a):
    def sem(name):
        return ctx.enter_context(nc.semaphore("latent_" + name))
    s_gq, s_gqk, s_sc, s_sm, s_mx, s_sub, s_exp = (sem(n) for n in ("q", "q_kept", "scores", "masked", "max", "shifted", "exp"))
    s_t, s_pt, s_pv, s_rec, s_lat, s_t2, s_lt, s_rm, s_gr = (sem(n) for n in ("turned", "turned_kept", "pv", "recip", "normed", "out_turned", "out_kept", "remote", "gated"))
    s_mix, s_t3, s_mt, s_wo, s_x, s_st = (sem(n) for n in ("mixed", "mix_turned", "mix_kept", "projected", "added", "stats"))
    W = B
    c = Cut(m.work)

    def two(n, shape=None, **k):
        out = [c.take(n) for _ in range(2)]
        return [v.rearrange(shape, **k) for v in out] if shape else out
    gq = [v[0:LD] for v in two(P)]
    Sl = two(LH * NL, "p (h n) -> p h n", h=LH)
    Pl = two(LH * NL)
    PT = two(LH * NL)
    latf = two(D)
    lat = [v[:, 0:LD].rearrange("p (h d) -> p h d", h=LH) for v in latf]
    rec = two(LH)
    mxl = two(LH)
    latT = [v[0:LD] for v in two(P)]
    rem = two(D)
    fin = two(D)
    finT = two(P)
    lmask = c.take(NJ * NL).rearrange("p (j n) -> p j n", j=NJ)
    s_lm = sem("mask")
    bq, bs, bw, bt, bo, b2, br, b3 = m.ps

    with nc.Block() as block:
        @block.tensor
        def _(e):
            def q(u, k, j):
                wait(e, s_gqk, u)
                e.matmul(bq[0:LD, 0:P], m.wgq[:, :], m.xnT[:, u, WIN:XW], start=True, stop=True).then_inc(s_gq, 1)

            def scores(u, k, j):
                e.wait_ge(s_gqk, u + 1)
                wait(e, s_sm, u)
                e.matmul(bs[:, :], gq[k % 2], m.gkbd[:, k, :, :].rearrange("p h n -> p (h n)"), start=True, stop=True).then_inc(s_sc, 1)

            def turn(u, k, j):
                e.wait_ge(s_exp, u + 1)
                wait(e, s_pt, u)
                for n in range(4):
                    last = e.transpose(bt[:, P * n:P * n + P], Pl[k % 2][:, P * n:P * n + P], m.ident[:, :])
                last.then_inc(s_t, 1)

            def pv(u, k, j):
                e.wait_ge(s_pt, u + 1)
                wait(e, s_lat, u)
                for n in range(4):
                    last = e.matmul(bo[:, 18 * n:18 * n + 18], PT[k % 2][:, P * n:P * n + P],
                                    m.gvx[:, 4 * k + n, :, :].rearrange("p g c -> p (g c)"), start=True, stop=True)
                last.then_inc(s_pv, 1)

            def turn_out(u, k, j):
                e.wait_ge(s_lat, u + 1)
                wait(e, s_lt, u)
                e.transpose(b2[:, 0:P], latf[k % 2], m.ident[:, :]).then_inc(s_t2, 1)

            def remote(u, k, j):
                e.wait_ge(s_lt, u + 1)
                wait(e, s_gr, u)
                e.matmul(br[:, 0:D], latT[k % 2], m.routp[:, :], start=True, stop=True).then_inc(s_rm, 1)

            def turn_mix(u, k, j):
                e.wait_ge(s_mix, u + 1)
                wait(e, s_mt, u)
                e.transpose(b3[:, 0:P], fin[k % 2], m.ident[:, :]).then_inc(s_t3, 1)

            def project(u, k, j):
                e.wait_ge(s_mt, u + 1)
                wait(e, s_x, u)
                e.matmul(bw[:, 0:D], finT[k % 2], m.wout[:, :], start=True, stop=True).then_inc(s_wo, 1)

            pipeline(e, [(0, q), (1, scores), (3, turn), (4, pv), (5, turn_out), (6, remote), (7, turn_mix), (8, project)],
                     NU, W, 2 * W)

        @block.vector
        def _(e):
            def top(u, k, j):
                e.wait_ge(s_sc, u + 1)
                wait(e, s_exp, u - 1)
                e.tensor_tensor(Sl[k % 2], bs[:, :].rearrange("p (h n) -> p h n", h=LH),
                                lmask[:, j, :].rearrange("p (o n) -> p o n", o=1).broadcast_to([P, LH, NL]),
                                ALU.add).then_inc(s_sm, 1)
                e.wait_ge(s_sm, u + 1)
                e.tensor_reduce(mxl[k % 2], Sl[k % 2], axis=AX.X, op=ALU.max).then_inc(s_mx, 1)

            def norm(u, k, j):
                e.wait_ge(s_pv, u + 1)
                wait(e, s_t2, u - 1)
                o = bo[:, 0:LH * 9].rearrange("p (h c) -> p h c", c=9)
                e.reciprocal(rec[k % 2], o[:, :, 8]).then_inc(s_rec, 1)
                e.wait_ge(s_rec, u + 1)
                e.tensor_tensor(lat[k % 2], o[:, :, 0:8],
                                rec[k % 2].rearrange("p (h o) -> p h o", o=1).broadcast_to([P, LH, 8]), ALU.mult).then_inc(s_lat, 1)

            def gate(u, k, j):
                e.wait_ge(s_rm, u + 1)
                wait(e, s_mix, u - 1)
                e.scalar_tensor_tensor(rem[k % 2].rearrange("p (s d) -> p s d", d=HD),
                                       m.glr[:, u, H:2 * H].rearrange("p (s o) -> p s o", o=1).broadcast_to([P, H, HD]), 1.0,
                                       br[:, 0:D].rearrange("p (s d) -> p s d", d=HD), ALU.add, ALU.mult).then_inc(s_gr, 1)

            def add(u, k, j):
                e.wait_ge(s_wo, u + 1)
                e.tensor_tensor(m.X[:, u, :], m.X[:, u, :], bw[:, 0:D], ALU.add).then_inc(s_x, 1)

            def stat(u, k, j):
                e.wait_ge(s_x, u + 1)
                e.bn_stats(m.stats[:, u, :], m.X[:, u, :]).then_inc(s_st, 1)

            for v in latf:
                e.memset(v[:, LD:D], 0.0)
            e.wait_ge(s_lm, 2)
            pipeline(e, [(1, top), (4, norm), (6, gate), (8, add), (9, stat)], NU, W, 2 * W)
            e.wait_ge(s_st, NU)

        @block.gpsimd
        def _(e):
            e.memset(lmask, 0.0).then_inc(s_lm, 1)
            e.wait_ge(s_lm, 1)
            e.affine_select(out=lmask, in_=lmask, compare_op=ALU.is_ge, fill=NEG, base=0,
                            pattern=[[P, NJ], [-CHUNK, NL]], channel_multiplier=1).then_inc(s_lm, 1)
            e.wait_ge(s_lm, 2)

            def sub(u, k, j):
                e.wait_ge(s_mx, u + 1)
                e.tensor_tensor(Sl[k % 2], Sl[k % 2], mxl[k % 2].rearrange("p (h o) -> p h o", o=1).broadcast_to([P, LH, NL]),
                                ALU.subtract).then_inc(s_sub, 1)

            def mixed(u, k, j):
                e.wait_ge(s_gr, u + 1)
                wait(e, s_t3, u - 1)
                e.tensor_tensor(fin[k % 2], m.mix[:, u, :], rem[k % 2], ALU.add).then_inc(s_mix, 1)

            pipeline(e, [(1, sub), (6, mixed)], NU, W, 2 * W)

        @block.scalar
        def _(e):
            def keep_q(u, k, j):
                e.wait_ge(s_gq, u + 1)
                wait(e, s_sc, u - 1)
                e.mul(gq[k % 2], bq[0:LD, 0:P], ISQ).then_inc(s_gqk, 1)

            def exps(u, k, j):
                e.wait_ge(s_sub, u + 1)
                wait(e, s_t, u - 1)
                e.activation(Pl[k % 2], Sl[k % 2].rearrange("p h n -> p (h n)"), ACT.Exp).then_inc(s_exp, 1)

            def keep_pt(u, k, j):
                e.wait_ge(s_t, u + 1)
                wait(e, s_pv, u - 1)
                e.copy(PT[k % 2], bt[:, :]).then_inc(s_pt, 1)

            def keep_out(u, k, j):
                e.wait_ge(s_t2, u + 1)
                wait(e, s_rm, u - 1)
                e.copy(latT[k % 2], b2[0:LD, 0:P]).then_inc(s_lt, 1)

            def keep_mix(u, k, j):
                e.wait_ge(s_t3, u + 1)
                wait(e, s_wo, u - 1)
                e.copy(finT[k % 2], b3[:, 0:P]).then_inc(s_mt, 1)

            pipeline(e, [(0, keep_q), (1, exps), (3, keep_pt), (5, keep_out), (7, keep_mix)], NU, W, 2 * W)


def ffn(nc, ctx, m, a):
    def sem(name):
        return ctx.enter_context(nc.semaphore("ffn_" + name))
    s_mo, s_rs, s_n, s_q, s_t, s_qt, s_y, s_y1, s_y2, s_x, s_st = (
        sem(n) for n in ("moments", "rstd", "normed", "rounded", "turned", "turned_kept", "product", "scaled", "biased", "added", "stats"))
    c = Cut(m.work)
    w = B * D
    xb = c.take(w, BF16)
    t, sc = c.take(w), c.take(w)
    q = c.take(w)
    qb = [c.take(w, BF16) for _ in range(2)]
    qT = [c.take(w, BF16) for _ in range(2)]
    y1 = [c.take(w, BF16) for _ in range(2)]
    y2 = [c.take(w, BF16) for _ in range(2)]
    steps = [0]

    with nc.Block() as block:
        @block.vector
        def _(e):
            moments(e, s_mo, 0, m.stats[:, :, :], m.mv[:, :, 0], m.mv[:, :, 1])
            e.wait_ge(s_rs, 1)
            per = [0]

            def rounded(i, k, j):
                for b in range(B):
                    u = B * i + b
                    last = e.tensor_scalar(xb[:, D * b:D * b + D], m.X[:, u, :], m.mv[:, u, 0:1], m.rstd[:, bass.ds(u, 1)],
                                           ALU.subtract, ALU.mult)
                n = [0]

                def step(ins):
                    ins.then_inc(s_n, 1)
                    n[0] += 1
                    e.wait_ge(s_n, FFN_STEPS * i + n[0])
                step(last)
                step(e.tensor_scalar(t, xb, m.fsc[:, 2:3], None, ALU.mult))
                round_e4m3fn(e, step, t, q, sc)
                wait(e, s_t, i - 1)
                e.tensor_copy(qb[k], q).then_inc(s_q, 1)
                assert n[0] == FFN_STEPS

            def stat(i, k, j):
                e.wait_ge(s_x, i + 1)
                for b in range(B):
                    last = e.bn_stats(m.stats[:, B * i + b, :], m.X[:, B * i + b, :])
                last.then_inc(s_st, 1)

            pipeline(e, [(0, rounded), (2, stat)], NJ, 2, 2)
            e.wait_ge(s_st, NJ)
            moments(e, s_mo, MOMENTS, m.stats[:, :, :], m.mv[:, :, 0], m.mv[:, :, 1])

        @block.gpsimd
        def _(e):
            e.wait_ge(s_mo, MOMENTS)
            e.tensor_tensor(m.rstd[:, :], m.mv[:, :, 1], m.nhalf[:, :], ALU.pow).then_inc(s_rs, 1)

            def bias(i, k, j):
                e.wait_ge(s_y1, 2 * i + 2)
                wait(e, s_x, i - 1)
                e.tensor_tensor(y2[k].rearrange("p (b n) -> p b n", b=B), y1[k].rearrange("p (b n) -> p b n", b=B),
                                m.fbias[:, :].rearrange("p (o n) -> p o n", o=1).broadcast_to([P, B, D]), ALU.add).then_inc(s_y2, 1)
                e.wait_ge(s_y2, i + 1)
                x = m.X[:, bass.ds(B * i, B), :]
                e.tensor_tensor(x, x, y2[k].rearrange("p (b n) -> p b n", b=B), ALU.add).then_inc(s_x, 1)
            pipeline(e, [(1, bias)], NJ, 2, 2)
            e.wait_ge(s_mo, 2 * MOMENTS)
            e.tensor_tensor(m.rstd[:, :], m.mv[:, :, 1], m.nhalf[:, :], ALU.pow).then_inc(s_rs, 1)
            e.wait_ge(s_rs, 2)

        @block.tensor
        def _(e):
            def turn(i, k, j):
                e.wait_ge(s_q, i + 1)
                wait(e, s_qt, i - 1)
                for b in range(B):
                    last = e.transpose(m.ps[k][:, :].bitcast(BF16)[:, P * b:P * b + P], qb[k][:, D * b:D * b + D], m.identb[:, :])
                last.then_inc(s_t, 1)

            def product(i, k, j):
                e.wait_ge(s_qt, i + 1)
                for h in range(2):
                    wait(e, s_y1, 2 * (i - 2) + h + 1)
                    for b in range(HALF):
                        u = HALF * h + b
                        last = e.matmul(m.ps[2 + 2 * k + h][:, D * b:D * b + D], qT[k][:, P * u:P * u + P], m.fkq[:, :], start=True, stop=True)
                    last.then_inc(s_y, 1)
            pipeline(e, [(0, turn), (1, product)], NJ, 2, 4)

        @block.scalar
        def _(e):
            def keep(i, k, j):
                e.wait_ge(s_t, i + 1)
                wait(e, s_y, 2 * (i - 1))
                e.copy(qT[k], m.ps[k][:, :].bitcast(BF16)).then_inc(s_qt, 1)

            def scale(i, k, j):
                wait(e, s_y2, i - 1)
                for h in range(2):
                    e.wait_ge(s_y, 2 * i + h + 1)
                    e.activation(y1[k][:, 512 * h:512 * h + 512], m.ps[2 + 2 * k + h][:, :], ACT.Copy, scale=m.fsc[:, 4:5]).then_inc(s_y1, 1)
            pipeline(e, [(0, keep), (1, scale)], NJ, 2, 2)


FFN_STEPS = 10


def split_weights(nc, ctx, m, a):
    s_in = ctx.enter_context(nc.semaphore("experts_loaded"))
    s_w3 = ctx.enter_context(nc.semaphore("experts_down_loaded"))
    s_z = ctx.enter_context(nc.semaphore("b3_zeros"))
    s_hi, s_lo = (ctx.enter_context(nc.semaphore(n)) for n in ("experts_high", "experts_low"))
    st = m.Wst.rearrange("p (e f) -> p e f", e=E)
    with nc.Block() as block:
        @block.sync
        def _(sp):
            sp.dma_start(st, a.W1.rearrange("e d f -> d e f")).then_inc(s_in, 16)
            for c in range(NC4):
                sp.dma_start(m.W3s[:, :, D * c:D * c + D], a.W3[:, P * c:P * c + P, :].rearrange("e p n -> p e n")).then_inc(s_w3, 16)
            sp.wait_ge(s_z, 1)
            for b in range(B):
                sp.dma_start(m.b3bd[E * b:E * (b + 1), D * b:D * (b + 1)], a.b3).then_inc(s_w3, 16)
            sp.wait_ge(s_lo, 1)
            sp.dma_start(st, a.W2.rearrange("e d f -> d e f")).then_inc(s_in, 16)
            sp.wait_ge(s_w3, 16 * (NC4 + B))

        @block.gpsimd
        def _(e):
            e.memset(m.b3bd, 0.0).then_inc(s_z, 1)

        @block.scalar
        def _(e):
            for n, hi in enumerate((m.W1h, m.W2h)):
                e.wait_ge(s_in, 16 * n + 16)
                e.copy(hi, st).then_inc(s_hi, 1)

        @block.vector
        def _(e):
            for n, (hi, lo) in enumerate(((m.W1h, m.W1l), (m.W2h, m.W2l))):
                e.wait_ge(s_hi, n + 1)
                e.tensor_tensor(lo, st, hi, ALU.subtract).then_inc(s_lo, 1)


def scan_and_experts(nc, ctx, m, a):
    def sem(name):
        return ctx.enter_context(nc.semaphore("x_" + name))
    s_n3, s_t3, s_x3, s_pi, s_in, s_pg, s_g, s_c, s_u = (sem(n) for n in ("normed", "turned", "xT", "in_proj", "inp", "gate_proj", "gate", "carry", "drive"))
    s_ch, s_th, s_r = (sem(n) for n in ("step_product", "step_tanh", "step_state"))
    s_a, s_sa, s_b, s_h, s_w3, s_yd = (sem(n) for n in ("up_a", "silu", "up_b", "hidden", "down", "summed"))
    s_S, s_po, s_xo, s_st, s_mo, s_rs, s_n4, s_t4, s_x4f, s_x4, s_pr, s_lg, s_d, s_w, s_k, s_cw, s_tc, s_ct, s_pb, s_xb = (
        sem(n) for n in ("states", "out_proj", "residual", "stats4", "moments4", "rstd4", "normed4", "turned4", "xT4", "parts4", "logits_raw",
                         "logits", "gap", "gap_tanh", "chain", "shares", "shares_turned", "shares_kept", "bias_sum", "biased"))
    s_out, s_z, s_tk = sem("written"), sem("zeroed"), sem("tick_zeroed")

    c = Cut(m.work)
    w = B * P
    n3 = c.take(w).rearrange("p (b d) -> p b d", b=B)
    x3T = c.take(w)
    Sx = x3T.rearrange("p (b t) -> p b t", b=B)
    inp = c.take(w)
    inpv = inp.rearrange("p (b t) -> p b t", b=B)
    g = c.take(w)
    gv = g.rearrange("p (b t) -> p b t", b=B)
    tmp = c.take(w)
    Cb = c.take(B * (P + 1)).rearrange("p (b t) -> p b t", b=B)
    R = c.take(B * (P + 1)).rearrange("p (b t) -> p b t", b=B)
    x4f = c.take(w)
    x4h, x4l = c.take(w, F16), c.take(w, F16)
    sa = [c.take(512) for _ in range(2)]
    hb = [c.take(512) for _ in range(2)]
    th = [c.take(B) for _ in range(2)]
    lg = c.take(B * E).rearrange("p (b e) -> p b e", b=B)
    mx8 = c.take(B * E).rearrange("p (b e) -> p b e", b=B)
    ix = c.take(B * E).bitcast(U32).rearrange("p (b e) -> p b e", b=B)
    ixf = c.take(B * 2).rearrange("p (b e) -> p b e", b=B)
    ws = c.take(B * 2).rearrange("p (b e) -> p b e", b=B)
    eq = [c.take(B * E).rearrange("p (b e) -> p b e", b=B) for _ in range(2)]
    cwp = c.take(P)
    cw = cwp[:, 0:B * E].rearrange("p (b e) -> p b e", b=B)
    cwT = c.take(P)[0:B * E]
    U = m.psum[:, 0:1024]
    bU, bA, bB, bY, bZ = m.ps[0:2], m.ps[2:4], m.ps[4:6], m.ps[6], m.ps[7]
    AT, BT, WinT, WgT, WoT = (m.w5T[:, n, :] for n in range(5))
    XR = 2 * MOMENTS

    def rounds(e, round_):
        round_(0, True, False)
        with e.Fori(1, NJ) as j:
            round_(j, True, True)
        round_(NJ, False, True)

    def halves(e, j, body, flush):
        with e.Fori(0, 2) as h:
            body(16 * (j - 1) + 8 * h, 16 * j + 8 * h, h, 0, True)
            with e.Fori(1, E) as x:
                body(16 * (j - 1) + 8 * h + x, 16 * j + 8 * h + x, h, x, False)
            flush(16 * (j - 1) + 8 * h + 7, h)

    def two_back(g, ch, fresh):
        return 4 * g if fresh and ch == 0 else 4 * g + ch - 1

    with nc.Block() as block:
        @block.tensor
        def _(e):
            def pre(j):
                wait(e, s_h, 64 * (j - 1))
                wait(e, s_yd, 16 * (j - 1))
                e.wait_ge(s_n3, j + 1)
                for h in range(2):
                    for b in range(HALF):
                        last = e.transpose(bA[h][:, P * b:P * b + P], n3[:, HALF * h + b, :], m.ident[:, :])
                    last.then_inc(s_t3, 1)
                for h in range(2):
                    e.wait_ge(s_x3, 2 * j + h + 1)
                    e.matmul(bB[h], WinT, x3T[:, 512 * h:512 * h + 512], start=True, stop=True).then_inc(s_pi, 1)
                for h in range(2):
                    e.wait_ge(s_in, 2 * j + h + 1)
                    e.matmul(bA[h], WgT, inp[:, 512 * h:512 * h + 512], start=True, stop=True).then_inc(s_pg, 1)
                for h in range(2):
                    e.matmul(bU[h], BT, inpv.rearrange("p b t -> p t b")[:, 64 * h:64 * h + 64, :], start=True, stop=True)
                e.wait_ge(s_c, j + 1)
                for h in range(2):
                    last = e.matmul(bU[h], AT, Cb[:, :, 0:P].rearrange("p b t -> p t b")[:, 64 * h:64 * h + 64, :], start=False, stop=True, skip_group_check=True)
                last.then_inc(s_u, 1)

            def step(T, t, s):
                wait(e, s_r, T + s)
                e.matmul(U[:, bass.ds(B * (t + s), B)], AT, R[:, :, bass.ds(t + s, 1)].rearrange("p b o -> p (b o)"),
                         start=False, stop=True, skip_group_check=True).then_inc(s_ch, 1)

            def down(g, x, ch):
                e.wait_ge(s_h, 4 * g + ch + 1)
                if ch == 0:
                    wait(e, s_yd, g)
                for n in range(HALF):
                    last = e.matmul(bY[:, D * n:D * n + D], hb[ch % 2][:, P * n:P * n + P], m.W3s[:, x, D * ch:D * ch + D],
                                    start=(ch == 0 and n == 0), stop=(ch == NC4 - 1), skip_group_check=True)
                last.then_inc(s_w3, 1)

            def round_(j, scan, moe):
                if scan:
                    pre(j)

                def body(g, T, h, x, fresh):
                    for s in range(STEPS):
                        if scan:
                            step(8 * T, 64 * h + 8 * x, s)
                        if not moe:
                            continue
                        ch = s // 2
                        f = slice(P * ch, P * ch + P)
                        xh, xl = x4h[:, bass.ds(512 * h, 512)], x4l[:, bass.ds(512 * h, 512)]
                        if s % 2 == 0:
                            if fresh and s == 0:
                                e.wait_ge(s_x4, j)
                                e.wait_ge(s_xb, j)
                            wait(e, s_sa, two_back(g, ch, fresh))
                            e.matmul(bA[ch % 2], m.W1h[:, x, f], xh, start=True, stop=False)
                            e.matmul(bA[ch % 2], m.W1h[:, x, f], xl, start=False, stop=False)
                            e.matmul(bA[ch % 2], m.W1l[:, x, f], xh, start=False, stop=True).then_inc(s_a, 1)
                            wait(e, s_h, two_back(g, ch, fresh))
                            e.matmul(bB[ch % 2], m.W2h[:, x, f], xh, start=True, stop=False)
                            e.matmul(bB[ch % 2], m.W2h[:, x, f], xl, start=False, stop=False)
                        else:
                            e.matmul(bB[ch % 2], m.W2l[:, x, f], xh, start=False, stop=True).then_inc(s_b, 1)
                            if ch > 0:
                                down(g, x, ch - 1)
                            elif not fresh:
                                down(g - 1, x - 1, NC4 - 1)

                def flush(g, h):
                    if moe:
                        down(g, E - 1, NC4 - 1)

                halves(e, j, body, flush)
                if scan:
                    post(j)

            def post(j):
                wait(e, s_h, 64 * j)
                wait(e, s_yd, 16 * j)
                e.wait_ge(s_S, j + 1)
                for h in range(2):
                    for b in range(HALF):
                        last = e.matmul(bA[h][:, D * b:D * b + D], Sx[:, HALF * h + b, :], WoT, start=True, stop=True)
                    last.then_inc(s_po, 1)
                e.wait_ge(s_n4, j + 1)
                for h in range(2):
                    for b in range(HALF):
                        last = e.transpose(bB[h][:, P * b:P * b + P], n3[:, HALF * h + b, :], m.ident[:, :])
                    last.then_inc(s_t4, 1)
                e.wait_ge(s_x4f, 2 * j + 2)
                for b in range(B):
                    last = e.matmul(bZ[:, E * b:E * b + E], x4f[:, P * b:P * b + P], m.wr[:, :], start=True, stop=True)
                last.then_inc(s_pr, 1)
                e.wait_ge(s_cw, j + 1)
                e.transpose(bY[:, 0:P], cwp, m.ident[:, :]).then_inc(s_tc, 1)
                e.wait_ge(s_ct, j + 1)
                e.wait_ge(s_xo, 2 * j + 2)
                for h in range(2):
                    last = e.matmul(bA[h], cwT, m.b3bd[:, 512 * h:512 * h + 512], start=True, stop=True)
                last.then_inc(s_pb, 1)

            rounds(e, round_)

        @block.scalar
        def _(e):
            e.preload_act_table_set("silu_and_others")

            def pre(j):
                for h in range(2):
                    e.wait_ge(s_t3, 2 * j + h + 1)
                    if h == 0:
                        wait(e, s_po, 2 * j)
                    e.copy(x3T[:, 512 * h:512 * h + 512], bA[h]).then_inc(s_x3, 1)
                for h in range(2):
                    e.wait_ge(s_pi, 2 * j + h + 1)
                    e.activation(inp[:, 512 * h:512 * h + 512], bB[h], ACT.Identity, bias=m.bcol[:, 0:1]).then_inc(s_in, 1)
                for h in range(2):
                    e.wait_ge(s_pg, 2 * j + h + 1)
                    e.activation(g[:, 512 * h:512 * h + 512], bA[h], ACT.Tanh, bias=m.bcol[:, 2:3], scale=0.5).then_inc(s_g, 1)

            def round_(j, scan, moe):
                if scan:
                    pre(j)

                def body(g_, T, h, x, fresh):
                    for s in range(STEPS):
                        if scan:
                            e.wait_ge(s_ch, 8 * T + s + 1)
                            e.activation(th[s % 2], U[:, bass.ds(B * (64 * h + 8 * x + s), B)], ACT.Tanh).then_inc(s_th, 1)
                        if moe and s % 2 == 0:
                            ch = s // 2
                            e.wait_ge(s_a, 4 * g_ + ch + 1)
                            wait(e, s_h, two_back(g_, ch, fresh))
                            e.activation(sa[ch % 2], bA[ch % 2], ACT.Silu, bias=m.b12[:, 0, ch, bass.ds(x, 1)]).then_inc(s_sa, 1)

                halves(e, j, body, lambda g_, h: None)
                if scan:
                    post(j)

            def post(j):
                for h in range(2):
                    e.wait_ge(s_t4, 2 * j + h + 1)
                    e.copy(x4f[:, 512 * h:512 * h + 512], bB[h]).then_inc(s_x4f, 1)
                e.wait_ge(s_d, j + 1)
                e.activation(ws[:, :, 0], ws[:, :, 1], ACT.Tanh, scale=0.5).then_inc(s_w, 1)
                e.wait_ge(s_tc, j + 1)
                e.copy(cwT, bY[0:B * E, 0:P]).then_inc(s_ct, 1)

            rounds(e, round_)

        @block.gpsimd
        def _(e):
            e.memset(R[:, :, 0:1], 0.0).then_inc(s_z, 1)
            e.memset(Cb[:, :, 0:1], 0.0).then_inc(s_z, 1)
            e.memset(cwp, 0.0).then_inc(s_z, 1)
            with e.Fori(0, NJ) as j:
                e.wait_ge(s_mo, MOMENTS * (j + 1))
                e.tensor_tensor(m.rstd4, m.mv4[:, :, 1], m.nhalf[:, 0:B], ALU.pow).then_inc(s_rs, 1)

        @block.vector
        def _(e):
            e.wait_ge(s_z, 3)
            e.memset(m.tick[:, :], 0.0).then_inc(s_tk, 1)
            e.wait_ge(s_tk, 1)

            def pre(j):
                if isinstance(j, int) and j == 0:
                    pass
                else:
                    wait(e, s_t4, 2 * j)
                for b in range(B):
                    u = B * j + b
                    last = e.tensor_scalar(n3[:, b, :], m.X[:, u, :], m.mv[:, u, 0:1], m.rstd[:, bass.ds(u, 1)], ALU.subtract, ALU.mult)
                last.then_inc(s_n3, 1)
                if not isinstance(j, int):
                    e.tensor_copy(Cb[:, :, 0:1], Cb[:, :, P:P + 1])
                    e.tensor_copy(R[:, :, 0:1], R[:, :, P:P + 1]).then_inc(s_k, 1)
                    e.wait_ge(s_k, KP * j)
                e.wait_ge(s_g, 2 * j + 2)
                e.tensor_scalar(g, g, 0.5, 0.5, ALU.mult, ALU.add).then_inc(s_k, 1)
                e.wait_ge(s_k, KP * j + 1)
                e.tensor_tensor(tmp, g, inp, ALU.mult).then_inc(s_k, 1)
                e.wait_ge(s_k, KP * j + 2)
                e.tensor_tensor(Cb[:, :, 1:P + 1], inpv, tmp.rearrange("p (b t) -> p b t", b=B), ALU.subtract).then_inc(s_c, 1)

            def round_(j, scan, moe):
                if scan:
                    pre(j)

                def summed(g_, h, x):
                    e.wait_ge(s_w3, 4 * g_ + 4)
                    for n in range(HALF):
                        u = B * (j - 1) + HALF * h + n
                        last = e.scalar_tensor_tensor(m.X[:, u, :], bY[:, D * n:D * n + D],
                                                      cw[:, HALF * h + n, bass.ds(x, 1)], m.X[:, u, :],
                                                      ALU.mult, ALU.add)
                    last.then_inc(s_yd, 1)

                def body(g_, T, h, x, fresh):
                    for s in range(STEPS):
                        if scan:
                            t = 64 * h + 8 * x + s
                            e.wait_ge(s_th, 8 * T + s + 1)
                            e.tensor_tensor(R[:, :, bass.ds(t + 1, 1)].rearrange("p b o -> p (b o)"), th[s % 2],
                                            gv[:, :, bass.ds(t, 1)].rearrange("p b o -> p (b o)"), ALU.mult).then_inc(s_r, 1)
                        if moe and s % 2 == 1:
                            ch = s // 2
                            e.wait_ge(s_b, 4 * g_ + ch + 1)
                            e.wait_ge(s_sa, 4 * g_ + ch + 1)
                            wait(e, s_w3, two_back(g_, ch, fresh))
                            e.scalar_tensor_tensor(hb[ch % 2], bB[ch % 2], m.b12[:, 1, ch, bass.ds(x, 1)], sa[ch % 2],
                                                   ALU.add, ALU.mult).then_inc(s_h, 1)
                        if moe and s == 2 and not fresh:
                            summed(g_ - 1, h, x - 1)

                halves(e, j, body, (lambda g_, h: summed(g_, h, E - 1)) if moe else (lambda g_, h: None))
                if scan:
                    post(j)

            def post(j):
                u8 = m.X[:, bass.ds(B * j, B), :]
                e.wait_ge(s_r, P * (j + 1))
                e.tensor_tensor(Sx, R[:, :, 1:P + 1], Cb[:, :, 1:P + 1], ALU.add).then_inc(s_S, 1)
                for h in range(2):
                    e.wait_ge(s_po, 2 * j + h + 1)
                    xh = m.X[:, bass.ds(B * j + HALF * h, HALF), :]
                    e.tensor_tensor(xh, xh, bA[h].rearrange("p (b n) -> p b n", b=HALF), ALU.add).then_inc(s_xo, 1)
                e.wait_ge(s_xo, 2 * j + 2)
                k = [KP * j + 2]

                def step(ins):
                    ins.then_inc(s_k, 1)
                    k[0] += 1
                    e.wait_ge(s_k, k[0])

                def tick():
                    e.tensor_copy(m.tick[:, 1:2], m.tick[:, 0:1])
                step(e.tensor_tensor(u8, u8, m.bout[:, :].rearrange("p (o n) -> p o n", o=1).broadcast_to([P, B, D]), ALU.add))
                tick()
                for b in range(B):
                    last = e.bn_stats(m.st4[:, b, :], m.X[:, B * j + b, :])
                step(last)
                moments(e, s_mo, MOMENTS * j, m.st4[:, :, :], m.mv4[:, :, 0], m.mv4[:, :, 1])
                e.wait_ge(s_rs, j + 1)
                e.wait_ge(s_t3, 2 * j + 2)
                for b in range(B):
                    last = e.tensor_scalar(n3[:, b, :], m.X[:, B * j + b, :], m.mv4[:, b, 0:1], m.rstd4[:, b:b + 1], ALU.subtract, ALU.mult)
                last.then_inc(s_n4, 1)
                e.wait_ge(s_x4f, 2 * j + 2)
                step(e.tensor_copy(x4h, x4f))
                e.tensor_tensor(x4l, x4f, x4h, ALU.subtract).then_inc(s_x4, 1)
                e.wait_ge(s_pr, j + 1)
                step(e.tensor_tensor(lg, bZ[:, 0:B * E].rearrange("p (b e) -> p b e", b=B),
                                     m.br[:, :].rearrange("p (o n) -> p o n", o=1).broadcast_to([P, B, E]), ALU.add))
                tick()
                for b in range(B):
                    last = e.max(mx8[:, b, :], lg[:, b, :])
                step(last)
                tick()
                for b in range(B):
                    last = e.max_index(ix[:, b, :], mx8[:, b, :], lg[:, b, :])
                step(last)
                e.tensor_tensor(ws[:, :, 1], mx8[:, :, 0], mx8[:, :, 1], ALU.subtract).then_inc(s_d, 1)
                step(e.tensor_copy(ixf, ix[:, :, 0:2]))
                for n in range(2):
                    last = e.tensor_tensor(eq[n], m.iota8[:, :].rearrange("p (o n) -> p o n", o=1).broadcast_to([P, B, E]),
                                           ixf[:, :, n:n + 1].broadcast_to([P, B, E]), ALU.is_equal)
                step(last)
                e.wait_ge(s_w, j + 1)
                step(e.tensor_scalar(ws[:, :, 1], ws[:, :, 0], -0.5, 0.5, ALU.mult, ALU.add))
                step(e.tensor_scalar(ws[:, :, 0], ws[:, :, 0], 0.5, 0.5, ALU.mult, ALU.add))
                for n in range(2):
                    last = e.tensor_tensor(eq[n], eq[n], ws[:, :, n:n + 1].broadcast_to([P, B, E]), ALU.mult)
                step(last)
                e.tensor_tensor(cw, eq[0], eq[1], ALU.add).then_inc(s_cw, 1)
                e.wait_ge(s_pb, j + 1)
                for h in range(2):
                    xh = m.X[:, bass.ds(B * j + HALF * h, HALF), :]
                    last = e.tensor_tensor(xh, xh, bA[h].rearrange("p (b n) -> p b n", b=HALF), ALU.add)
                last.then_inc(s_xb, 1)
                e.wait_ge(s_xb, j + 1)
                e.wait_ge(s_cw, j + 1)
                assert not isinstance(j, int) or k[0] == KP * j + KP - 1

            rounds(e, round_)

        @block.sync
        def _(e):
            with e.Fori(0, NJ) as j:
                e.wait_ge(s_yd, 16 * (j + 1))
                e.dma_start(m.out[:, bass.ds(P * j, P), :].rearrange("b p f -> p b f"), m.X[:, bass.ds(B * j, B), :]).then_inc(s_out, 16)
            e.wait_ge(s_out, 16 * NJ)


KP = 14


STAGES = (setup, norm_all, local_attention, latent_attention, ffn, split_weights, scan_and_experts)


def mixer_moe(nc, arrays, out, stages=STAGES, dump=None):
    with ExitStack() as ctx:
        m = lay_out(nc, ctx)
        m.out = out
        a = Arrays(arrays)
        for stage in stages:
            stage(nc, ctx, m, a)
        if dump:
            dump(nc, ctx, m)


_INS = {"x": "L0_attn_x", "wq": "L0_attn_wq", "wk": "L0_attn_wk", "wv": "L0_attn_wv", "wgq": "L0_attn_wgq",
        "wgk": "L0_attn_wgk", "wgv": "L0_attn_wgv", "r_out_w": "L0_attn_r_out_w",
        "gate_local_w": "L0_attn_gate_local_w", "gate_remote_w": "L0_attn_gate_remote_w", "w_out": "L0_attn_w_out",
        "f_kernel": "L0_ffn_kernel", "f_sin": "L0_ffn_input_scale", "f_sk": "L0_ffn_kernel_scale",
        "f_bias": "L0_ffn_bias", "A": "L1_attn_A", "B": "L1_attn_B", "W_in": "L1_attn_W_in", "b_in": "L1_attn_b_in",
        "W_gate": "L1_attn_W_gate", "b_gate": "L1_attn_b_gate", "W_out": "L1_attn_W_out", "b_out": "L1_attn_b_out",
        "Wr": "L1_ffn_Wr", "br": "L1_ffn_br", "W1": "L1_ffn_W1", "b1": "L1_ffn_b1", "W2": "L1_ffn_W2",
        "b2": "L1_ffn_b2", "W3": "L1_ffn_W3", "b3": "L1_ffn_b3"}


def kernel(**inputs):
    import numpy as _np
    import concourse.bacc as _bacc
    from concourse import mybir as _mybir
    from concourse.bass_utils import run_bass_kernel_spmd as _run

    nc = _bacc.Bacc("TRN2", target_bir_lowering=False, num_devices=1)
    arrays, aps = {}, []
    for short, name in _INS.items():
        v = _np.ascontiguousarray(inputs[name])
        arrays[f"in_{short}"] = v
        aps.append(nc.dram_tensor(f"in_{short}", v.shape, _mybir.dt.from_np(v.dtype), kind="ExternalInput").ap())
    out = nc.dram_tensor("out_0", (B, S, D), _mybir.dt.float32, kind="ExternalOutput").ap()
    mixer_moe(nc, aps, out)
    r = _run(nc, [arrays], core_ids=[0])
    return r.results[0]["out_0"]
```

```python
from contextlib import ExitStack

import concourse.bass as bass
from concourse import mybir

F32 = mybir.dt.float32
BF16 = mybir.dt.bfloat16
F16 = mybir.dt.float16
U32 = mybir.dt.uint32
ALU = mybir.AluOpType
ACT = mybir.ActivationFunctionType
AX = mybir.AxisListType

P = 128
B, S, D = 8, 1024, 128
NJ = S // P
NU = NJ * B
H, HD = 16, 8
HG, HH = 4, 4
E, DFF = 8, 512
WIN = 32
NB = P // WIN
KW = 2 * WIN
XW = P + WIN
LH, LD, NL = 8, 64, 64
CHUNK = S // NL
NC4 = DFF // P
EPS = 1e-5
NEG = -1.0e30
ISQ = float(1.0 / (8.0 ** 0.5))
STEPS = 7
FIRST = P - STEPS * 2 * E
PARTS = 5
POST_TURN, POST_LOGITS, POST_GAP, POST_SHARES = 5, 9, 12, 14
KP = 10
HALF = 4
N5 = HALF * P



WORK = 14592


class Cut:

    def __init__(self, area):
        self.area, self.at = area, 0

    def take(self, n, dt=F32):
        words = n if dt == F32 else (n + 1) // 2
        words += words % 2
        v = self.area[:, self.at:self.at + words]
        self.at += words
        assert self.at <= WORK, self.at
        return v if dt == F32 else v.bitcast(dt)


class Memory:
    pass


class Arrays:

    def __init__(self, aps):
        (self.x, self.wq, self.wk, self.wv, self.wgq, self.wgk, self.wgv, self.r_out_w, self.gate_local_w,
         self.gate_remote_w, self.w_out, self.f_kernel, self.f_sin, self.f_sk, self.f_bias, self.A, self.B,
         self.W_in, self.b_in, self.W_gate, self.b_gate, self.W_out, self.b_out, self.Wr, self.br, self.W1, self.b1,
         self.W2, self.b2, self.W3, self.b3) = aps


def lay_out(nc, ctx):
    def sb(name, shape, dt=F32):
        return ctx.enter_context(nc.sbuf_tensor(name, shape, dt))

    m = Memory()
    m.X = sb("X", [P, NU, D])
    m.xnT = sb("xnT", [P, NU + B, XW])
    m.mix = sb("mix", [P, NU, D])
    m.work = sb("work", [P, WORK])
    wflat = m.xnT[:, :, :].rearrange("p u x -> p (u x)").bitcast(F16)
    ef = E * DFF
    m.W1h, m.W1l, m.W2h, m.W2l = [wflat[:, n * ef:(n + 1) * ef].rearrange("p (e f) -> p e f", e=E) for n in range(4)]
    mflat = m.mix[:, :, :].rearrange("p u x -> p (u x)")
    m.Wst = mflat[:, 0:ef]
    m.W3s = mflat[:, ef:2 * ef].rearrange("p (e n) -> p e n", e=E)
    m.stats = sb("stats", [P, NU, 6])
    m.mv = sb("mv", [P, NU, 2])
    m.rstd = sb("rstd", [P, NU])
    m.nhalf = sb("nhalf", [P, NU])
    m.ident = sb("ident", [P, P])
    m.identb = sb("identb", [P, P], BF16)
    m.identh = sb("identh", [P, P], F16)
    m.hm = sb("hm", [P, HH])
    m.par = sb("par", [P, 2])
    m.lhm = sb("lhm", [P, LH])
    m.m16 = sb("m16", [P, H])
    m.cmask = sb("cmask", [P, 2, NB, KW])
    m.wq = sb("wq", [P, D])
    m.wk = sb("wk", [P, D])
    m.wv = sb("wv", [P, D])
    m.wgq = sb("wgq", [P, 2 * LD])
    m.wgk = sb("wgk", [P, 2 * LD])
    m.wgv = sb("wgv", [P, LD])
    m.wout = sb("wout", [P, D])
    m.wr = sb("wr", [P, E])
    m.gbd = sb("gbd", [P, 2 * H])
    m.wg = sb("wg", [P, 2 * H])
    m.gcol = sb("gcol", [P, 2])
    m.bcol = sb("bcol", [P, 3])
    m.bout = sb("bout", [P, D])
    m.fsc = sb("fsc", [P, 5])
    m.br = sb("br", [P, E])
    m.iota8 = sb("iota8", [P, E])
    m.routp = sb("routp", [P, D])
    m.w5T = sb("w5T", [P, 6, D])
    m.fk = sb("fk", [P, D], BF16)
    m.fkq = sb("fkq", [P, D], BF16)
    m.fbias = sb("fbias", [P, D], BF16)
    m.b12 = sb("b12", [P, 2, NC4, E])
    m.st4 = sb("st4", [P, B, 6])
    m.mv4 = sb("mv4", [P, B, 2])
    m.tick = sb("tick", [P, 8])
    m.rstd4 = sb("rstd4", [P, B])[:, :]
    gk = sb("gk", [P, 2 * B * LH * NL], F16)
    m.gkh, m.gkl = [gk[:, n * B * LH * NL:(n + 1) * B * LH * NL].rearrange("p (b n) -> p b n", b=B) for n in range(2)]
    m.b3bd = gk[0:B * E, 0:2 * B * D].bitcast(F32)
    m.gvx = m.work[:, WORK - B * NC4 * 18:].rearrange("p (k g c) -> p k g c", g=2, c=9)
    m.gvh, m.gvl = [sb(n, [P, B * NC4, 2, 9], F16) for n in ("gvh", "gvl")]
    m.glr = sb("glr", [P, NU, 2 * H])
    m.psum = ctx.enter_context(nc.psum_tensor("psum", [P, 8 * 512], F32))
    m.ps = [m.psum[:, 512 * n:512 * (n + 1)] for n in range(8)]
    return m


def setup(nc, ctx, m, a):
    s_w = ctx.enter_context(nc.semaphore("s_w"))
    s_const = ctx.enter_context(nc.semaphore("s_const"))
    s_dve = ctx.enter_context(nc.semaphore("s_setup_dve"))
    s_pe = ctx.enter_context(nc.semaphore("s_setup_pe"))
    m.s_x = [ctx.enter_context(nc.semaphore(f"s_x{j}")) for j in range(NJ)]
    loads = []
    c = Cut(m.work)
    m.raw5 = c.take(5 * D).rearrange("p (n d) -> p n d", n=5)
    m.b12r = c.take(2 * DFF)[0:E].rearrange("p (n d) -> p n d", n=2)
    m.rout = c.take(D)[0:LD]

    def ld(dst, src):
        loads.append((dst, src))

    def rowb(v):
        return v.rearrange("(o n) -> o n", o=1).broadcast_to([P, v.shape[0]])

    for dst, src in ((m.wq, a.wq), (m.wk, a.wk), (m.wv, a.wv), (m.wgq[:, 0:LD], a.wgq), (m.wgq[:, LD:2 * LD], a.wgq),
                     (m.wgk[:, 0:LD], a.wgk), (m.wgk[:, LD:2 * LD], a.wgk), (m.wgv, a.wgv),
                     (m.rout, a.r_out_w), (m.fk, a.f_kernel), (m.wr, a.Wr)):
        ld(dst[:, :], src)
    wo_v = a.w_out.rearrange("(r g h d) n -> r h g d n", r=2, g=2, h=HH)
    for r in range(2):
        for h in range(HH):
            for g in range(2):
                at = 64 * r + 16 * h + 8 * g
                ld(m.wout[at:at + 8, :], wo_v[r, h, g])
    ld(m.gcol[:, 0:1], a.gate_local_w.rearrange("h (d o) -> (h d) o", o=1))
    ld(m.gcol[:, 1:2], a.gate_remote_w.rearrange("h (d o) -> (h d) o", o=1))
    for n, w in enumerate((a.A, a.B, a.W_in, a.W_gate, a.W_out)):
        ld(m.raw5[:, n, :], w)
    ld(m.bcol[:, 0:1], a.b_in.rearrange("(d o) -> d o", o=1))
    ld(m.bcol[:, 1:2], a.b_gate.rearrange("(d o) -> d o", o=1))
    ld(m.bout[:, :], rowb(a.b_out))
    ld(m.fbias[:, :], rowb(a.f_bias))
    ld(m.fsc[:, 0:1], rowb(a.f_sin))
    ld(m.fsc[:, 1:2], rowb(a.f_sk))
    ld(m.br[:, :], rowb(a.br))
    for n, b in enumerate((a.b1, a.b2)):
        ld(m.b12r[:, n, :], b)

    with nc.Block() as block:
        @block.sync
        def _(sp):
            for j in range(NJ):
                sp.dma_start(m.X[:, B * j:B * (j + 1), :],
                             a.x[:, P * j:P * (j + 1), :].rearrange("b p f -> p b f")).then_inc(m.s_x[j], 16)

        @block.scalar
        def _(act):
            for dst, src in loads:
                act.dma_start(dst, src).then_inc(s_w, 16)

        @block.gpsimd
        def _(e):
            done = [0]

            def step(ins):
                ins.then_inc(s_const, 1)
                done[0] += 1
                e.wait_ge(s_const, done[0])

            step(e.memset(m.ident[:, :], 0.0))
            step(e.affine_select(out=m.ident[:, :], in_=m.ident[:, :], compare_op=ALU.not_equal, fill=1.0, base=0,
                                 pattern=[[-1, P]], channel_multiplier=1))
            step(e.memset(m.gvx[:, :, :, :], 1.0))
            m.const_ident = done[0]
            step(e.memset(m.nhalf[:, :], -0.5))
            step(e.memset(m.xnT[:, 0:B, 0:WIN], 0.0))
            step(e.iota(m.iota8[:, :], pattern=[[1, E]], base=0, channel_multiplier=0,
                        allow_small_or_imprecise_dtypes=True))
            step(e.memset(m.cmask[:, :, :, :], 0.0))
            for q in range(HH):
                v = m.cmask[WIN * q:WIN * (q + 1), :, :, :].rearrange("p v b k -> p (v b) k")
                step(e.affine_select(out=v, in_=v, compare_op=ALU.is_ge, fill=NEG, base=-1,
                                     pattern=[[0, 2 * NB], [1, KW]], channel_multiplier=-1))
                step(e.affine_select(out=v, in_=v, compare_op=ALU.is_ge, fill=NEG, base=WIN,
                                     pattern=[[0, 2 * NB], [-1, KW]], channel_multiplier=1))
            step(e.affine_select(out=m.cmask[:, 1, 0, :], in_=m.cmask[:, 1, 0, :], compare_op=ALU.is_ge, fill=NEG,
                                 base=-WIN, pattern=[[1, KW]], channel_multiplier=0))

        @block.vector
        def _(e):
            done = [0]

            def step(ins):
                ins.then_inc(s_dve, 1)
                done[0] += 1
                e.wait_ge(s_dve, done[0])

            e.wait_ge(s_const, m.const_ident)
            step(e.tensor_reduce(m.hm[:, :], m.ident[:, :].rearrange("p (a h d) -> p h a d", a=HG, h=HH), axis=AX.XY, op=ALU.add))
            step(e.tensor_scalar(m.hm[:, :], m.hm[:, :], ISQ, None, ALU.mult))
            step(e.tensor_reduce(m.par[:, :], m.ident[:, :].rearrange("p (r k) -> p r k", r=2), axis=AX.X, op=ALU.add))
            step(e.tensor_reduce(m.lhm[:, :], m.ident[:, :].rearrange("p (r h d) -> p h r d", r=2, h=LH), axis=AX.XY, op=ALU.add))
            step(e.tensor_scalar(m.lhm[:, :], m.lhm[:, :], 1.0 / CHUNK, None, ALU.mult))
            for r in range(2):
                for g in range(2):
                    step(e.tensor_reduce(m.m16[:, 8 * r + g:8 * r + 8:2],
                                         m.ident[:, 64 * r + 32 * g:64 * r + 32 * g + 32].rearrange("p (h d) -> p h d", h=HH),
                                         axis=AX.X, op=ALU.add))
            step(e.tensor_copy(m.identb[:, :], m.ident[:, :]))
            step(e.tensor_copy(m.identh[:, :], m.ident[:, :]))
            step(e.memset(m.routp[LD:P, :], 0.0))
            for g in range(2):
                step(e.tensor_scalar(m.gvx[:, :, g, 8], m.gvx[:, :, g, 8], m.par[:, g:g + 1], None, ALU.mult))
            for j in range(NJ):
                e.wait_ge(m.s_x[j], 16)
                for u in range(B * j, B * (j + 1)):
                    last = e.bn_stats(m.stats[:, u, :], m.X[:, u, :])
            step(last)
            e.wait_ge(s_w, 16 * len(loads))
            for n in range(2):
                step(e.tensor_scalar(m.gbd[:, H * n:H * (n + 1)], m.m16[:, :], m.gcol[:, n:n + 1], None, ALU.mult))
            step(e.tensor_scalar(m.wout[:, :], m.wout[:, :], 0.5, None, ALU.mult))
            step(e.tensor_scalar(m.bcol[:, 2:3], m.bcol[:, 1:2], 0.5, None, ALU.mult))
            for r in range(2):
                for g in range(2):
                    step(e.tensor_copy(m.routp[0:LD, 64 * r:64 * r + 64].rearrange("p (h g d) -> p h g d", h=HH, g=2)[:, :, g, :],
                                       m.rout[:, 64 * r + 32 * g:64 * r + 32 * g + 32].rearrange("p (h d) -> p h d", h=HH)))
            step(e.reciprocal(m.fsc[:, 2:4], m.fsc[:, 0:2]))
            step(e.tensor_tensor(m.fsc[:, 4:5], m.fsc[:, 0:1], m.fsc[:, 1:2], ALU.mult))
            t, q, w = c.take(D), c.take(D), c.take(D)
            step(e.tensor_scalar(t, m.fk[:, :], m.fsc[:, 3:4], None, ALU.mult))
            step(round_e4m3fn(e, step, t, q, w, m.fkq[:, :]))
            e.wait_ge(s_pe, 1)
            step(e.tensor_copy(m.w5T[:, 0:4, :].rearrange("p n d -> p (n d)"), m.ps[0][:, :]))
            step(e.tensor_copy(m.w5T[:, 4:6, :].rearrange("p n d -> p (n d)"), m.ps[1][:, 0:256]))
            step(e.tensor_copy(m.b12[:, :, :, :].rearrange("p n j e -> p (n j e)"), m.ps[1][:, 256:256 + 2 * NC4 * E]))
            e.wait_ge(s_pe, 2)
            step(e.tensor_copy(m.wg[:, :], m.ps[2][:, 0:2 * H]))
            m.setup_steps = done[0]

        @block.tensor
        def _(e):
            e.wait_ge(s_const, m.const_ident)
            e.wait_ge(s_w, 16 * len(loads))
            for n in range(6):
                src = m.raw5[:, n, :] if n < 5 else m.wq[:, :]
                last = e.transpose(m.ps[n // 4][:, D * (n % 4):D * (n % 4) + D], src, m.ident[:, :])
            for n in range(2):
                for j in range(NC4):
                    last = e.transpose(m.ps[1][:, 256 + E * (NC4 * n + j):256 + E * (NC4 * n + j + 1)],
                                       m.b12r[:, n, P * j:P * (j + 1)], m.ident[0:E, 0:E])
            last.then_inc(s_pe, 1)
            e.wait_ge(s_dve, m.setup_steps - 1)
            e.matmul(m.ps[2][:, 0:2 * H], m.w5T[:, 5, :], m.gbd[:, :], start=True, stop=True).then_inc(s_pe, 1)


def round_e4m3fn(e, step, t, q, w, out):
    step(e.tensor_scalar(w.bitcast(U32), t.bitcast(U32), 0x7F800000, None, ALU.bitwise_and))
    step(e.tensor_scalar(w, w, 2.0 ** -6, 1.5 * 2.0 ** 20, ALU.max, ALU.mult))
    step(e.tensor_tensor(q, t, w, ALU.add))
    step(e.tensor_tensor(q, q, w, ALU.subtract))
    step(e.tensor_scalar(w.bitcast(U32), q.bitcast(U32), 0x7FFFFFFF, None, ALU.bitwise_and))
    step(e.tensor_scalar(w, w, 448.0, 448.0, ALU.max, ALU.subtract))
    step(e.tensor_scalar(w, w, 3.0e38, 0.0, ALU.mult, ALU.mult))
    return e.tensor_tensor(out, q, w, ALU.add)


MOMENTS = 6


def moments(e, s_step, before, st, mean, ve):
    n = [0]

    def step(ins):
        ins.then_inc(s_step, 1)
        n[0] += 1
        e.wait_ge(s_step, before + n[0])

    m1, q1, m2, q2 = (st[:, :, k] for k in (1, 2, 4, 5))
    step(e.tensor_tensor(mean, m1, m2, ALU.subtract))
    step(e.scalar_tensor_tensor(ve, mean, 0.25, mean, ALU.mult, ALU.mult))
    step(e.tensor_tensor(q1, q1, q2, ALU.add))
    step(e.scalar_tensor_tensor(ve, q1, 1.0 / D, ve, ALU.mult, ALU.add))
    step(e.tensor_tensor(mean, m1, m2, ALU.add))
    e.tensor_scalar(mean, mean, 0.5, None, ALU.mult)
    step(e.tensor_scalar(ve, ve, EPS, None, ALU.add))
    assert n[0] == MOMENTS


def norm_all(nc, ctx, m, a):
    def sem(name):
        return ctx.enter_context(nc.semaphore(name))
    s_var, s_rs = sem("ln1_var"), sem("ln1_rstd")
    s_xn, s_tr, s_cp, s_tail, s_pool = sem("ln1_normed"), sem("ln1_turned"), sem("ln1_stored"), sem("ln1_tails"), sem("ln1_pooled")
    s_lat, s_gk = sem("latents_made"), sem("latents_kept")
    c = Cut(m.work)
    xn = [c.take(B * D).rearrange("p (b d) -> p b d", b=B) for _ in range(2)]
    m.pool = c.take(B * NL).rearrange("p (b n) -> p b n", b=B)
    pool2 = c.take(B * 2 * NL).rearrange("p (b o n) -> p b o n", b=B, o=2)
    gk = c.take(B * LH * NL).rearrange("p (b h n) -> p b h n", b=B, h=LH)
    s_hi = sem("latents_high")

    with nc.Block() as block:
        @block.vector
        def _(e):
            moments(e, s_var, 0, m.stats[:, :, :], m.mv[:, :, 0], m.mv[:, :, 1])
            e.wait_ge(s_rs, 1)

            def norm(j, k):
                for b in range(B):
                    last = e.tensor_scalar(xn[k][:, b, :], m.X[:, B * j + b, :], m.mv[:, B * j + b, 0:1],
                                           m.rstd[:, bass.ds(B * j + b, 1)], ALU.subtract, ALU.mult)
                last.then_inc(s_xn, 1)

            def pooled(j):
                e.wait_ge(s_cp, 2 * j + 2)
                e.tensor_reduce(m.pool[:, :, bass.ds(8 * j, 8)],
                                m.xnT[:, bass.ds(B * j, B), WIN:XW].rearrange("p b (n t) -> p b n t", t=CHUNK), axis=AX.X, op=ALU.add).then_inc(s_pool, 1)

            norm(0, 0)
            norm(1, 1)
            with e.Fori(0, NJ // 2 - 1) as jj:
                for k in range(2):
                    j = 2 * jj
                    e.wait_ge(s_tr, 2 * (j + k) + 2)
                    norm(j + k + 2, k)
                    pooled(j + k)
            pooled(NJ - 2)
            pooled(NJ - 1)
            e.wait_ge(s_lat, 1)
            for b in range(B):
                e.tensor_tensor(gk[:, b, :, :],
                                m.ps[4][:, NL * b:NL * (b + 1)].rearrange("p (o n) -> p o n", o=1).broadcast_to([P, LH, NL]),
                                m.lhm[:, :].rearrange("p (h o) -> p h o", o=1).broadcast_to([P, LH, NL]), ALU.mult).then_inc(s_gk, 1)
            for g in range(2):
                last = e.tensor_scalar(m.gvx[:, :, g, 0:8], m.ps[5][:, :].rearrange("p (k g d) -> p k g d", g=2, d=8)[:, :, g, :],
                                       m.par[:, g:g + 1], 1.0 / CHUNK, ALU.mult, ALU.mult)
            last.then_inc(s_gk, 1)
            for b in range(B):
                e.wait_ge(s_hi, b + 1)
                e.tensor_tensor(m.gkl[:, b, :], gk[:, b, :, :].rearrange("p h n -> p (h n)"), m.gkh[:, b, :], ALU.subtract)
            e.wait_ge(s_hi, B + 1)
            e.tensor_tensor(m.gvl[:, :, :, :], m.gvx[:, :, :, :], m.gvh[:, :, :, :], ALU.subtract).then_inc(s_gk, 1)

        @block.gpsimd
        def _(e):
            e.wait_ge(s_var, MOMENTS)
            e.tensor_tensor(m.rstd[:, :], m.mv[:, :, 1], m.nhalf[:, :], ALU.pow).then_inc(s_rs, 1)
            with e.Fori(0, NJ) as j:
                e.wait_ge(s_cp, 2 * j + 2)
                e.tensor_copy(m.xnT[:, bass.ds(B * j + B, B), 0:WIN], m.xnT[:, bass.ds(B * j, B), P:XW]).then_inc(s_tail, 1)
            e.wait_ge(s_pool, NJ)
            e.tensor_copy(pool2[:, :, :, :], m.pool[:, :, :].rearrange("p b (o n) -> p b o n", o=1).broadcast_to([P, B, 2, NL])).then_inc(s_pool, 1)

        @block.tensor
        def _(e):
            def turn(j, k):
                e.wait_ge(s_xn, j + 1)
                for h in range(2):
                    if not isinstance(j, int) or j >= 2:
                        e.wait_ge(s_cp, 2 * (j - 2) + h + 1)
                    for b in range(HALF):
                        last = e.transpose(m.ps[2 * k + h][:, D * b:D * (b + 1)], xn[k][:, HALF * h + b, :], m.ident[:, :])
                    last.then_inc(s_tr, 1)

            turn(0, 0)
            turn(1, 1)
            with e.Fori(1, NJ // 2) as jj:
                for k in range(2):
                    turn(2 * jj + k, k)
            e.wait_ge(s_pool, NJ + 1)
            e.matmul(m.ps[4][:, :], m.wgk[:, :], m.pool[:, :, :].rearrange("p b n -> p (b n)"), start=True, stop=True)
            for b in range(B):
                last = e.matmul(m.ps[5][:, LD * b:LD * (b + 1)],
                                pool2[:, b, :, :].rearrange("p o n -> p (o n)"),
                                m.wgv[:, :], start=True, stop=True)
            last.then_inc(s_lat, 1)

        @block.scalar
        def _(e):
            def store(j, k):
                for h in range(2):
                    e.wait_ge(s_tr, 2 * j + h + 1)
                    e.copy(m.xnT[:, bass.ds(B * j + HALF * h, HALF), WIN:XW], m.ps[2 * k + h][:, :].rearrange("p (b t) -> p b t", b=HALF)).then_inc(s_cp, 1)
            with e.Fori(0, NJ // 2) as jj:
                for k in range(2):
                    store(2 * jj + k, k)
            for b in range(B):
                e.wait_ge(s_gk, b + 1)
                e.copy(m.gkh[:, b, :], gk[:, b, :, :].rearrange("p h n -> p (h n)")).then_inc(s_hi, 1)
            e.wait_ge(s_gk, B + 1)
            e.copy(m.gvh[:, :, :, :], m.gvx[:, :, :, :]).then_inc(s_hi, 1)


def wait(e, semaphore, value):
    if not isinstance(value, int) or value > 0:
        e.wait_ge(semaphore, value)


def skewed(e, front, back, n, peeled=1):
    def body(t):
        front(2 * t + 1, 1)
        back(2 * t, 0)
        front(2 * t + 2, 0)
        back(2 * t + 1, 1)

    front(0, 0)
    for t in range(peeled):
        body(t)
    with e.Fori(peeled, n // 2 - 1) as t:
        body(t)
    front(n - 1, 1)
    back(n - 2, 0)
    back(n - 1, 1)


def local_attention(nc, ctx, m, a):
    def sem(name):
        return ctx.enter_context(nc.semaphore("local_" + name))
    s_xd, s_qkg, s_kt, s_gt, s_qx, s_v, s_vx, s_ones = (sem(n) for n in ("windows", "qkg", "k", "gates", "q", "v", "v_kept", "ones"))
    s_sc, s_sm, s_mx, s_sub, s_exp = (sem(n) for n in ("scores", "masked", "max", "shifted", "exp"))
    s_t, s_ptd, s_pta, s_pv, s_rec, s_o = (sem(n) for n in ("turned", "turned_dve", "turned_act", "pv", "norm", "out"))
    NP = NU // 2
    NG = 4
    c = Cut(m.work)
    xd = [c.take(NB * 2 * KW).rearrange("p (b o k) -> p b o k", b=NB, o=2) for _ in range(2)]
    qx = [c.take(NB * P).rearrange("p (b h q) -> p b h q", b=NB, h=HH) for _ in range(2)]
    kx = [c.take(HG * XW).rearrange("p (g t) -> p g t", g=HG) for _ in range(2)]
    vx = c.take(4 * 576).rearrange("p (n g c) -> p n g c", g=2, c=9)
    Sc = [c.take(4 * 2 * HG * KW).rearrange("p (n u k) -> p n u k", n=4, u=2 * HG) for _ in range(2)]
    Pr = c.take(2 * NB * HG * KW).rearrange("p (u g k) -> p u g k", u=2 * NB, g=HG)
    PT = c.take(NG * NB * P).rearrange("p (n b c) -> p n b c", n=NG, b=NB)
    mx = c.take(2 * 4 * 2 * HG).rearrange("p (v n u) -> p v n u", v=2, n=4)
    rec = c.take(2 * H).rearrange("p (u s) -> p u s", u=2)
    bank_s, bank_t, bank_q, bank_v = m.ps[0:4], m.ps[4:6], m.ps[6], m.ps[7]

    def vbuf(v, k):
        return vx[:, 32 * (2 * v + k):32 * (2 * v + k) + 32, :, :]

    with nc.Block() as block:
        @block.gpsimd
        def _(e):
            def windows(i):
                for k in range(2):
                    wait(e, s_v, 2 * i + k - 1)
                    for h in range(2):
                        e.tensor_copy(xd[k][:, :, :, WIN * h:WIN * h + WIN],
                                      m.xnT[:, 2 * i + k, WIN * h:WIN * h + P].rearrange("p (b o k) -> p b o k", b=NB, o=1)
                                      .broadcast_to([P, NB, 2, WIN])).then_inc(s_xd, 1)

            def front(i, v):
                if not (isinstance(i, int) and i == NP - 1):
                    windows(i + 1)
                for n in range(4):
                    e.wait_ge(s_mx, 4 * i + n + 1)
                    e.tensor_tensor(Sc[v][:, n, :, :], Sc[v][:, n, :, :],
                                    mx[:, v, n, :].rearrange("p (u o) -> p u o", o=1).broadcast_to([P, 2 * HG, KW]),
                                    ALU.subtract).then_inc(s_sub, 1)

            windows(0)
            skewed(e, front, lambda i, v: None, NP)

        @block.tensor
        def _(e):
            def turn(i, k):
                e.wait_ge(s_exp, 2 * i + k + 1)
                for r in range(2):
                    if k == 0:
                        wait(e, s_pta if r else s_ptd, 2 * i)
                    else:
                        e.wait_ge(s_pta if r else s_ptd, 2 * i + 1)
                    for b in range(NB):
                        last = e.transpose(bank_t[r][:, P * b:P * b + P],
                                           Pr[:, NB * k + b, 2 * r:2 * r + 2, :].rearrange("p g k -> p (g k)"), m.ident[:, :])
                    last.then_inc(s_t, 1)

            def front(i, v):
                for k in range(2):
                    if not (isinstance(i, int) and i == 0):
                        turn(i - 1, k)
                    u = 2 * i + k
                    wait(e, s_qx, u)
                    e.wait_ge(s_xd, 2 * u + 2)
                    e.matmul(bank_q[:, 0:P], m.wq[:, :], m.xnT[:, u, WIN:XW], start=True, stop=True)
                    e.matmul(bank_q[:, P:P + XW], m.wk[:, :], m.xnT[:, u, :], start=True, stop=True)
                    for b in range(NB):
                        last = e.matmul(bank_q[WIN * b:WIN * b + WIN, P + XW:P + XW + 2 * H], xd[k][:, b, 0, WIN:KW],
                                        m.wg[:, :], start=True, stop=True)
                    last.then_inc(s_qkg, 1)
                    if k == 0:
                        wait(e, s_o, i - 1)
                    wait(e, s_vx, u)
                    for b in range(NB):
                        last = e.matmul(bank_v[:, D * b:D * b + D], xd[k][:, b, :, :].rearrange("p o k -> p (o k)"),
                                        m.wv[:, :], start=True, stop=True)
                    last.then_inc(s_v, 1)
                e.wait_ge(s_kt, 2 * i + 2)
                e.wait_ge(s_qx, 2 * i + 2)
                for n in range(4):
                    wait(e, s_sm, 4 * (i - 1) + n + 1)
                    k = n // 2
                    for t in range(2):
                        b = 2 * (n % 2) + t
                        last = e.matmul(bank_s[n][:, HG * KW * t:HG * KW * (t + 1)], qx[k][:, b, :, :].rearrange("p h q -> p (h q)"),
                                        kx[k][:, :, WIN * b:WIN * b + KW], start=True, stop=True)
                    last.then_inc(s_sc, 1)

            def back(i, v):
                if isinstance(i, int) and i == NP - 1:
                    for k in range(2):
                        turn(i, k)
                e.wait_ge(s_vx, 2 * i + 2)
                wait(e, s_v, 2 * i + 2)
                for n in range(NG):
                    k, r = n // 2, n % 2
                    e.wait_ge(s_ptd if n % 2 == 0 else s_pta, 2 * i + n // 2 + 1)
                    for b in range(NB):
                        for h in range(HH):
                            at = 144 * k + 18 * (HH * r + h)
                            last = e.matmul(bank_v[WIN * b:WIN * b + WIN, at:at + 18], PT[:, n, b, WIN * h:WIN * h + WIN],
                                            vbuf(v, k)[:, 8 * b + 4 * r + h, :, :].rearrange("p g c -> p (g c)"),
                                            start=True, stop=True)
                last.then_inc(s_pv, 1)

            def back_after(i, v):
                wait(e, s_vx, 2 * i + 4) if not (isinstance(i, int) and i == NP - 1) else None
                back(i, v)
            skewed(e, front, back_after, NP)

        @block.vector
        def _(e):
            e.memset(vx[:, :, :, :], 1.0).then_inc(s_ones, 1)
            e.wait_ge(s_ones, 1)
            for g in range(2):
                last = e.tensor_scalar(vx[:, :, g, 8], vx[:, :, g, 8], m.par[:, g:g + 1], None, ALU.mult)
            last.then_inc(s_ones, 1)
            for k in range(2):
                e.memset(kx[k], 0.0).then_inc(s_ones, 1)

            def keep(i, k):
                wait(e, s_pv, i)
                e.wait_ge(s_t, 4 * i + 2 * k + 1)
                e.tensor_copy(PT[:, 2 * k, :, :].rearrange("p b c -> p (b c)"), bank_t[0][:, :]).then_inc(s_ptd, 1)

            def front(i, v, var):
                for k in range(2):
                    if not (isinstance(i, int) and i == 0):
                        keep(i - 1, k)
                    u = 2 * i + k
                    e.wait_ge(s_gt, u + 1)
                    wait(e, s_sc, 4 * i)
                    e.tensor_tensor(qx[k].rearrange("p b h q -> p h b q"),
                                    bank_q[:, 0:P].rearrange("p (o b q) -> p o b q", o=1, b=NB).broadcast_to([P, HH, NB, WIN]),
                                    m.hm[:, :].rearrange("p (h o w) -> p h o w", o=1, w=1).broadcast_to([P, HH, NB, WIN]),
                                    ALU.mult).then_inc(s_qx, 1)
                for n in range(4):
                    e.wait_ge(s_sc, 4 * i + n + 1)
                    wait(e, s_exp, 2 * (i - 1))
                    half = slice(2 * (n % 2), 2 * (n % 2) + 2)
                    e.tensor_tensor(Sc[v][:, n, :, :].rearrange("p (b g) k -> p b g k", b=2),
                                    bank_s[n][:, :].rearrange("p (b g k) -> p b g k", b=2, g=HG),
                                    m.cmask[:, var, half, :].rearrange("p b (o k) -> p b o k", o=1).broadcast_to([P, 2, HG, KW]),
                                    ALU.add).then_inc(s_sm, 1)
                    e.wait_ge(s_sm, 4 * i + n + 1)
                    e.tensor_reduce(mx[:, v, n, :], Sc[v][:, n, :, :], axis=AX.X, op=ALU.max).then_inc(s_mx, 1)

            def back(i, v):
                if isinstance(i, int) and i == NP - 1:
                    for k in range(2):
                        keep(i, k)
                e.wait_ge(s_pv, i + 1)
                o = bank_v[:, 0:288].rearrange("p (u s c) -> p u s c", u=2, c=9)
                e.reciprocal(rec, o[:, :, :, 8]).then_inc(s_rec, 1)
                e.wait_ge(s_rec, 2 * i + 1)
                e.scalar_tensor_tensor(rec, m.glr[:, bass.ds(2 * i, 2), 0:H], 1.0, rec, ALU.add, ALU.mult).then_inc(s_rec, 1)
                e.wait_ge(s_rec, 2 * i + 2)
                e.tensor_tensor(m.mix[:, bass.ds(2 * i, 2), :].rearrange("p u (s d) -> p u s d", d=HD), o[:, :, :, 0:8],
                                rec.rearrange("p u (s o) -> p u s o", o=1).broadcast_to([P, 2, H, HD]), ALU.mult).then_inc(s_o, 1)

            def front_by_span(i, v):
                front(i, v, 1 if isinstance(i, int) and i < B // 2 else 0)
            skewed(e, front_by_span, back, NP, 2)

        @block.scalar
        def _(e):
            def keep(i, k):
                wait(e, s_pv, i)
                e.wait_ge(s_t, 4 * i + 2 * k + 2)
                e.copy(PT[:, 2 * k + 1, :, :].rearrange("p b c -> p (b c)"), bank_t[1][:, :]).then_inc(s_pta, 1)

            def exps(i, v):
                wait(e, s_t, 4 * i)
                for h in range(2):
                    e.wait_ge(s_sub, 4 * i + 2 * h + 2)
                    e.activation(Pr[:, NB * h:NB * h + NB, :, :].rearrange("p b g k -> p (b g k)"),
                                 Sc[v][:, 2 * h:2 * h + 2, :, :].rearrange("p n u k -> p (n u k)"), ACT.Exp).then_inc(s_exp, 1)

            def front(i, v):
                for k in range(2):
                    if not (isinstance(i, int) and i == 0):
                        keep(i - 1, k)
                    u = 2 * i + k
                    wait(e, s_sc, 4 * i)
                    e.wait_ge(s_qkg, u + 1)
                    if isinstance(i, int) and i == 0:
                        e.wait_ge(s_ones, 4)
                    for g in range(HG):
                        rows = slice(WIN * g, WIN * g + WIN)
                        last = e.copy(kx[k][rows, g, :], bank_q[rows, P:P + XW])
                    last.then_inc(s_kt, 1)
                    e.activation(m.glr[:, u, :], bank_q[:, P + XW:P + XW + 2 * H], ACT.Tanh, scale=0.5).then_inc(s_gt, 1)
                    e.wait_ge(s_v, u + 1)
                    if k == 0:
                        wait(e, s_pv, i - 1)
                    for g in range(2):
                        for r in range(2):
                            o = vbuf(v, k)[:, :, g, 0:8].rearrange("p (b r h) d -> p r b h d", b=NB, r=2)[:, r]
                            x = bank_v[:, :].rearrange("p (b r g h d) -> p r g b h d", b=NB, r=2, g=2, h=HH)[:, r, g]
                            last = e.activation(o, x, ACT.Copy, scale=m.par[:, g:g + 1])
                    last.then_inc(s_vx, 1)
                exps(i, v)

            def back(i, v):
                if isinstance(i, int) and i == NP - 1:
                    for k in range(2):
                        keep(i, k)

            skewed(e, front, back, NP)


def pipeline(e, stages, n, width, first, in_order=False):
    if not in_order:
        stages = sorted(stages, key=lambda x: -x[0])
    for r in range(first):
        for lag, f in stages:
            if r - lag >= 0:
                f(r - lag, (r - lag) % width, (r - lag) // width)
    with e.Fori(first // width, n // width) as t:
        for r in range(width):
            for lag, f in stages:
                f(width * t + (r - lag), (r - lag) % width, t + (r - lag) // width)
    for r in range(n, n + max(lag for lag, _ in stages)):
        for lag, f in stages:
            if r - lag < n:
                f(r - lag, (r - lag) % width, (r - lag) // width)


def latent_attention(nc, ctx, m, a):
    def sem(name):
        return ctx.enter_context(nc.semaphore("latent_" + name))
    s_gq, s_gqk, s_sc, s_sm, s_mx, s_sub, s_exp = (sem(n) for n in ("q", "q_kept", "scores", "masked", "max", "shifted", "exp"))
    s_t, s_pt, s_pv, s_rec, s_lat, s_t2, s_lt, s_rm, s_gr = (sem(n) for n in ("turned", "turned_kept", "pv", "recip", "normed", "out_turned", "out_kept", "remote", "gated"))
    s_ql, s_ph, s_pl = (sem(n) for n in ("q_low", "weights_high", "weights_low"))
    s_mix, s_t3, s_mt, s_wo, s_x, s_st = (sem(n) for n in ("mixed", "mix_turned", "mix_kept", "projected", "added", "stats"))
    W = B
    c = Cut(m.work)

    def two(n, shape=None, **k):
        out = [c.take(n) for _ in range(2)]
        return [v.rearrange(shape, **k) for v in out] if shape else out
    gq = [c.take(P, F16) for _ in range(2)]
    Sl = two(LH * NL, "p (h n) -> p h n", h=LH)
    Pl = two(LH * NL)
    Ph = [c.take(2 * LH * NL, F16) for _ in range(2)]
    PT = [c.take(2 * LH * NL, F16) for _ in range(2)]
    latf = two(D)
    lat = [v[:, 0:LD].rearrange("p (h d) -> p h d", h=LH) for v in latf]
    rec = two(LH)
    mxl = two(LH)
    latT = two(P)
    rem = two(D)
    fin = two(D)
    finT = two(P)
    lmask = c.take(NJ * NL).rearrange("p (j n) -> p j n", j=NJ)
    s_lm = sem("mask")
    bq, bs, bw, bt, bo, b2, br, b3 = m.ps

    with nc.Block() as block:
        @block.tensor
        def _(e):
            def q(u, k, j):
                wait(e, s_ql, u)
                e.matmul(bq[:, 0:P], m.wgq[:, :], m.xnT[:, u, WIN:XW], start=True, stop=True).then_inc(s_gq, 1)

            def scores(u, k, j):
                e.wait_ge(s_ql, u + 1)
                wait(e, s_sm, u)
                e.matmul(bs[:, :], gq[k % 2], m.gkh[:, k, :], start=True, stop=False)
                e.matmul(bs[:, :], gq[k % 2], m.gkl[:, k, :], start=False, stop=True).then_inc(s_sc, 1)

            def turn(u, k, j):
                e.wait_ge(s_pl, u + 1)
                wait(e, s_pt, u)
                for n in range(8):
                    last = e.transpose(bt.bitcast(F16)[:, P * n:P * n + P], Ph[k % 2][:, P * n:P * n + P], m.identh[:, :])
                last.then_inc(s_t, 1)

            def pv(u, k, j):
                e.wait_ge(s_pt, u + 1)
                wait(e, s_lat, u)
                for n in range(4):
                    high, low = PT[k % 2][:, P * n:P * n + P], PT[k % 2][:, P * (4 + n):P * (4 + n) + P]
                    vh, vl = [v[:, 4 * k + n, :, :].rearrange("p g c -> p (g c)") for v in (m.gvh, m.gvl)]
                    o = bo[:, 18 * n:18 * n + 18]
                    e.matmul(o, high, vh, start=n == 0, stop=False, skip_group_check=True)
                    e.matmul(o, high, vl, start=False, stop=False, skip_group_check=True)
                    last = e.matmul(o, low, vh, start=False, stop=n == 3, skip_group_check=True)
                last.then_inc(s_pv, 1)

            def turn_out(u, k, j):
                e.wait_ge(s_lat, u + 1)
                wait(e, s_lt, u)
                e.transpose(b2[:, 0:P], latf[k % 2], m.ident[:, :]).then_inc(s_t2, 1)

            def remote(u, k, j):
                e.wait_ge(s_lt, u + 1)
                wait(e, s_gr, u)
                e.matmul(br[:, 0:D], latT[k % 2], m.routp[:, :], start=True, stop=True).then_inc(s_rm, 1)

            def turn_mix(u, k, j):
                e.wait_ge(s_mix, u + 1)
                wait(e, s_mt, u)
                e.transpose(b3[:, 0:P], fin[k % 2], m.ident[:, :]).then_inc(s_t3, 1)

            def project(u, k, j):
                e.wait_ge(s_mt, u + 1)
                wait(e, s_x, u)
                e.matmul(bw[:, 0:D], finT[k % 2], m.wout[:, :], start=True, stop=True).then_inc(s_wo, 1)

            pipeline(e, [(0, q), (2, scores), (5, turn), (6, pv), (7, turn_out), (8, remote), (9, turn_mix), (10, project)],
                     NU, W, 2 * W)

        @block.vector
        def _(e):
            def top(u, k, j):
                e.wait_ge(s_sc, u + 1)
                wait(e, s_exp, u - 1)
                e.tensor_tensor(Sl[k % 2], bs[:, :].rearrange("p (h n) -> p h n", h=LH),
                                lmask[:, j, :].rearrange("p (o n) -> p o n", o=1).broadcast_to([P, LH, NL]),
                                ALU.add).then_inc(s_sm, 1)
                e.wait_ge(s_sm, u + 1)
                e.tensor_reduce(mxl[k % 2], Sl[k % 2], axis=AX.X, op=ALU.max).then_inc(s_mx, 1)

            def norm(u, k, j):
                e.wait_ge(s_pv, u + 1)
                wait(e, s_t2, u - 1)
                o = bo[:, 0:LH * 9].rearrange("p (h c) -> p h c", c=9)
                e.reciprocal(rec[k % 2], o[:, :, 8]).then_inc(s_rec, 1)
                e.wait_ge(s_rec, u + 1)
                e.tensor_tensor(lat[k % 2], o[:, :, 0:8],
                                rec[k % 2].rearrange("p (h o) -> p h o", o=1).broadcast_to([P, LH, 8]), ALU.mult).then_inc(s_lat, 1)

            def gate(u, k, j):
                e.wait_ge(s_rm, u + 1)
                wait(e, s_mix, u - 1)
                e.scalar_tensor_tensor(rem[k % 2].rearrange("p (s d) -> p s d", d=HD),
                                       m.glr[:, u, H:2 * H].rearrange("p (s o) -> p s o", o=1).broadcast_to([P, H, HD]), 1.0,
                                       br[:, 0:D].rearrange("p (s d) -> p s d", d=HD), ALU.add, ALU.mult).then_inc(s_gr, 1)

            def add(u, k, j):
                e.wait_ge(s_wo, u + 1)
                e.tensor_tensor(m.X[:, u, :], m.X[:, u, :], bw[:, 0:D], ALU.add).then_inc(s_x, 1)

            def stat(u, k, j):
                e.wait_ge(s_x, u + 1)
                e.bn_stats(m.stats[:, u, :], m.X[:, u, :]).then_inc(s_st, 1)

            def low_q(u, k, j):
                e.wait_ge(s_gqk, u + 1)
                q = gq[k % 2][LD:P]
                e.scalar_tensor_tensor(q, bq[LD:P, 0:P], ISQ, q, ALU.mult, ALU.subtract).then_inc(s_ql, 1)

            for v in latf:
                e.memset(v[:, LD:D], 0.0)
            e.wait_ge(s_lm, 2)
            pipeline(e, [(1, low_q), (11, stat), (10, add), (8, gate), (6, norm), (2, top)], NU, W, 2 * W, in_order=True)
            e.wait_ge(s_st, NU)

        @block.gpsimd
        def _(e):
            e.memset(lmask, 0.0).then_inc(s_lm, 1)
            e.wait_ge(s_lm, 1)
            e.affine_select(out=lmask, in_=lmask, compare_op=ALU.is_ge, fill=NEG, base=0,
                            pattern=[[P, NJ], [-CHUNK, NL]], channel_multiplier=1).then_inc(s_lm, 1)
            e.wait_ge(s_lm, 2)

            def sub(u, k, j):
                e.wait_ge(s_mx, u + 1)
                e.tensor_tensor(Sl[k % 2], Sl[k % 2], mxl[k % 2].rearrange("p (h o) -> p h o", o=1).broadcast_to([P, LH, NL]),
                                ALU.subtract).then_inc(s_sub, 1)

            def mixed(u, k, j):
                e.wait_ge(s_gr, u + 1)
                wait(e, s_t3, u - 1)
                e.tensor_tensor(fin[k % 2], m.mix[:, u, :], rem[k % 2], ALU.add).then_inc(s_mix, 1)

            def low(u, k, j):
                e.wait_ge(s_ph, u + 1)
                e.tensor_tensor(Ph[k % 2][:, LH * NL:2 * LH * NL], Pl[k % 2], Ph[k % 2][:, 0:LH * NL], ALU.subtract).then_inc(s_pl, 1)

            pipeline(e, [(8, mixed), (3, sub), (4, low)], NU, W, 2 * W, in_order=True)

        @block.scalar
        def _(e):
            def keep_q(u, k, j):
                e.wait_ge(s_gq, u + 1)
                wait(e, s_sc, u - 1)
                e.mul(gq[k % 2], bq[:, 0:P], ISQ).then_inc(s_gqk, 1)

            def exps(u, k, j):
                e.wait_ge(s_sub, u + 1)
                wait(e, s_pl, u - 1)
                e.activation(Pl[k % 2], Sl[k % 2].rearrange("p h n -> p (h n)"), ACT.Exp).then_inc(s_exp, 1)

            def high(u, k, j):
                e.wait_ge(s_exp, u + 1)
                wait(e, s_t, u - 1)
                e.copy(Ph[k % 2][:, 0:LH * NL], Pl[k % 2]).then_inc(s_ph, 1)

            def keep_pt(u, k, j):
                e.wait_ge(s_t, u + 1)
                wait(e, s_pv, u - 1)
                e.copy(PT[k % 2], bt.bitcast(F16)).then_inc(s_pt, 1)

            def keep_out(u, k, j):
                e.wait_ge(s_t2, u + 1)
                wait(e, s_rm, u - 1)
                e.copy(latT[k % 2], b2[:, 0:P]).then_inc(s_lt, 1)

            def keep_mix(u, k, j):
                e.wait_ge(s_t3, u + 1)
                wait(e, s_wo, u - 1)
                e.copy(finT[k % 2], b3[:, 0:P]).then_inc(s_mt, 1)

            pipeline(e, [(1, keep_q), (9, keep_mix), (7, keep_out), (3, exps), (5, keep_pt), (4, high)], NU, W, 2 * W, in_order=True)


def ffn(nc, ctx, m, a):
    def sem(name):
        return ctx.enter_context(nc.semaphore("ffn_" + name))
    s_mo, s_rs, s_n, s_q, s_t, s_qt, s_y, s_y1, s_y2, s_x, s_st = (
        sem(n) for n in ("moments", "rstd", "normed", "rounded", "turned", "turned_kept", "product", "scaled", "biased", "added", "stats"))
    c = Cut(m.work)
    w = B * D
    xb = c.take(w, BF16)
    t, sc = c.take(w), c.take(w)
    q = c.take(w)
    qb = [c.take(w, BF16) for _ in range(2)]
    qT = [c.take(w, BF16) for _ in range(2)]
    y1 = [c.take(w, BF16) for _ in range(2)]
    y2 = [c.take(w, BF16) for _ in range(2)]
    s_in, s_w3, s_z, s_hi, s_lo = (sem(n) for n in ("experts_loaded", "experts_down_loaded", "b3_zeros", "experts_high", "experts_low"))
    st = m.Wst.rearrange("p (e f) -> p e f", e=E)
    high, low = (m.W1h, m.W2h), (m.W1l, m.W2l)

    with nc.Block() as block:
        @block.vector
        def _(e):
            moments(e, s_mo, 0, m.stats[:, :, :], m.mv[:, :, 0], m.mv[:, :, 1])
            e.wait_ge(s_rs, 1)

            def rounded(i, k, j):
                for b in range(B):
                    u = B * i + b
                    last = e.tensor_scalar(xb[:, D * b:D * b + D], m.X[:, u, :], m.mv[:, u, 0:1], m.rstd[:, bass.ds(u, 1)],
                                           ALU.subtract, ALU.mult)
                n = [0]

                def step(ins):
                    ins.then_inc(s_n, 1)
                    n[0] += 1
                    e.wait_ge(s_n, FFN_STEPS * i + n[0])
                step(last)
                step(e.tensor_scalar(t, xb, m.fsc[:, 2:3], None, ALU.mult))
                wait(e, s_t, i - 1)
                round_e4m3fn(e, step, t, q, sc, qb[k]).then_inc(s_q, 1)
                e.wait_ge(s_q, i + 1)
                assert n[0] == FFN_STEPS

            def stat(i, k, j):
                e.wait_ge(s_x, i + 1)
                for b in range(B):
                    last = e.bn_stats(m.stats[:, B * i + b, :], m.X[:, B * i + b, :])
                last.then_inc(s_st, 1)

            pipeline(e, [(0, rounded), (2, stat)], NJ, 2, 2)
            e.wait_ge(s_st, NJ)
            moments(e, s_mo, MOMENTS, m.stats[:, :, :], m.mv[:, :, 0], m.mv[:, :, 1])

        @block.gpsimd
        def _(e):
            e.wait_ge(s_mo, MOMENTS)
            e.tensor_tensor(m.rstd[:, :], m.mv[:, :, 1], m.nhalf[:, :], ALU.pow).then_inc(s_rs, 1)

            e.memset(m.b3bd, 0.0).then_inc(s_z, 1)

            def lows(i, k, j):
                if isinstance(i, int) and i < 2:
                    e.wait_ge(s_hi, i + 1)
                    e.tensor_tensor(low[i], st, high[i], ALU.subtract).then_inc(s_lo, 1)

            def bias(i, k, j):
                e.wait_ge(s_y1, 2 * i + 2)
                wait(e, s_x, i - 1)
                e.tensor_tensor(y2[k].rearrange("p (b n) -> p b n", b=B), y1[k].rearrange("p (b n) -> p b n", b=B),
                                m.fbias[:, :].rearrange("p (o n) -> p o n", o=1).broadcast_to([P, B, D]), ALU.add).then_inc(s_y2, 1)
                e.wait_ge(s_y2, i + 1)
                x = m.X[:, bass.ds(B * i, B), :]
                e.tensor_tensor(x, x, y2[k].rearrange("p (b n) -> p b n", b=B), ALU.add).then_inc(s_x, 1)
            pipeline(e, [(0, lows), (1, bias)], NJ, 2, 2)
            e.wait_ge(s_mo, 2 * MOMENTS)
            e.tensor_tensor(m.rstd[:, :], m.mv[:, :, 1], m.nhalf[:, :], ALU.pow).then_inc(s_rs, 1)
            e.wait_ge(s_rs, 2)

        @block.tensor
        def _(e):
            def turn(i, k, j):
                e.wait_ge(s_q, i + 1)
                wait(e, s_qt, i - 1)
                for b in range(B):
                    last = e.transpose(m.ps[k][:, :].bitcast(BF16)[:, P * b:P * b + P], qb[k][:, D * b:D * b + D], m.identb[:, :])
                last.then_inc(s_t, 1)

            def product(i, k, j):
                e.wait_ge(s_qt, i + 1)
                for h in range(2):
                    wait(e, s_y1, 2 * (i - 2) + h + 1)
                    for b in range(HALF):
                        u = HALF * h + b
                        last = e.matmul(m.ps[2 + 2 * k + h][:, D * b:D * b + D], qT[k][:, P * u:P * u + P], m.fkq[:, :], start=True, stop=True)
                    last.then_inc(s_y, 1)
            pipeline(e, [(0, turn), (1, product)], NJ, 2, 4)

        @block.scalar
        def _(e):
            def keep(i, k, j):
                e.wait_ge(s_t, i + 1)
                wait(e, s_y, 2 * (i - 1))
                e.copy(qT[k], m.ps[k][:, :].bitcast(BF16)).then_inc(s_qt, 1)

            def scale(i, k, j):
                wait(e, s_y2, i - 1)
                for h in range(2):
                    e.wait_ge(s_y, 2 * i + h + 1)
                    e.activation(y1[k][:, 512 * h:512 * h + 512], m.ps[2 + 2 * k + h][:, :], ACT.Copy, scale=m.fsc[:, 4:5]).then_inc(s_y1, 1)
            def highs(i, k, j):
                if isinstance(i, int) and i < 2:
                    e.wait_ge(s_in, 16 * i + 16)
                    e.copy(high[i], st).then_inc(s_hi, 1)

            pipeline(e, [(0, keep), (0, highs), (1, scale)], NJ, 2, 2)

        @block.sync
        def _(sp):
            sp.dma_start(st, a.W1.rearrange("e d f -> d e f")).then_inc(s_in, 16)
            for n in range(NC4):
                sp.dma_start(m.W3s[:, :, D * n:D * n + D], a.W3[:, P * n:P * n + P, :].rearrange("e p n -> p e n")).then_inc(s_w3, 16)
            sp.wait_ge(s_z, 1)
            for b in range(B):
                sp.dma_start(m.b3bd[E * b:E * (b + 1), D * b:D * (b + 1)], a.b3).then_inc(s_w3, 16)
            sp.wait_ge(s_lo, 1)
            sp.dma_start(st, a.W2.rearrange("e d f -> d e f")).then_inc(s_in, 16)
            sp.wait_ge(s_w3, 16 * (NC4 + B))


FFN_STEPS = 9


def scan_and_experts(nc, ctx, m, a):
    def sem(name):
        return ctx.enter_context(nc.semaphore("x_" + name))
    s_n3, s_t3, s_x3, s_pi, s_in, s_pg, s_g, s_gl, s_c = (
        sem(n) for n in ("normed", "turned", "xT", "in_proj", "inp", "gate_proj", "gate_tanh", "gate_links", "carry"))
    s_gc, s_k2, s_cb, s_u = (sem(n) for n in ("gate_moved", "carry_links", "carry_moved", "drive"))
    s_ch, s_th, s_r = (sem(n) for n in ("step_product", "step_tanh", "step_state"))
    s_a, s_sa, s_b, s_h, s_w3, s_ys, s_yd = (
        sem(n) for n in ("up_a", "silu", "up_b", "hidden", "down", "weighed", "summed"))
    s_bo, s_S, s_po, s_xo, s_mo, s_rs, s_n4, s_t4, s_x4f, s_x4, s_pr, s_d, s_w, s_k, s_cw, s_tc, s_ct, s_pb, s_xb = (
        sem(n) for n in ("out_biased", "states", "out_proj", "residual", "moments4", "rstd4", "normed4", "turned4", "xT4", "parts4",
                         "logits", "gap", "gap_tanh", "chain", "shares", "shares_turned", "shares_kept", "bias_sum", "biased"))
    s_out, s_z, s_tk = sem("written"), sem("zeroed"), sem("tick_zeroed")

    c = Cut(m.work)
    w = B * P
    n4 = c.take(w).rearrange("p (b d) -> p b d", b=B)
    Sx = c.take(w).rearrange("p (b t) -> p b t", b=B)
    g = c.take(w)
    gv = g.rearrange("p (b t) -> p b t", b=B)
    inpN, gN, CN = [m.Wst[:, n * w:(n + 1) * w] for n in range(3)]
    n3 = c.take(N5).rearrange("p (b d) -> p b d", b=HALF)
    x3 = c.take(N5)
    tmp = c.take(N5)
    Cb = c.take(B * (P + 1)).rearrange("p (b t) -> p b t", b=B)
    R = c.take(B * (P + 1)).rearrange("p (b t) -> p b t", b=B)
    x4f = c.take(w)
    x4h, x4l = c.take(w, F16), c.take(w, F16)
    sa = [c.take(N5) for _ in range(2)]
    hb = [c.take(N5) for _ in range(2)]
    gT = c.take(N5)
    yw = c.take(N5)
    th = [c.take(B) for _ in range(2)]
    lg = c.take(B * E).rearrange("p (b e) -> p b e", b=B)
    mx8 = c.take(B * E).rearrange("p (b e) -> p b e", b=B)
    ix = c.take(B * E).bitcast(U32).rearrange("p (b e) -> p b e", b=B)
    ixf = c.take(B * 2).rearrange("p (b e) -> p b e", b=B)
    ws = c.take(B * 2).rearrange("p (b e) -> p b e", b=B)
    eq = [c.take(B * E).rearrange("p (b e) -> p b e", b=B) for _ in range(2)]
    cwp = c.take(P)
    cw = cwp[:, 0:B * E].rearrange("p (b e) -> p b e", b=B)
    cwT = c.take(P)[0:B * E]
    U = m.psum[:, 0:1024]
    bU, bA, bB, bY, bZ = m.ps[0:2], m.ps[2:4], m.ps[4:6], m.ps[6], m.ps[7]
    AT, BT, WinT, WgT, WoT = (m.w5T[:, n, :] for n in range(5))

    def rounds(e, round_):
        round_(0, True, False, True)
        with e.Fori(1, NJ - 1) as j:
            round_(j, True, True, True)
        round_(NJ - 1, True, True, False)
        round_(NJ, False, True, False)

    def halves(e, j, body, flush, ahead):
        def turn(h, x, fresh, part):
            body(16 * (j - 1) + 8 * h + x, FIRST + STEPS * (8 * h + x), h, x, fresh, part)

        with e.Fori(0, 2) as h:
            written = PARTS if ahead else 1
            for x in range(written):
                turn(h, x, x == 0, x if ahead else None)
            with e.Fori(written, E) as x:
                turn(h, x, False, None)
            flush(16 * (j - 1) + 8 * h + 7, h)

    def two_back(g, ch, fresh):
        return 4 * g if fresh and ch == 0 else 4 * g + ch - 1

    with nc.Block() as block:
        @block.tensor
        def _(e):
            def turned(q, h):
                e.wait_ge(s_n3, q + 1)
                wait(e, s_g, q)
                for b in range(HALF):
                    last = e.transpose(bZ[:, P * b:P * b + P], n3[:, b, :], m.ident[:, :])
                last.then_inc(s_t3, 1)

            def in_proj(q, h):
                e.wait_ge(s_x3, q + 1)
                e.matmul(bZ, WinT, x3, start=True, stop=True).then_inc(s_pi, 1)

            def gate_proj(q, h):
                e.wait_ge(s_in, q + 1)
                e.matmul(bZ, WgT, inpN[:, bass.ds(N5 * h, N5)], start=True, stop=True).then_inc(s_pg, 1)

            parts = {1: turned, 2: in_proj, 3: gate_proj}

            def step(j, t):
                wait(e, s_r, P * j + t)
                if isinstance(t, int) and t == 0:
                    e.wait_ge(s_u, j + 1)
                e.matmul(U[:, bass.ds(B * t, B)], AT, R[:, :, bass.ds(t, 1)].rearrange("p b o -> p (b o)"),
                         start=False, stop=True, skip_group_check=True).then_inc(s_ch, 1)

            def start(j, scan, post):
                if scan:
                    wait(e, s_th, P * j)
                    e.wait_ge(s_in, 2 * j + 2)
                    for h in range(2):
                        e.matmul(bU[h], BT, inpN.rearrange("p (b t) -> p t b", b=B)[:, 64 * h:64 * h + 64, :], start=True, stop=True)
                if post:
                    wait(e, s_h, 64 * (j - 1))
                    wait(e, s_sa, 64 * (j - 1))
                    e.wait_ge(s_S, j)
                    for h in range(2):
                        for b in range(HALF):
                            last = e.matmul(bA[h][:, D * b:D * b + D], Sx[:, HALF * h + b, :], WoT, start=True, stop=True)
                        last.then_inc(s_po, 1)
                if scan:
                    e.wait_ge(s_cb, j + 1)
                    for h in range(2):
                        last = e.matmul(bU[h], AT, Cb[:, :, 0:P].rearrange("p b t -> p t b")[:, 64 * h:64 * h + 64, :], start=False, stop=True, skip_group_check=True)
                    last.then_inc(s_u, 1)

            def turn4(j, h):
                e.wait_ge(s_n4, 2 * (j - 1) + h + 1)
                for b in range(HALF):
                    last = e.transpose(bB[h][:, P * b:P * b + P], n4[:, HALF * h + b, :], m.ident[:, :])
                last.then_inc(s_t4, 1)

            def logits(j):
                e.wait_ge(s_x4f, 2 * j)
                wait(e, s_g, 2 * j + 2) if not isinstance(j, int) or j < NJ - 1 else e.wait_ge(s_g, 2 * NJ)
                for b in range(B):
                    last = e.matmul(bZ[:, E * b:E * b + E], x4f[:, P * b:P * b + P], m.wr[:, :], start=True, stop=True)
                last.then_inc(s_pr, 1)

            def turn_shares(j):
                e.wait_ge(s_cw, j)
                wait(e, s_ys, 16 * (j - 1))
                e.transpose(bY[:, 0:P], cwp, m.ident[:, :]).then_inc(s_tc, 1)

            def bias_sum(j):
                e.wait_ge(s_ct, j)
                e.matmul(bY, cwT, m.b3bd[:, 0:N5], start=True, stop=True)
                e.matmul(bZ, cwT, m.b3bd[:, N5:2 * N5], start=True, stop=True).then_inc(s_pb, 1)

            def down(g, x, ch, new):
                e.wait_ge(s_h, 4 * g + ch + 1)
                if ch == 0:
                    if new is not None:
                        e.wait_ge(s_xb, new)
                    wait(e, s_ys, g)
                for b in range(HALF):
                    last = e.matmul(bY[:, D * b:D * b + D], hb[ch % 2][:, P * b:P * b + P],
                                    m.W3s[:, x, D * ch:D * ch + D],
                                    start=(ch == 0 and b == 0), stop=(ch == NC4 - 1), skip_group_check=True)
                last.then_inc(s_w3, 1)

            def round_(j, scan, moe, ahead):
                start(j, scan, moe)
                beside = {POST_TURN: lambda: turn4(j, 0), POST_TURN + 1: lambda: turn4(j, 1), POST_LOGITS: lambda: logits(j),
                          POST_SHARES: lambda: turn_shares(j), FIRST - 1: lambda: bias_sum(j)}
                for t in range(FIRST):
                    if scan:
                        step(j, t)
                    if moe and t in beside:
                        beside[t]()

                def body(g, t, h, x, fresh, part):
                    for s in range(8):
                        if scan and s < STEPS:
                            step(j, t + s)
                        ch = s // 2
                        if part in parts and s == 5:
                            parts[part](2 * (j + 1) + h, h)
                        if not moe:
                            continue
                        f = slice(P * ch, P * ch + P)
                        xh, xl = x4h[:, bass.ds(N5 * h, N5)], x4l[:, bass.ds(N5 * h, N5)]
                        if s % 2 == 0:
                            if fresh and s == 0:
                                e.wait_ge(s_x4, j)
                                e.wait_ge(s_xo, 2 * j)
                            wait(e, s_sa, two_back(g, ch, fresh))
                            e.matmul(bA[ch % 2], m.W1h[:, x, f], xh, start=True, stop=False)
                            e.matmul(bA[ch % 2], m.W1h[:, x, f], xl, start=False, stop=False)
                            e.matmul(bA[ch % 2], m.W1l[:, x, f], xh, start=False, stop=True).then_inc(s_a, 1)
                            wait(e, s_h, two_back(g, ch, fresh))
                            e.matmul(bB[ch % 2], m.W2h[:, x, f], xh, start=True, stop=False)
                            e.matmul(bB[ch % 2], m.W2h[:, x, f], xl, start=False, stop=False)
                        else:
                            e.matmul(bB[ch % 2], m.W2l[:, x, f], xh, start=False, stop=True).then_inc(s_b, 1)
                            if ch > 0:
                                down(g, x, ch - 1, j if fresh else None)
                            elif not fresh:
                                down(g - 1, x - 1, NC4 - 1, None)

                def flush(g, h):
                    if moe:
                        down(g, E - 1, NC4 - 1, None)

                halves(e, j, body, flush, ahead)

            for h in range(2):
                for part in (1, 2, 3):
                    parts[part](h, h)
            rounds(e, round_)

        @block.scalar
        def _(e):
            e.preload_act_table_set("silu_and_others")

            def keep_x(q, h):
                e.wait_ge(s_t3, q + 1)
                wait(e, s_pi, q)
                e.copy(x3, bZ).then_inc(s_x3, 1)

            def keep_inp(q, h):
                e.wait_ge(s_pi, q + 1)
                e.activation(inpN[:, bass.ds(N5 * h, N5)], bZ, ACT.Identity, bias=m.bcol[:, 0:1]).then_inc(s_in, 1)

            def keep_gate(q, h):
                e.wait_ge(s_pg, q + 1)
                wait(e, s_c, q)
                e.activation(gT, bZ, ACT.Tanh, bias=m.bcol[:, 2:3], scale=0.5).then_inc(s_g, 1)

            parts = {1: keep_x, 2: keep_inp, 3: keep_gate}

            def step(j, t, k):
                e.wait_ge(s_ch, P * j + t + 1)
                e.activation(th[k], U[:, bass.ds(B * t, B)], ACT.Tanh).then_inc(s_th, 1)

            def keep4(j, h):
                e.wait_ge(s_t4, 2 * (j - 1) + h + 1)
                wait(e, s_pr, j - 1)
                e.copy(x4f[:, N5 * h:N5 * h + N5], bB[h]).then_inc(s_x4f, 1)

            def gap(j):
                e.wait_ge(s_d, j)
                e.activation(ws[:, :, 0], ws[:, :, 1], ACT.Tanh, scale=0.5).then_inc(s_w, 1)

            def keep_shares(j):
                e.wait_ge(s_tc, j)
                e.copy(cwT, bY[0:B * E, 0:P]).then_inc(s_ct, 1)

            def round_(j, scan, moe, ahead):
                if scan:
                    e.wait_ge(s_c, 2 * j + 2)
                    wait(e, s_r, P * j)
                    e.copy(g, gN).then_inc(s_gc, 1)
                beside = {POST_TURN + 1: lambda: keep4(j, 0), POST_TURN + 2: lambda: keep4(j, 1), POST_GAP: lambda: gap(j),
                          POST_SHARES + 1: lambda: keep_shares(j)}
                for t in range(FIRST):
                    if scan:
                        step(j, t, t % 2)
                    if moe and t in beside:
                        beside[t]()

                def body(g_, t, h, x, fresh, part):
                    for s in range(8):
                        if scan and s < STEPS:
                            step(j, t + s, s % 2)
                        if moe and s % 2 == 0:
                            ch = s // 2
                            e.wait_ge(s_a, 4 * g_ + ch + 1)
                            wait(e, s_h, two_back(g_, ch, fresh))
                            e.activation(sa[ch % 2], bA[ch % 2], ACT.Silu, bias=m.b12[:, 0, ch, bass.ds(x, 1)]).then_inc(s_sa, 1)
                        if part in parts and s == 7:
                            parts[part](2 * (j + 1) + h, h)

                halves(e, j, body, lambda g_, h: None, ahead)

            for h in range(2):
                for part in (1, 2, 3):
                    parts[part](h, h)
            rounds(e, round_)

        @block.gpsimd
        def _(e):
            e.memset(R[:, :, 0:1], 0.0).then_inc(s_z, 1)
            e.memset(Cb[:, :, 0:1], 0.0).then_inc(s_z, 1)
            e.memset(cwp, 0.0).then_inc(s_z, 1)
            tick = m.tick[:, 5:8]
            e.memset(tick, 0.0).then_inc(s_z, 1)
            e.wait_ge(s_z, 4)

            def bear(k):
                e.tensor_tensor(tick[:, k:k + 1], tick[:, 0:1], tick[:, 0:1], ALU.add)

            def gates(q, h):
                half = bass.ds(N5 * h, N5)
                e.wait_ge(s_g, q + 1)
                bear(1)
                e.tensor_scalar(gT, gT, 0.5, 0.5, ALU.mult, ALU.add).then_inc(s_gl, 1)
                e.wait_ge(s_gl, 3 * q + 1)
                e.tensor_copy(gN[:, half], gT).then_inc(s_gl, 1)
                e.wait_ge(s_gl, 3 * q + 2)
                e.tensor_tensor(tmp, gT, inpN[:, half], ALU.mult).then_inc(s_gl, 1)
                e.wait_ge(s_gl, 3 * q + 3)
                bear(1)
                e.tensor_tensor(CN[:, half], inpN[:, half], tmp, ALU.subtract).then_inc(s_c, 1)

            def round_(j, scan, moe, ahead):
                if moe:
                    e.wait_ge(s_mo, MOMENTS * j)
                    e.tensor_tensor(m.rstd4, m.mv4[:, :, 1], m.nhalf[:, 0:B], ALU.pow).then_inc(s_rs, 1)
                if scan:
                    e.wait_ge(s_n3, 2 * j + 2)
                    u8 = m.X[:, bass.ds(B * j, B), :]
                    e.tensor_tensor(u8, u8, m.bout[:, :].rearrange("p (o n) -> p o n", o=1).broadcast_to([P, B, D]), ALU.add).then_inc(s_bo, 1)

                def summed(g_, h, x):
                    e.wait_ge(s_ys, g_ + 1)
                    e.wait_ge(s_xb, j)
                    e.wait_ge(s_yd, g_) if not isinstance(g_, int) or g_ > 0 else None
                    bear(2)
                    xh = m.X[:, bass.ds(B * (j - 1) + HALF * h, HALF), :]
                    e.tensor_tensor(xh, xh, yw.rearrange("p (b n) -> p b n", b=HALF), ALU.add).then_inc(s_yd, 1)

                def body(g_, t, h, x, fresh, part):
                    if moe and not fresh:
                        summed(g_ - 1, h, x - 1)
                    if part == 4:
                        gates(2 * (j + 1) + h, h)

                halves(e, j, body, (lambda g_, h: summed(g_, h, E - 1)) if moe else (lambda g_, h: None), ahead)

            for h in range(2):
                gates(h, h)
            rounds(e, round_)

        @block.vector
        def _(e):
            e.wait_ge(s_z, 4)
            e.memset(m.tick[:, 0:5], 0.0).then_inc(s_tk, 1)
            e.wait_ge(s_tk, 1)

            def tick(k=1):
                e.tensor_copy(m.tick[:, k:k + 1], m.tick[:, 0:1])

            def normed(j, q, h, b):
                u = B * j + HALF * h + b
                if b == 0:
                    wait(e, s_t3, q)
                last = e.tensor_scalar(n3[:, b, :], m.X[:, u, :], m.mv[:, u, 0:1], m.rstd[:, bass.ds(u, 1)], ALU.subtract, ALU.mult)
                if b == HALF - 1:
                    last.then_inc(s_n3, 1)

            def step(j, t, k):
                e.wait_ge(s_th, P * j + t + 1)
                if isinstance(t, int) and t == 0:
                    e.wait_ge(s_gc, j + 1)
                e.tensor_tensor(R[:, :, bass.ds(t + 1, 1)].rearrange("p b o -> p (b o)"), th[k],
                                gv[:, :, bass.ds(t, 1)].rearrange("p b o -> p (b o)"), ALU.mult).then_inc(s_r, 1)

            def start(j, scan, post):
                if post:
                    e.wait_ge(s_r, P * j)
                    wait(e, s_po, 2 * (j - 1))
                    wait(e, s_cb, j)
                    e.tensor_tensor(Sx, R[:, :, 1:P + 1], Cb[:, :, 1:P + 1], ALU.add).then_inc(s_S, 1)
                if scan:
                    if post:
                        e.tensor_copy(Cb[:, :, 0:1], Cb[:, :, P:P + 1])
                        e.tensor_copy(R[:, :, 0:1], R[:, :, P:P + 1]).then_inc(s_k2, 1)
                        e.wait_ge(s_k2, j)
                        e.wait_ge(s_S, j)
                    e.wait_ge(s_c, 2 * j + 2)
                    e.tensor_copy(Cb[:, :, 1:P + 1], CN.rearrange("p (b t) -> p b t", b=B)).then_inc(s_cb, 1)
                if post:
                    e.wait_ge(s_bo, j)
                    for h in range(2):
                        e.wait_ge(s_po, 2 * (j - 1) + h + 1)
                        xh = m.X[:, bass.ds(B * (j - 1) + HALF * h, HALF), :]
                        e.tensor_tensor(xh, xh, bA[h].rearrange("p (b n) -> p b n", b=HALF), ALU.add).then_inc(s_xo, 1)

            def ending(j):
                n = [0]
                iota = m.iota8[:, :].rearrange("p (o n) -> p o n", o=1).broadcast_to([P, B, E])

                def link(ins):
                    ins.then_inc(s_k, 1)
                    n[0] += 1
                    e.wait_ge(s_k, KP * (j - 1) + n[0])

                def stat(h):
                    e.wait_ge(s_xo, 2 * (j - 1) + h + 1)
                    tick(2 + h)
                    for b in range(HALF * h, HALF * h + HALF):
                        last = e.bn_stats(m.st4[:, b, :], m.X[:, B * (j - 1) + b, :])
                    if h:
                        link(last)

                def norm4(h):
                    if h == 0:
                        e.wait_ge(s_rs, j)
                    for b in range(HALF * h, HALF * h + HALF):
                        last = e.tensor_scalar(n4[:, b, :], m.X[:, B * (j - 1) + b, :], m.mv4[:, b, 0:1], m.rstd4[:, b:b + 1], ALU.subtract, ALU.mult)
                    last.then_inc(s_n4, 1)

                def split_high():
                    e.wait_ge(s_x4f, 2 * j)
                    link(e.tensor_copy(x4h, x4f))

                def split_low():
                    e.tensor_tensor(x4l, x4f, x4h, ALU.subtract).then_inc(s_x4, 1)

                def best():
                    e.wait_ge(s_pr, j)
                    link(e.tensor_tensor(lg, bZ[:, 0:B * E].rearrange("p (b e) -> p b e", b=B),
                                         m.br[:, :].rearrange("p (o n) -> p o n", o=1).broadcast_to([P, B, E]), ALU.add))
                    tick()
                    for b in range(B):
                        last = e.max(mx8[:, b, :], lg[:, b, :])
                    link(last)

                def which():
                    e.tensor_tensor(ws[:, :, 1], mx8[:, :, 0], mx8[:, :, 1], ALU.subtract).then_inc(s_d, 1)
                    for b in range(B):
                        last = e.max_index(ix[:, b, :], mx8[:, b, :], lg[:, b, :])
                    link(last)

                def match():
                    link(e.tensor_copy(ixf, ix[:, :, 0:2]))
                    for k in range(2):
                        last = e.tensor_tensor(eq[k], iota, ixf[:, :, k:k + 1].broadcast_to([P, B, E]), ALU.is_equal)
                    link(last)

                def shares():
                    e.wait_ge(s_w, j)
                    link(e.tensor_scalar(ws[:, :, 1], ws[:, :, 0], -0.5, 0.5, ALU.mult, ALU.add))
                    link(e.tensor_scalar(ws[:, :, 0], ws[:, :, 0], 0.5, 0.5, ALU.mult, ALU.add))
                    for k in range(2):
                        last = e.tensor_tensor(eq[k], eq[k], ws[:, :, k:k + 1].broadcast_to([P, B, E]), ALU.mult)
                    link(last)
                    wait(e, s_tc, j - 1)
                    e.tensor_tensor(cw, eq[0], eq[1], ALU.add).then_inc(s_cw, 1)
                    assert n[0] == KP, n[0]

                return {0: lambda: stat(0), 1: lambda: stat(1),
                        2: lambda: moments(e, s_mo, MOMENTS * (j - 1), m.st4[:, :, :], m.mv4[:, :, 0], m.mv4[:, :, 1]),
                        3: lambda: norm4(0), 4: lambda: norm4(1), POST_TURN + 3: split_high, POST_LOGITS: split_low,
                        POST_LOGITS + 1: best, POST_GAP - 1: which, POST_GAP: match, POST_GAP + 1: shares}

            def round_(j, scan, moe, ahead):
                start(j, scan, moe)
                beside = ending(j) if moe else {}
                for t in range(FIRST):
                    if scan:
                        step(j, t, t % 2)
                    if t in beside:
                        beside[t]()
                if moe:
                    e.wait_ge(s_pb, j)
                    for h in range(2):
                        xh = m.X[:, bass.ds(B * (j - 1) + HALF * h, HALF), :]
                        last = e.tensor_tensor(xh, xh, (bY, bZ)[h].rearrange("p (b n) -> p b n", b=HALF), ALU.add)
                    last.then_inc(s_xb, 1)
                    e.wait_ge(s_cw, j)
                    tick(4)

                def weighed(g_, h, x):
                    e.wait_ge(s_w3, 4 * g_ + 4)
                    wait(e, s_yd, g_)
                    share = cw[:, bass.ds(HALF * h, HALF), bass.ds(x, 1)].broadcast_to([P, HALF, D])
                    e.tensor_tensor(yw.rearrange("p (b n) -> p b n", b=HALF), bY.rearrange("p (b n) -> p b n", b=HALF), share,
                                    ALU.mult).then_inc(s_ys, 1)

                def body(g_, t, h, x, fresh, part):
                    for s in range(8):
                        if scan and s < STEPS:
                            step(j, t + s, s % 2)
                        if part == 0 and s % 2 == 0:
                            normed(j + 1, 2 * (j + 1) + h, h, s // 2)
                        if moe and s % 2 == 1:
                            ch = s // 2
                            e.wait_ge(s_b, 4 * g_ + ch + 1)
                            e.wait_ge(s_sa, 4 * g_ + ch + 1)
                            wait(e, s_w3, two_back(g_, ch, fresh))
                            e.scalar_tensor_tensor(hb[ch % 2], bB[ch % 2], m.b12[:, 1, ch, bass.ds(x, 1)], sa[ch % 2],
                                                   ALU.add, ALU.mult).then_inc(s_h, 1)
                        if moe and s == 2 and not fresh:
                            weighed(g_ - 1, h, x - 1)

                halves(e, j, body, (lambda g_, h: weighed(g_, h, E - 1)) if moe else (lambda g_, h: None), ahead)

            for h in range(2):
                for b in range(HALF):
                    normed(0, h, h, b)
            rounds(e, round_)

        @block.sync
        def _(e):
            with e.Fori(0, NJ) as j:
                e.wait_ge(s_yd, 16 * (j + 1))
                e.dma_start(m.out[:, bass.ds(P * j, P), :].rearrange("b p f -> p b f"), m.X[:, bass.ds(B * j, B), :]).then_inc(s_out, 16)
            e.wait_ge(s_out, 16 * NJ)


STAGES = (setup, norm_all, local_attention, latent_attention, ffn, scan_and_experts)


def mixer_moe(nc, arrays, out, stages=STAGES, dump=None):
    with ExitStack() as ctx:
        m = lay_out(nc, ctx)
        m.out = out
        a = Arrays(arrays)
        for stage in stages:
            stage(nc, ctx, m, a)
        if dump:
            dump(nc, ctx, m)


_INS = {"x": "L0_attn_x", "wq": "L0_attn_wq", "wk": "L0_attn_wk", "wv": "L0_attn_wv", "wgq": "L0_attn_wgq",
        "wgk": "L0_attn_wgk", "wgv": "L0_attn_wgv", "r_out_w": "L0_attn_r_out_w",
        "gate_local_w": "L0_attn_gate_local_w", "gate_remote_w": "L0_attn_gate_remote_w", "w_out": "L0_attn_w_out",
        "f_kernel": "L0_ffn_kernel", "f_sin": "L0_ffn_input_scale", "f_sk": "L0_ffn_kernel_scale",
        "f_bias": "L0_ffn_bias", "A": "L1_attn_A", "B": "L1_attn_B", "W_in": "L1_attn_W_in", "b_in": "L1_attn_b_in",
        "W_gate": "L1_attn_W_gate", "b_gate": "L1_attn_b_gate", "W_out": "L1_attn_W_out", "b_out": "L1_attn_b_out",
        "Wr": "L1_ffn_Wr", "br": "L1_ffn_br", "W1": "L1_ffn_W1", "b1": "L1_ffn_b1", "W2": "L1_ffn_W2",
        "b2": "L1_ffn_b2", "W3": "L1_ffn_W3", "b3": "L1_ffn_b3"}


def kernel(**inputs):
    import numpy as _np
    import concourse.bacc as _bacc
    from concourse import mybir as _mybir
    from concourse.bass_utils import run_bass_kernel_spmd as _run

    nc = _bacc.Bacc("TRN2", target_bir_lowering=False, num_devices=1)
    arrays, aps = {}, []
    for short, name in _INS.items():
        v = _np.ascontiguousarray(inputs[name])
        arrays[f"in_{short}"] = v
        aps.append(nc.dram_tensor(f"in_{short}", v.shape, _mybir.dt.from_np(v.dtype), kind="ExternalInput").ap())
    out = nc.dram_tensor("out_0", (B, S, D), _mybir.dt.float32, kind="ExternalOutput").ap()
    mixer_moe(nc, aps, out)
    r = _run(nc, [arrays], core_ids=[0])
    return r.results[0]["out_0"]
```

```python
from contextlib import ExitStack

import concourse.bass as bass
from concourse import mybir

F32 = mybir.dt.float32
BF16 = mybir.dt.bfloat16
F16 = mybir.dt.float16
U32 = mybir.dt.uint32
ALU = mybir.AluOpType
ACT = mybir.ActivationFunctionType
AX = mybir.AxisListType

P = 128
B, S, D = 8, 1024, 128
NJ = S // P
NU = NJ * B
H, HD = 16, 8
HG, HH = 4, 4
E, DFF = 8, 512
WIN = 32
NB = P // WIN
KW = 2 * WIN
XW = P + WIN
LH, LD, NL = 8, 64, 64
CHUNK = S // NL
NC4 = DFF // P
EPS = 1e-5
NEG = -1.0e30
ISQ = float(1.0 / (8.0 ** 0.5))
STEPS = 8
HALF = 4
N5 = HALF * P
TURNS = 2 * E
DEEP = 2
LATE = 3
KP = 9


WORK = 14592


class Cut:

    def __init__(self, area):
        self.area, self.at = area, 0

    def take(self, n, dt=F32):
        words = n if dt == F32 else (n + 1) // 2
        words += words % 2
        v = self.area[:, self.at:self.at + words]
        self.at += words
        assert self.at <= WORK, self.at
        return v if dt == F32 else v.bitcast(dt)


class Memory:
    pass


class Arrays:

    def __init__(self, aps):
        (self.x, self.wq, self.wk, self.wv, self.wgq, self.wgk, self.wgv, self.r_out_w, self.gate_local_w,
         self.gate_remote_w, self.w_out, self.f_kernel, self.f_sin, self.f_sk, self.f_bias, self.A, self.B,
         self.W_in, self.b_in, self.W_gate, self.b_gate, self.W_out, self.b_out, self.Wr, self.br, self.W1, self.b1,
         self.W2, self.b2, self.W3, self.b3) = aps


def lay_out(nc, ctx):
    def sb(name, shape, dt=F32):
        return ctx.enter_context(nc.sbuf_tensor(name, shape, dt))

    m = Memory()
    m.X = sb("X", [P, NU, D])
    m.xnT = sb("xnT", [P, NU + B, XW])
    m.mix = sb("mix", [P, NU, D])
    m.work = sb("work", [P, WORK])
    wflat = m.xnT[:, :, :].rearrange("p u x -> p (u x)").bitcast(F16)
    ef = E * DFF
    m.W1h, m.W1l, m.W2h, m.W2l = [wflat[:, n * ef:(n + 1) * ef].rearrange("p (e f) -> p e f", e=E) for n in range(4)]
    mflat = m.mix[:, :, :].rearrange("p u x -> p (u x)")
    m.Wst = mflat[:, 0:ef]
    m.W3st = mflat[:, ef:2 * ef]
    m.W3h, m.W3l = [m.Wst.bitcast(F16)[:, n * ef:(n + 1) * ef].rearrange("p (e n) -> p e n", e=E) for n in range(2)]
    m.stats = sb("stats", [P, NU, 6])
    m.mv = sb("mv", [P, NU, 2])
    m.rstd = sb("rstd", [P, NU])
    m.nhalf = sb("nhalf", [P, NU])
    m.ident = sb("ident", [P, P])
    m.identb = sb("identb", [P, P], BF16)
    m.identh = sb("identh", [P, P], F16)
    m.hm = sb("hm", [P, HH])
    m.par = sb("par", [P, 2])
    m.lhm = sb("lhm", [P, LH])
    m.m16 = sb("m16", [P, H])
    m.cmask = sb("cmask", [P, 2, NB, KW])
    m.wq = sb("wq", [P, D])
    m.wk = sb("wk", [P, D])
    m.wv = sb("wv", [P, D])
    m.wgq = sb("wgq", [P, 2 * LD])
    m.wgk = sb("wgk", [P, 2 * LD])
    m.wgv = sb("wgv", [P, LD])
    m.wout = sb("wout", [P, D])
    m.wr = sb("wr", [P, E])
    m.gbd = sb("gbd", [P, 2 * H])
    m.wg = sb("wg", [P, 2 * H])
    m.gcol = sb("gcol", [P, 2])
    m.bcol = sb("bcol", [P, 3])
    m.bout = sb("bout", [P, D])
    m.fsc = sb("fsc", [P, 5])
    m.br = sb("br", [P, E])
    m.iota8 = sb("iota8", [P, E])
    m.routp = sb("routp", [P, D])
    m.w5T = sb("w5T", [P, 6, D])
    m.fk = sb("fk", [P, D], BF16)
    m.fkq = sb("fkq", [P, D], BF16)
    m.fbias = sb("fbias", [P, D], BF16)
    m.b12 = sb("b12", [P, 2, NC4, E])
    m.st4 = sb("st4", [P, B, 6])
    m.mv4 = sb("mv4", [P, B, 2])
    m.tick = sb("tick", [P, 12])
    m.rstd4 = sb("rstd4", [P, B])[:, :]
    gk = sb("gk", [P, 2 * B * LH * NL], F16)
    m.gkh, m.gkl = [gk[:, n * B * LH * NL:(n + 1) * B * LH * NL].rearrange("p (b n) -> p b n", b=B) for n in range(2)]
    m.b3bd = gk[0:B * E, 0:2 * B * D].bitcast(F32)
    m.gvx = m.work[:, WORK - B * NC4 * 18:].rearrange("p (k g c) -> p k g c", g=2, c=9)
    m.gvh, m.gvl = [sb(n, [P, B * NC4, 2, 9], F16) for n in ("gvh", "gvl")]
    m.glr = sb("glr", [P, NU, 2 * H])
    m.psum = ctx.enter_context(nc.psum_tensor("psum", [P, 8 * 512], F32))
    m.ps = [m.psum[:, 512 * n:512 * (n + 1)] for n in range(8)]
    return m


def setup(nc, ctx, m, a):
    s_w = ctx.enter_context(nc.semaphore("s_w"))
    s_const = ctx.enter_context(nc.semaphore("s_const"))
    s_dve = ctx.enter_context(nc.semaphore("s_setup_dve"))
    s_pe = ctx.enter_context(nc.semaphore("s_setup_pe"))
    m.s_x = [ctx.enter_context(nc.semaphore(f"s_x{j}")) for j in range(NJ)]
    loads = []
    c = Cut(m.work)
    m.raw5 = c.take(5 * D).rearrange("p (n d) -> p n d", n=5)
    m.b12r = c.take(2 * DFF)[0:E].rearrange("p (n d) -> p n d", n=2)
    m.rout = c.take(D)[0:LD]

    def ld(dst, src):
        loads.append((dst, src))

    def rowb(v):
        return v.rearrange("(o n) -> o n", o=1).broadcast_to([P, v.shape[0]])

    for dst, src in ((m.wq, a.wq), (m.wk, a.wk), (m.wv, a.wv), (m.wgq[:, 0:LD], a.wgq), (m.wgq[:, LD:2 * LD], a.wgq),
                     (m.wgk[:, 0:LD], a.wgk), (m.wgk[:, LD:2 * LD], a.wgk), (m.wgv, a.wgv),
                     (m.rout, a.r_out_w), (m.fk, a.f_kernel), (m.wr, a.Wr)):
        ld(dst[:, :], src)
    wo_v = a.w_out.rearrange("(r g h d) n -> r h g d n", r=2, g=2, h=HH)
    for r in range(2):
        for h in range(HH):
            for g in range(2):
                at = 64 * r + 16 * h + 8 * g
                ld(m.wout[at:at + 8, :], wo_v[r, h, g])
    ld(m.gcol[:, 0:1], a.gate_local_w.rearrange("h (d o) -> (h d) o", o=1))
    ld(m.gcol[:, 1:2], a.gate_remote_w.rearrange("h (d o) -> (h d) o", o=1))
    for n, w in enumerate((a.A, a.B, a.W_in, a.W_gate, a.W_out)):
        ld(m.raw5[:, n, :], w)
    ld(m.bcol[:, 0:1], a.b_in.rearrange("(d o) -> d o", o=1))
    ld(m.bcol[:, 1:2], a.b_gate.rearrange("(d o) -> d o", o=1))
    ld(m.bout[:, :], rowb(a.b_out))
    ld(m.fbias[:, :], rowb(a.f_bias))
    ld(m.fsc[:, 0:1], rowb(a.f_sin))
    ld(m.fsc[:, 1:2], rowb(a.f_sk))
    ld(m.br[:, :], rowb(a.br))
    for n, b in enumerate((a.b1, a.b2)):
        ld(m.b12r[:, n, :], b)

    with nc.Block() as block:
        @block.sync
        def _(sp):
            for j in range(NJ):
                sp.dma_start(m.X[:, B * j:B * (j + 1), :],
                             a.x[:, P * j:P * (j + 1), :].rearrange("b p f -> p b f")).then_inc(m.s_x[j], 16)

        @block.scalar
        def _(act):
            for dst, src in loads:
                act.dma_start(dst, src).then_inc(s_w, 16)

        @block.gpsimd
        def _(e):
            done = [0]

            def step(ins):
                ins.then_inc(s_const, 1)
                done[0] += 1
                e.wait_ge(s_const, done[0])

            step(e.memset(m.ident[:, :], 0.0))
            step(e.affine_select(out=m.ident[:, :], in_=m.ident[:, :], compare_op=ALU.not_equal, fill=1.0, base=0,
                                 pattern=[[-1, P]], channel_multiplier=1))
            step(e.memset(m.gvx[:, :, :, :], 1.0))
            m.const_ident = done[0]
            step(e.memset(m.nhalf[:, :], -0.5))
            step(e.memset(m.xnT[:, 0:B, 0:WIN], 0.0))
            step(e.iota(m.iota8[:, :], pattern=[[1, E]], base=0, channel_multiplier=0,
                        allow_small_or_imprecise_dtypes=True))
            step(e.memset(m.cmask[:, :, :, :], 0.0))
            for q in range(HH):
                v = m.cmask[WIN * q:WIN * (q + 1), :, :, :].rearrange("p v b k -> p (v b) k")
                step(e.affine_select(out=v, in_=v, compare_op=ALU.is_ge, fill=NEG, base=-1,
                                     pattern=[[0, 2 * NB], [1, KW]], channel_multiplier=-1))
                step(e.affine_select(out=v, in_=v, compare_op=ALU.is_ge, fill=NEG, base=WIN,
                                     pattern=[[0, 2 * NB], [-1, KW]], channel_multiplier=1))
            step(e.affine_select(out=m.cmask[:, 1, 0, :], in_=m.cmask[:, 1, 0, :], compare_op=ALU.is_ge, fill=NEG,
                                 base=-WIN, pattern=[[1, KW]], channel_multiplier=0))

        @block.vector
        def _(e):
            done = [0]

            def step(ins):
                ins.then_inc(s_dve, 1)
                done[0] += 1
                e.wait_ge(s_dve, done[0])

            e.wait_ge(s_const, m.const_ident)
            step(e.tensor_reduce(m.hm[:, :], m.ident[:, :].rearrange("p (a h d) -> p h a d", a=HG, h=HH), axis=AX.XY, op=ALU.add))
            step(e.tensor_scalar(m.hm[:, :], m.hm[:, :], ISQ, None, ALU.mult))
            step(e.tensor_reduce(m.par[:, :], m.ident[:, :].rearrange("p (r k) -> p r k", r=2), axis=AX.X, op=ALU.add))
            step(e.tensor_reduce(m.lhm[:, :], m.ident[:, :].rearrange("p (r h d) -> p h r d", r=2, h=LH), axis=AX.XY, op=ALU.add))
            step(e.tensor_scalar(m.lhm[:, :], m.lhm[:, :], 1.0 / CHUNK, None, ALU.mult))
            for r in range(2):
                for g in range(2):
                    step(e.tensor_reduce(m.m16[:, 8 * r + g:8 * r + 8:2],
                                         m.ident[:, 64 * r + 32 * g:64 * r + 32 * g + 32].rearrange("p (h d) -> p h d", h=HH),
                                         axis=AX.X, op=ALU.add))
            step(e.tensor_copy(m.identb[:, :], m.ident[:, :]))
            step(e.tensor_copy(m.identh[:, :], m.ident[:, :]))
            step(e.memset(m.routp[LD:P, :], 0.0))
            for g in range(2):
                step(e.tensor_scalar(m.gvx[:, :, g, 8], m.gvx[:, :, g, 8], m.par[:, g:g + 1], None, ALU.mult))
            for j in range(NJ):
                e.wait_ge(m.s_x[j], 16)
                for u in range(B * j, B * (j + 1)):
                    last = e.bn_stats(m.stats[:, u, :], m.X[:, u, :])
            step(last)
            e.wait_ge(s_w, 16 * len(loads))
            for n in range(2):
                step(e.tensor_scalar(m.gbd[:, H * n:H * (n + 1)], m.m16[:, :], m.gcol[:, n:n + 1], None, ALU.mult))
            step(e.tensor_scalar(m.wout[:, :], m.wout[:, :], 0.5, None, ALU.mult))
            step(e.tensor_scalar(m.bcol[:, 2:3], m.bcol[:, 1:2], 0.5, None, ALU.mult))
            for r in range(2):
                for g in range(2):
                    step(e.tensor_copy(m.routp[0:LD, 64 * r:64 * r + 64].rearrange("p (h g d) -> p h g d", h=HH, g=2)[:, :, g, :],
                                       m.rout[:, 64 * r + 32 * g:64 * r + 32 * g + 32].rearrange("p (h d) -> p h d", h=HH)))
            step(e.reciprocal(m.fsc[:, 2:4], m.fsc[:, 0:2]))
            step(e.tensor_tensor(m.fsc[:, 4:5], m.fsc[:, 0:1], m.fsc[:, 1:2], ALU.mult))
            t, q, w = c.take(D), c.take(D), c.take(D)
            step(e.tensor_scalar(t, m.fk[:, :], m.fsc[:, 3:4], None, ALU.mult))
            step(round_e4m3fn(e, step, t, q, w, m.fkq[:, :]))
            e.wait_ge(s_pe, 1)
            step(e.tensor_copy(m.w5T[:, 0:4, :].rearrange("p n d -> p (n d)"), m.ps[0][:, :]))
            step(e.tensor_copy(m.w5T[:, 4:6, :].rearrange("p n d -> p (n d)"), m.ps[1][:, 0:256]))
            step(e.tensor_copy(m.b12[:, :, :, :].rearrange("p n j e -> p (n j e)"), m.ps[1][:, 256:256 + 2 * NC4 * E]))
            e.wait_ge(s_pe, 2)
            step(e.tensor_copy(m.wg[:, :], m.ps[2][:, 0:2 * H]))
            m.setup_steps = done[0]

        @block.tensor
        def _(e):
            e.wait_ge(s_const, m.const_ident)
            e.wait_ge(s_w, 16 * len(loads))
            for n in range(6):
                src = m.raw5[:, n, :] if n < 5 else m.wq[:, :]
                last = e.transpose(m.ps[n // 4][:, D * (n % 4):D * (n % 4) + D], src, m.ident[:, :])
            for n in range(2):
                for j in range(NC4):
                    last = e.transpose(m.ps[1][:, 256 + E * (NC4 * n + j):256 + E * (NC4 * n + j + 1)],
                                       m.b12r[:, n, P * j:P * (j + 1)], m.ident[0:E, 0:E])
            last.then_inc(s_pe, 1)
            e.wait_ge(s_dve, m.setup_steps - 1)
            e.matmul(m.ps[2][:, 0:2 * H], m.w5T[:, 5, :], m.gbd[:, :], start=True, stop=True).then_inc(s_pe, 1)


def round_e4m3fn(e, step, t, q, w, out):
    step(e.tensor_scalar(w.bitcast(U32), t.bitcast(U32), 0x7F800000, None, ALU.bitwise_and))
    step(e.tensor_scalar(w, w, 2.0 ** -6, 1.5 * 2.0 ** 20, ALU.max, ALU.mult))
    step(e.tensor_tensor(q, t, w, ALU.add))
    step(e.tensor_tensor(q, q, w, ALU.subtract))
    step(e.tensor_scalar(w.bitcast(U32), q.bitcast(U32), 0x7FFFFFFF, None, ALU.bitwise_and))
    step(e.tensor_scalar(w, w, 448.0, 448.0, ALU.max, ALU.subtract))
    step(e.tensor_scalar(w, w, 3.0e38, 0.0, ALU.mult, ALU.mult))
    return e.tensor_tensor(out, q, w, ALU.add)


MOMENTS = 6


def moments(e, s_step, before, st, mean, ve):
    n = [0]

    def step(ins):
        ins.then_inc(s_step, 1)
        n[0] += 1
        e.wait_ge(s_step, before + n[0])

    m1, q1, m2, q2 = (st[:, :, k] for k in (1, 2, 4, 5))
    step(e.tensor_tensor(mean, m1, m2, ALU.subtract))
    step(e.scalar_tensor_tensor(ve, mean, 0.25, mean, ALU.mult, ALU.mult))
    step(e.tensor_tensor(q1, q1, q2, ALU.add))
    step(e.scalar_tensor_tensor(ve, q1, 1.0 / D, ve, ALU.mult, ALU.add))
    step(e.tensor_tensor(mean, m1, m2, ALU.add))
    e.tensor_scalar(mean, mean, 0.5, None, ALU.mult)
    step(e.tensor_scalar(ve, ve, EPS, None, ALU.add))
    assert n[0] == MOMENTS


def norm_all(nc, ctx, m, a):
    def sem(name):
        return ctx.enter_context(nc.semaphore(name))
    s_var, s_rs = sem("ln1_var"), sem("ln1_rstd")
    s_xn, s_tr, s_cp, s_tail, s_pool = sem("ln1_normed"), sem("ln1_turned"), sem("ln1_stored"), sem("ln1_tails"), sem("ln1_pooled")
    s_lat, s_gk = sem("latents_made"), sem("latents_kept")
    c = Cut(m.work)
    xn = [c.take(B * D).rearrange("p (b d) -> p b d", b=B) for _ in range(2)]
    m.pool = c.take(B * NL).rearrange("p (b n) -> p b n", b=B)
    pool2 = c.take(B * 2 * NL).rearrange("p (b o n) -> p b o n", b=B, o=2)
    gk = c.take(B * LH * NL).rearrange("p (b h n) -> p b h n", b=B, h=LH)
    s_hi = sem("latents_high")

    with nc.Block() as block:
        @block.vector
        def _(e):
            moments(e, s_var, 0, m.stats[:, :, :], m.mv[:, :, 0], m.mv[:, :, 1])
            e.wait_ge(s_rs, 1)

            def norm(j, k):
                for b in range(B):
                    last = e.tensor_scalar(xn[k][:, b, :], m.X[:, B * j + b, :], m.mv[:, B * j + b, 0:1],
                                           m.rstd[:, bass.ds(B * j + b, 1)], ALU.subtract, ALU.mult)
                last.then_inc(s_xn, 1)

            def pooled(j):
                e.wait_ge(s_cp, 2 * j + 2)
                e.tensor_reduce(m.pool[:, :, bass.ds(8 * j, 8)],
                                m.xnT[:, bass.ds(B * j, B), WIN:XW].rearrange("p b (n t) -> p b n t", t=CHUNK), axis=AX.X, op=ALU.add).then_inc(s_pool, 1)

            norm(0, 0)
            norm(1, 1)
            for j in range(NJ - 2):
                e.wait_ge(s_tr, 2 * j + 2)
                norm(j + 2, j % 2)
                pooled(j)
            pooled(NJ - 2)
            pooled(NJ - 1)
            e.wait_ge(s_lat, 1)
            for b in range(B):
                e.tensor_tensor(gk[:, b, :, :],
                                m.ps[4][:, NL * b:NL * (b + 1)].rearrange("p (o n) -> p o n", o=1).broadcast_to([P, LH, NL]),
                                m.lhm[:, :].rearrange("p (h o) -> p h o", o=1).broadcast_to([P, LH, NL]), ALU.mult).then_inc(s_gk, 1)
            e.wait_ge(s_lat, 2)
            for g in range(2):
                last = e.tensor_scalar(m.gvx[:, :, g, 0:8], m.ps[5][:, :].rearrange("p (k g d) -> p k g d", g=2, d=8)[:, :, g, :],
                                       m.par[:, g:g + 1], 1.0 / CHUNK, ALU.mult, ALU.mult)
            last.then_inc(s_gk, 1)
            for b in range(B):
                e.wait_ge(s_hi, b + 1)
                e.tensor_tensor(m.gkl[:, b, :], gk[:, b, :, :].rearrange("p h n -> p (h n)"), m.gkh[:, b, :], ALU.subtract)
            e.wait_ge(s_hi, B + 1)
            e.tensor_tensor(m.gvl[:, :, :, :], m.gvx[:, :, :, :], m.gvh[:, :, :, :], ALU.subtract).then_inc(s_gk, 1)

        @block.gpsimd
        def _(e):
            e.wait_ge(s_var, MOMENTS)
            e.tensor_tensor(m.rstd[:, :], m.mv[:, :, 1], m.nhalf[:, :], ALU.pow).then_inc(s_rs, 1)
            with e.Fori(0, NJ) as j:
                e.wait_ge(s_cp, 2 * j + 2)
                e.tensor_copy(m.xnT[:, bass.ds(B * j + B, B), 0:WIN], m.xnT[:, bass.ds(B * j, B), P:XW]).then_inc(s_tail, 1)
            e.wait_ge(s_pool, NJ)
            e.tensor_copy(pool2[:, :, :, :], m.pool[:, :, :].rearrange("p b (o n) -> p b o n", o=1).broadcast_to([P, B, 2, NL])).then_inc(s_pool, 1)

        @block.tensor
        def _(e):
            def turn(j, k):
                e.wait_ge(s_xn, j + 1)
                for h in range(2):
                    if not isinstance(j, int) or j >= 2:
                        e.wait_ge(s_cp, 2 * (j - 2) + h + 1)
                    for b in range(HALF):
                        last = e.transpose(m.ps[2 * k + h][:, D * b:D * (b + 1)], xn[k][:, HALF * h + b, :], m.ident[:, :])
                    last.then_inc(s_tr, 1)

            turn(0, 0)
            turn(1, 1)
            with e.Fori(1, NJ // 2) as jj:
                for k in range(2):
                    turn(2 * jj + k, k)
            e.wait_ge(s_pool, NJ)
            e.matmul(m.ps[4][:, :], m.wgk[:, :], m.pool[:, :, :].rearrange("p b n -> p (b n)"), start=True, stop=True).then_inc(s_lat, 1)
            e.wait_ge(s_pool, NJ + 1)
            for b in range(B):
                last = e.matmul(m.ps[5][:, LD * b:LD * (b + 1)],
                                pool2[:, b, :, :].rearrange("p o n -> p (o n)"),
                                m.wgv[:, :], start=True, stop=True)
            last.then_inc(s_lat, 1)

        @block.scalar
        def _(e):
            def store(j, k):
                for h in range(2):
                    e.wait_ge(s_tr, 2 * j + h + 1)
                    e.copy(m.xnT[:, bass.ds(B * j + HALF * h, HALF), WIN:XW], m.ps[2 * k + h][:, :].rearrange("p (b t) -> p b t", b=HALF)).then_inc(s_cp, 1)
            with e.Fori(0, NJ // 2) as jj:
                for k in range(2):
                    store(2 * jj + k, k)
            for b in range(B):
                e.wait_ge(s_gk, b + 1)
                e.copy(m.gkh[:, b, :], gk[:, b, :, :].rearrange("p h n -> p (h n)")).then_inc(s_hi, 1)
            e.wait_ge(s_gk, B + 1)
            e.copy(m.gvh[:, :, :, :], m.gvx[:, :, :, :]).then_inc(s_hi, 1)


def wait(e, semaphore, value):
    if not isinstance(value, int) or value > 0:
        e.wait_ge(semaphore, value)


def skewed(e, front, back, n, peeled=1):
    def body(t):
        front(2 * t + 1, 1)
        back(2 * t, 0)
        front(2 * t + 2, 0)
        back(2 * t + 1, 1)

    front(0, 0)
    for t in range(peeled):
        body(t)
    with e.Fori(peeled, n // 2 - 1) as t:
        body(t)
    front(n - 1, 1)
    back(n - 2, 0)
    back(n - 1, 1)


def local_attention(nc, ctx, m, a):
    def sem(name):
        return ctx.enter_context(nc.semaphore("local_" + name))
    s_xd, s_qkg, s_kt, s_gt, s_qx, s_v, s_vx, s_ones = (sem(n) for n in ("windows", "qkg", "k", "gates", "q", "v", "v_kept", "ones"))
    s_sc, s_sm, s_mx, s_sub, s_exp = (sem(n) for n in ("scores", "masked", "max", "shifted", "exp"))
    s_t, s_ptd, s_pta, s_pv, s_rec, s_o = (sem(n) for n in ("turned", "turned_dve", "turned_act", "pv", "norm", "out"))
    NP = NU // 2
    NG = 4
    c = Cut(m.work)
    xd = [c.take(NB * 2 * KW).rearrange("p (b o k) -> p b o k", b=NB, o=2) for _ in range(2)]
    qx = [c.take(NB * P).rearrange("p (b h q) -> p b h q", b=NB, h=HH) for _ in range(2)]
    kx = [c.take(HG * XW).rearrange("p (g t) -> p g t", g=HG) for _ in range(2)]
    vx = c.take(4 * 576).rearrange("p (n g c) -> p n g c", g=2, c=9)
    Sc = [c.take(4 * 2 * HG * KW).rearrange("p (n u k) -> p n u k", n=4, u=2 * HG) for _ in range(2)]
    Pr = c.take(2 * NB * HG * KW).rearrange("p (u g k) -> p u g k", u=2 * NB, g=HG)
    PT = c.take(NG * NB * P).rearrange("p (n b c) -> p n b c", n=NG, b=NB)
    mx = c.take(2 * 4 * 2 * HG).rearrange("p (v n u) -> p v n u", v=2, n=4)
    rec = c.take(2 * H).rearrange("p (u s) -> p u s", u=2)
    bank_s, bank_t, bank_q, bank_v = m.ps[0:4], m.ps[4:6], m.ps[6], m.ps[7]

    def vbuf(v, k):
        return vx[:, 32 * (2 * v + k):32 * (2 * v + k) + 32, :, :]

    with nc.Block() as block:
        @block.gpsimd
        def _(e):
            def windows(i, units=(0, 1)):
                for k in units:
                    wait(e, s_v, 2 * i + k - 1)
                    for h in range(2):
                        e.tensor_copy(xd[k][:, :, :, WIN * h:WIN * h + WIN],
                                      m.xnT[:, 2 * i + k, WIN * h:WIN * h + P].rearrange("p (b o k) -> p b o k", b=NB, o=1)
                                      .broadcast_to([P, NB, 2, WIN])).then_inc(s_xd, 1)

            def front(i, v):
                for n in range(4):
                    if n % 2 == 0 and not (isinstance(i, int) and i == NP - 1):
                        windows(i + 1, (n // 2,))
                    e.wait_ge(s_mx, 4 * i + n + 1)
                    e.tensor_tensor(Sc[v][:, n, :, :], Sc[v][:, n, :, :],
                                    mx[:, v, n, :].rearrange("p (u o) -> p u o", o=1).broadcast_to([P, 2 * HG, KW]),
                                    ALU.subtract).then_inc(s_sub, 1)

            windows(0)
            skewed(e, front, lambda i, v: None, NP)

        @block.tensor
        def _(e):
            def turn(i, k):
                e.wait_ge(s_exp, 2 * i + k + 1)
                for r in range(2):
                    if k == 0:
                        wait(e, s_pta if r else s_ptd, 2 * i)
                    else:
                        e.wait_ge(s_pta if r else s_ptd, 2 * i + 1)
                    for b in range(NB):
                        last = e.transpose(bank_t[r][:, P * b:P * b + P],
                                           Pr[:, NB * k + b, 2 * r:2 * r + 2, :].rearrange("p g k -> p (g k)"), m.ident[:, :])
                    last.then_inc(s_t, 1)

            def front(i, v):
                for k in range(2):
                    if not (isinstance(i, int) and i == 0):
                        turn(i - 1, k)
                    if k == 1:
                        scores(i, 0)
                    u = 2 * i + k
                    wait(e, s_qx, u)
                    e.wait_ge(s_xd, 2 * u + 2)
                    e.matmul(bank_q[:, 0:P], m.wq[:, :], m.xnT[:, u, WIN:XW], start=True, stop=True)
                    e.matmul(bank_q[:, P:P + XW], m.wk[:, :], m.xnT[:, u, :], start=True, stop=True)
                    for b in range(NB):
                        last = e.matmul(bank_q[WIN * b:WIN * b + WIN, P + XW:P + XW + 2 * H], xd[k][:, b, 0, WIN:KW],
                                        m.wg[:, :], start=True, stop=True)
                    last.then_inc(s_qkg, 1)
                    if k == 0:
                        wait(e, s_o, i - 1)
                    wait(e, s_vx, u)
                    for b in range(NB):
                        last = e.matmul(bank_v[:, D * b:D * b + D], xd[k][:, b, :, :].rearrange("p o k -> p (o k)"),
                                        m.wv[:, :], start=True, stop=True)
                    last.then_inc(s_v, 1)
                scores(i, 1)

            def scores(i, k):
                e.wait_ge(s_kt, 2 * i + k + 1)
                e.wait_ge(s_qx, 2 * i + k + 1)
                for n in range(2 * k, 2 * k + 2):
                    wait(e, s_sm, 4 * (i - 1) + n + 1)
                    for t in range(2):
                        b = 2 * (n % 2) + t
                        last = e.matmul(bank_s[n][:, HG * KW * t:HG * KW * (t + 1)], qx[k][:, b, :, :].rearrange("p h q -> p (h q)"),
                                        kx[k][:, :, WIN * b:WIN * b + KW], start=True, stop=True)
                    last.then_inc(s_sc, 1)

            def back(i, v):
                if isinstance(i, int) and i == NP - 1:
                    for k in range(2):
                        turn(i, k)
                e.wait_ge(s_vx, 2 * i + 2)
                wait(e, s_v, 2 * i + 2)
                for n in range(NG):
                    k, r = n // 2, n % 2
                    e.wait_ge(s_ptd if n % 2 == 0 else s_pta, 2 * i + n // 2 + 1)
                    for b in range(NB):
                        for h in range(HH):
                            at = 144 * k + 18 * (HH * r + h)
                            last = e.matmul(bank_v[WIN * b:WIN * b + WIN, at:at + 18], PT[:, n, b, WIN * h:WIN * h + WIN],
                                            vbuf(v, k)[:, 8 * b + 4 * r + h, :, :].rearrange("p g c -> p (g c)"),
                                            start=True, stop=True)
                last.then_inc(s_pv, 1)

            def back_after(i, v):
                wait(e, s_vx, 2 * i + 4) if not (isinstance(i, int) and i == NP - 1) else None
                back(i, v)
            skewed(e, front, back_after, NP)

        @block.vector
        def _(e):
            e.memset(vx[:, :, :, :], 1.0).then_inc(s_ones, 1)
            e.wait_ge(s_ones, 1)
            for g in range(2):
                last = e.tensor_scalar(vx[:, :, g, 8], vx[:, :, g, 8], m.par[:, g:g + 1], None, ALU.mult)
            last.then_inc(s_ones, 1)
            for k in range(2):
                e.memset(kx[k], 0.0).then_inc(s_ones, 1)

            def keep(i, k):
                wait(e, s_pv, i)
                e.wait_ge(s_t, 4 * i + 2 * k + 1)
                e.tensor_copy(PT[:, 2 * k, :, :].rearrange("p b c -> p (b c)"), bank_t[0][:, :]).then_inc(s_ptd, 1)

            def front(i, v, var):
                for k in range(2):
                    if not (isinstance(i, int) and i == 0):
                        keep(i - 1, k)
                    if k == 1:
                        masked(i, v, var, 0)
                    u = 2 * i + k
                    e.wait_ge(s_gt, u + 1)
                    wait(e, s_sc, 4 * i)
                    e.tensor_tensor(qx[k].rearrange("p b h q -> p h b q"),
                                    bank_q[:, 0:P].rearrange("p (o b q) -> p o b q", o=1, b=NB).broadcast_to([P, HH, NB, WIN]),
                                    m.hm[:, :].rearrange("p (h o w) -> p h o w", o=1, w=1).broadcast_to([P, HH, NB, WIN]),
                                    ALU.mult).then_inc(s_qx, 1)
                masked(i, v, var, 1)

            def masked(i, v, var, k):
                for n in range(2 * k, 2 * k + 2):
                    e.wait_ge(s_sc, 4 * i + n + 1)
                    wait(e, s_exp, 2 * (i - 1))
                    half = slice(2 * (n % 2), 2 * (n % 2) + 2)
                    e.tensor_tensor(Sc[v][:, n, :, :].rearrange("p (b g) k -> p b g k", b=2),
                                    bank_s[n][:, :].rearrange("p (b g k) -> p b g k", b=2, g=HG),
                                    m.cmask[:, var, half, :].rearrange("p b (o k) -> p b o k", o=1).broadcast_to([P, 2, HG, KW]),
                                    ALU.add).then_inc(s_sm, 1)
                    e.wait_ge(s_sm, 4 * i + n + 1)
                    e.tensor_reduce(mx[:, v, n, :], Sc[v][:, n, :, :], axis=AX.X, op=ALU.max).then_inc(s_mx, 1)

            def back(i, v):
                if isinstance(i, int) and i == NP - 1:
                    for k in range(2):
                        keep(i, k)
                e.wait_ge(s_pv, i + 1)
                o = bank_v[:, 0:288].rearrange("p (u s c) -> p u s c", u=2, c=9)
                e.reciprocal(rec, o[:, :, :, 8]).then_inc(s_rec, 1)
                e.wait_ge(s_rec, 2 * i + 1)
                e.scalar_tensor_tensor(rec, m.glr[:, bass.ds(2 * i, 2), 0:H], 1.0, rec, ALU.add, ALU.mult).then_inc(s_rec, 1)
                e.wait_ge(s_rec, 2 * i + 2)
                e.tensor_tensor(m.mix[:, bass.ds(2 * i, 2), :].rearrange("p u (s d) -> p u s d", d=HD), o[:, :, :, 0:8],
                                rec.rearrange("p u (s o) -> p u s o", o=1).broadcast_to([P, 2, H, HD]), ALU.mult).then_inc(s_o, 1)

            def front_by_span(i, v):
                front(i, v, 1 if isinstance(i, int) and i < B // 2 else 0)
            skewed(e, front_by_span, back, NP, 2)

        @block.scalar
        def _(e):
            def keep(i, k):
                wait(e, s_pv, i)
                e.wait_ge(s_t, 4 * i + 2 * k + 2)
                e.copy(PT[:, 2 * k + 1, :, :].rearrange("p b c -> p (b c)"), bank_t[1][:, :]).then_inc(s_pta, 1)

            def exps(i, v):
                wait(e, s_t, 4 * i)
                for h in range(2):
                    e.wait_ge(s_sub, 4 * i + 2 * h + 2)
                    e.activation(Pr[:, NB * h:NB * h + NB, :, :].rearrange("p b g k -> p (b g k)"),
                                 Sc[v][:, 2 * h:2 * h + 2, :, :].rearrange("p n u k -> p (n u k)"), ACT.Exp).then_inc(s_exp, 1)

            def front(i, v):
                for k in range(2):
                    if not (isinstance(i, int) and i == 0):
                        keep(i - 1, k)
                    u = 2 * i + k
                    wait(e, s_sc, 4 * i)
                    e.wait_ge(s_qkg, u + 1)
                    if isinstance(i, int) and i == 0:
                        e.wait_ge(s_ones, 4)
                    for g in range(HG):
                        rows = slice(WIN * g, WIN * g + WIN)
                        last = e.copy(kx[k][rows, g, :], bank_q[rows, P:P + XW])
                    last.then_inc(s_kt, 1)
                    e.activation(m.glr[:, u, :], bank_q[:, P + XW:P + XW + 2 * H], ACT.Tanh, scale=0.5).then_inc(s_gt, 1)
                    e.wait_ge(s_v, u + 1)
                    if k == 0:
                        wait(e, s_pv, i - 1)
                    for g in range(2):
                        for r in range(2):
                            o = vbuf(v, k)[:, :, g, 0:8].rearrange("p (b r h) d -> p r b h d", b=NB, r=2)[:, r]
                            x = bank_v[:, :].rearrange("p (b r g h d) -> p r g b h d", b=NB, r=2, g=2, h=HH)[:, r, g]
                            last = e.activation(o, x, ACT.Copy, scale=m.par[:, g:g + 1])
                    last.then_inc(s_vx, 1)
                exps(i, v)

            def back(i, v):
                if isinstance(i, int) and i == NP - 1:
                    for k in range(2):
                        keep(i, k)

            skewed(e, front, back, NP)


def pipeline(e, stages, n, width, first, in_order=False):
    if not in_order:
        stages = sorted(stages, key=lambda x: -x[0])
    for r in range(first):
        for lag, f in stages:
            if r - lag >= 0:
                f(r - lag, (r - lag) % width, (r - lag) // width)
    if first < n:
        with e.Fori(first // width, n // width) as t:
            for r in range(width):
                for lag, f in stages:
                    f(width * t + (r - lag), (r - lag) % width, t + (r - lag) // width)
    for r in range(n, n + max(lag for lag, _ in stages)):
        for lag, f in stages:
            if r - lag < n:
                f(r - lag, (r - lag) % width, (r - lag) // width)


def latent_attention(nc, ctx, m, a):
    def sem(name):
        return ctx.enter_context(nc.semaphore("latent_" + name))
    s_gq, s_gqk, s_sc, s_sm, s_mx, s_sub, s_exp = (sem(n) for n in ("q", "q_kept", "scores", "masked", "max", "shifted", "exp"))
    s_t, s_pt, s_pv, s_rec, s_lat, s_t2, s_lt, s_rm, s_gr = (sem(n) for n in ("turned", "turned_kept", "pv", "recip", "normed", "out_turned", "out_kept", "remote", "gated"))
    s_ql, s_ph, s_pl = (sem(n) for n in ("q_low", "weights_high", "weights_low"))
    s_mix, s_t3, s_mt, s_wo, s_x, s_st = (sem(n) for n in ("mixed", "mix_turned", "mix_kept", "projected", "added", "stats"))
    W = B
    c = Cut(m.work)

    def two(n, shape=None, **k):
        out = [c.take(n) for _ in range(2)]
        return [v.rearrange(shape, **k) for v in out] if shape else out
    gq = [c.take(P, F16) for _ in range(2)]
    Sl = two(LH * NL, "p (h n) -> p h n", h=LH)
    Pl = two(LH * NL)
    Ph = [c.take(2 * LH * NL, F16) for _ in range(2)]
    PT = [c.take(2 * LH * NL, F16) for _ in range(2)]
    latf = two(D)
    lat = [v[:, 0:LD].rearrange("p (h d) -> p h d", h=LH) for v in latf]
    rec = two(LH)
    mxl = two(LH)
    latT = two(P)
    rem = two(D)
    fin = two(D)
    finT = two(P)
    lmask = c.take(NJ * NL).rearrange("p (j n) -> p j n", j=NJ)
    s_lm = sem("mask")
    bq, bs, bw, bt, bo, b2, br, b3 = m.ps

    with nc.Block() as block:
        @block.tensor
        def _(e):
            def q(u, k, j):
                wait(e, s_ql, u)
                e.matmul(bq[:, 0:P], m.wgq[:, :], m.xnT[:, u, WIN:XW], start=True, stop=True).then_inc(s_gq, 1)

            def scores(u, k, j):
                e.wait_ge(s_ql, u + 1)
                wait(e, s_sm, u)
                e.matmul(bs[:, :], gq[k % 2], m.gkh[:, k, :], start=True, stop=False)
                e.matmul(bs[:, :], gq[k % 2], m.gkl[:, k, :], start=False, stop=True).then_inc(s_sc, 1)

            def turn(u, k, j):
                e.wait_ge(s_pl, u + 1)
                wait(e, s_pt, u)
                for n in range(8):
                    last = e.transpose(bt.bitcast(F16)[:, P * n:P * n + P], Ph[k % 2][:, P * n:P * n + P], m.identh[:, :])
                last.then_inc(s_t, 1)

            def pv(u, k, j):
                e.wait_ge(s_pt, u + 1)
                wait(e, s_lat, u)
                for n in range(4):
                    high, low = PT[k % 2][:, P * n:P * n + P], PT[k % 2][:, P * (4 + n):P * (4 + n) + P]
                    vh, vl = [v[:, 4 * k + n, :, :].rearrange("p g c -> p (g c)") for v in (m.gvh, m.gvl)]
                    o = bo[:, 18 * n:18 * n + 18]
                    e.matmul(o, high, vh, start=n == 0, stop=False, skip_group_check=True)
                    e.matmul(o, high, vl, start=False, stop=False, skip_group_check=True)
                    last = e.matmul(o, low, vh, start=False, stop=n == 3, skip_group_check=True)
                last.then_inc(s_pv, 1)

            def turn_out(u, k, j):
                e.wait_ge(s_lat, u + 1)
                wait(e, s_lt, u)
                e.transpose(b2[:, 0:P], latf[k % 2], m.ident[:, :]).then_inc(s_t2, 1)

            def remote(u, k, j):
                e.wait_ge(s_lt, u + 1)
                wait(e, s_gr, u)
                e.matmul(br[:, 0:D], latT[k % 2], m.routp[:, :], start=True, stop=True).then_inc(s_rm, 1)

            def turn_mix(u, k, j):
                e.wait_ge(s_mix, u + 1)
                wait(e, s_mt, u)
                e.transpose(b3[:, 0:P], fin[k % 2], m.ident[:, :]).then_inc(s_t3, 1)

            def project(u, k, j):
                e.wait_ge(s_mt, u + 1)
                wait(e, s_x, u)
                e.matmul(bw[:, 0:D], finT[k % 2], m.wout[:, :], start=True, stop=True).then_inc(s_wo, 1)

            pipeline(e, [(10, project), (9, turn_mix), (8, remote), (7, turn_out), (6, pv), (5, turn), (2, scores), (0, q)], NU, W, 2 * W, in_order=True)

        @block.vector
        def _(e):
            def top(u, k, j):
                e.wait_ge(s_sc, u + 1)
                wait(e, s_exp, u - 1)
                e.tensor_tensor(Sl[k % 2], bs[:, :].rearrange("p (h n) -> p h n", h=LH),
                                lmask[:, j, :].rearrange("p (o n) -> p o n", o=1).broadcast_to([P, LH, NL]),
                                ALU.add).then_inc(s_sm, 1)
                e.wait_ge(s_sm, u + 1)
                e.tensor_reduce(mxl[k % 2], Sl[k % 2], axis=AX.X, op=ALU.max).then_inc(s_mx, 1)

            def norm(u, k, j):
                e.wait_ge(s_pv, u + 1)
                wait(e, s_t2, u - 1)
                o = bo[:, 0:LH * 9].rearrange("p (h c) -> p h c", c=9)
                e.reciprocal(rec[k % 2], o[:, :, 8]).then_inc(s_rec, 1)
                e.wait_ge(s_rec, u + 1)
                e.tensor_tensor(lat[k % 2], o[:, :, 0:8],
                                rec[k % 2].rearrange("p (h o) -> p h o", o=1).broadcast_to([P, LH, 8]), ALU.mult).then_inc(s_lat, 1)

            def gate(u, k, j):
                e.wait_ge(s_rm, u + 1)
                wait(e, s_mix, u - 1)
                e.scalar_tensor_tensor(rem[k % 2].rearrange("p (s d) -> p s d", d=HD),
                                       m.glr[:, u, H:2 * H].rearrange("p (s o) -> p s o", o=1).broadcast_to([P, H, HD]), 1.0,
                                       br[:, 0:D].rearrange("p (s d) -> p s d", d=HD), ALU.add, ALU.mult).then_inc(s_gr, 1)

            def add(u, k, j):
                e.wait_ge(s_wo, u + 1)
                e.tensor_tensor(m.X[:, u, :], m.X[:, u, :], bw[:, 0:D], ALU.add).then_inc(s_x, 1)

            def stat(u, k, j):
                e.wait_ge(s_x, u + 1)
                e.bn_stats(m.stats[:, u, :], m.X[:, u, :]).then_inc(s_st, 1)

            def low_q(u, k, j):
                e.wait_ge(s_gqk, u + 1)
                q = gq[k % 2][LD:P]
                e.scalar_tensor_tensor(q, bq[LD:P, 0:P], ISQ, q, ALU.mult, ALU.subtract).then_inc(s_ql, 1)

            for v in latf:
                e.memset(v[:, LD:D], 0.0)
            e.wait_ge(s_lm, 2)
            pipeline(e, [(1, low_q), (11, stat), (10, add), (8, gate), (6, norm), (2, top)], NU, W, 2 * W, in_order=True)
            e.wait_ge(s_st, NU)

        @block.gpsimd
        def _(e):
            e.memset(lmask, 0.0).then_inc(s_lm, 1)
            e.wait_ge(s_lm, 1)
            e.affine_select(out=lmask, in_=lmask, compare_op=ALU.is_ge, fill=NEG, base=0,
                            pattern=[[P, NJ], [-CHUNK, NL]], channel_multiplier=1).then_inc(s_lm, 1)
            e.wait_ge(s_lm, 2)

            def sub(u, k, j):
                e.wait_ge(s_mx, u + 1)
                e.tensor_tensor(Sl[k % 2], Sl[k % 2], mxl[k % 2].rearrange("p (h o) -> p h o", o=1).broadcast_to([P, LH, NL]),
                                ALU.subtract).then_inc(s_sub, 1)

            def mixed(u, k, j):
                e.wait_ge(s_gr, u + 1)
                wait(e, s_t3, u - 1)
                e.tensor_tensor(fin[k % 2], m.mix[:, u, :], rem[k % 2], ALU.add).then_inc(s_mix, 1)

            def low(u, k, j):
                e.wait_ge(s_ph, u + 1)
                e.tensor_tensor(Ph[k % 2][:, LH * NL:2 * LH * NL], Pl[k % 2], Ph[k % 2][:, 0:LH * NL], ALU.subtract).then_inc(s_pl, 1)

            pipeline(e, [(3, sub), (8, mixed), (4, low)], NU, W, 2 * W, in_order=True)

        @block.scalar
        def _(e):
            def keep_q(u, k, j):
                e.wait_ge(s_gq, u + 1)
                wait(e, s_sc, u - 1)
                e.mul(gq[k % 2], bq[:, 0:P], ISQ).then_inc(s_gqk, 1)

            def exps(u, k, j):
                e.wait_ge(s_sub, u + 1)
                wait(e, s_pl, u - 1)
                e.activation(Pl[k % 2], Sl[k % 2].rearrange("p h n -> p (h n)"), ACT.Exp).then_inc(s_exp, 1)

            def high(u, k, j):
                e.wait_ge(s_exp, u + 1)
                wait(e, s_t, u - 1)
                e.copy(Ph[k % 2][:, 0:LH * NL], Pl[k % 2]).then_inc(s_ph, 1)

            def keep_pt(u, k, j):
                e.wait_ge(s_t, u + 1)
                wait(e, s_pv, u - 1)
                e.copy(PT[k % 2], bt.bitcast(F16)).then_inc(s_pt, 1)

            def keep_out(u, k, j):
                e.wait_ge(s_t2, u + 1)
                wait(e, s_rm, u - 1)
                e.copy(latT[k % 2], b2[:, 0:P]).then_inc(s_lt, 1)

            def keep_mix(u, k, j):
                e.wait_ge(s_t3, u + 1)
                wait(e, s_wo, u - 1)
                e.copy(finT[k % 2], b3[:, 0:P]).then_inc(s_mt, 1)

            pipeline(e, [(1, keep_q), (4, high), (9, keep_mix), (7, keep_out), (3, exps), (5, keep_pt)], NU, W, 2 * W, in_order=True)


def ffn(nc, ctx, m, a):
    def sem(name):
        return ctx.enter_context(nc.semaphore("ffn_" + name))
    s_mo, s_rs, s_n, s_q, s_t, s_qt, s_y, s_y1, s_y2, s_x, s_st = (
        sem(n) for n in ("moments", "rstd", "normed", "rounded", "turned", "turned_kept", "product", "scaled", "biased", "added", "stats"))
    c = Cut(m.work)
    w = B * D
    xb = c.take(w, BF16)
    t, sc = c.take(w), c.take(w)
    q = c.take(w)
    qb = [c.take(w, BF16) for _ in range(2)]
    qT = [c.take(w, BF16) for _ in range(2)]
    y1 = [c.take(w, BF16) for _ in range(2)]
    y2 = [c.take(w, BF16) for _ in range(2)]
    s_in, s_w3, s_b3, s_z, s_hi, s_lo = (
        sem(n) for n in ("experts_loaded", "experts_down_loaded", "b3_loaded", "b3_zeros", "experts_high", "experts_low"))
    st, st3 = [v.rearrange("p (e f) -> p e f", e=E) for v in (m.Wst, m.W3st)]
    whole, high, low = (st, st, st3), (m.W1h, m.W2h, m.W3h), (m.W1l, m.W2l, m.W3l)

    with nc.Block() as block:
        @block.vector
        def _(e):
            moments(e, s_mo, 0, m.stats[:, :, :], m.mv[:, :, 0], m.mv[:, :, 1])
            e.wait_ge(s_rs, 1)

            def rounded(i, k, j):
                for b in range(B):
                    u = B * i + b
                    last = e.tensor_scalar(xb[:, D * b:D * b + D], m.X[:, u, :], m.mv[:, u, 0:1], m.rstd[:, bass.ds(u, 1)],
                                           ALU.subtract, ALU.mult)
                n = [0]

                def step(ins):
                    ins.then_inc(s_n, 1)
                    n[0] += 1
                    e.wait_ge(s_n, FFN_STEPS * i + n[0])
                step(last)
                step(e.tensor_scalar(t, xb, m.fsc[:, 2:3], None, ALU.mult))
                wait(e, s_t, i - 1)
                round_e4m3fn(e, step, t, q, sc, qb[k]).then_inc(s_q, 1)
                e.wait_ge(s_q, i + 1)
                assert n[0] == FFN_STEPS

            def stat(i, k, j):
                e.wait_ge(s_x, i + 1)
                for b in range(B):
                    last = e.bn_stats(m.stats[:, B * i + b, :], m.X[:, B * i + b, :])
                last.then_inc(s_st, 1)

            pipeline(e, [(0, rounded), (2, stat)], NJ, 2, NJ, in_order=True)
            e.wait_ge(s_st, NJ)
            moments(e, s_mo, MOMENTS, m.stats[:, :, :], m.mv[:, :, 0], m.mv[:, :, 1])

        @block.gpsimd
        def _(e):
            e.wait_ge(s_mo, MOMENTS)
            e.tensor_tensor(m.rstd[:, :], m.mv[:, :, 1], m.nhalf[:, :], ALU.pow).then_inc(s_rs, 1)

            e.memset(m.b3bd, 0.0).then_inc(s_z, 1)

            def lows(i, k, j):
                if isinstance(i, int) and i < 3:
                    e.wait_ge(s_hi, i + 1)
                    e.tensor_tensor(low[i], whole[i], high[i], ALU.subtract).then_inc(s_lo, 1)

            def bias(i, k, j):
                e.wait_ge(s_y1, 2 * i + 2)
                wait(e, s_x, i - 1)
                e.tensor_tensor(y2[k].rearrange("p (b n) -> p b n", b=B), y1[k].rearrange("p (b n) -> p b n", b=B),
                                m.fbias[:, :].rearrange("p (o n) -> p o n", o=1).broadcast_to([P, B, D]), ALU.add).then_inc(s_y2, 1)
                e.wait_ge(s_y2, i + 1)
                x = m.X[:, bass.ds(B * i, B), :]
                e.tensor_tensor(x, x, y2[k].rearrange("p (b n) -> p b n", b=B), ALU.add).then_inc(s_x, 1)
            pipeline(e, [(0, lows), (1, bias)], NJ, 2, 4)
            e.wait_ge(s_mo, 2 * MOMENTS)
            e.tensor_tensor(m.rstd[:, :], m.mv[:, :, 1], m.nhalf[:, :], ALU.pow).then_inc(s_rs, 1)
            e.wait_ge(s_rs, 2)

        @block.tensor
        def _(e):
            def turn(i, k, j):
                e.wait_ge(s_q, i + 1)
                wait(e, s_qt, i - 1)
                for b in range(B):
                    last = e.transpose(m.ps[k][:, :].bitcast(BF16)[:, P * b:P * b + P], qb[k][:, D * b:D * b + D], m.identb[:, :])
                last.then_inc(s_t, 1)

            def product(i, k, j):
                e.wait_ge(s_qt, i + 1)
                for h in range(2):
                    wait(e, s_y1, 2 * (i - 2) + h + 1)
                    for b in range(HALF):
                        u = HALF * h + b
                        last = e.matmul(m.ps[2 + 2 * k + h][:, D * b:D * b + D], qT[k][:, P * u:P * u + P], m.fkq[:, :], start=True, stop=True)
                    last.then_inc(s_y, 1)
            pipeline(e, [(0, turn), (1, product)], NJ, 2, 4)

        @block.scalar
        def _(e):
            def keep(i, k, j):
                e.wait_ge(s_t, i + 1)
                wait(e, s_y, 2 * (i - 1))
                e.copy(qT[k], m.ps[k][:, :].bitcast(BF16)).then_inc(s_qt, 1)

            def scale(i, k, j):
                wait(e, s_y2, i - 1)
                for h in range(2):
                    e.wait_ge(s_y, 2 * i + h + 1)
                    e.activation(y1[k][:, 512 * h:512 * h + 512], m.ps[2 + 2 * k + h][:, :], ACT.Copy, scale=m.fsc[:, 4:5]).then_inc(s_y1, 1)
            def highs(i, k, j):
                if isinstance(i, int) and i < 3:
                    if i < 2:
                        e.wait_ge(s_in, 16 * i + 16)
                    else:
                        e.wait_ge(s_w3, 16 * NC4)
                        e.wait_ge(s_lo, 2)
                    e.copy(high[i], whole[i]).then_inc(s_hi, 1)

            pipeline(e, [(0, keep), (0, highs), (1, scale)], NJ, 2, 4)

        @block.sync
        def _(sp):
            sp.dma_start(st, a.W1.rearrange("e d f -> d e f")).then_inc(s_in, 16)
            for n in range(NC4):
                sp.dma_start(st3[:, :, D * n:D * n + D], a.W3[:, P * n:P * n + P, :].rearrange("e p n -> p e n")).then_inc(s_w3, 16)
            sp.wait_ge(s_z, 1)
            for b in range(B):
                sp.dma_start(m.b3bd[E * b:E * (b + 1), D * b:D * (b + 1)], a.b3).then_inc(s_b3, 16)
            sp.wait_ge(s_lo, 1)
            sp.dma_start(st, a.W2.rearrange("e d f -> d e f")).then_inc(s_in, 16)
            sp.wait_ge(s_b3, 16 * B)


FFN_STEPS = 9


def scan_and_experts(nc, ctx, m, a):
    def sem(name):
        return ctx.enter_context(nc.semaphore("x_" + name))
    s_n3, s_t3, s_x3, s_pi, s_in, s_pg, s_g, s_gl, s_c = (
        sem(n) for n in ("normed", "turned", "xT", "in_proj", "inp", "gate_proj", "gate_tanh", "gate_links", "carry"))
    s_gc, s_k2, s_cb, s_u = (sem(n) for n in ("gate_moved", "carry_links", "carry_moved", "drive"))
    s_ch, s_th, s_r = (sem(n) for n in ("step_product", "step_tanh", "step_state"))
    s_a, s_sa, s_b, s_h, s_hh, s_hl, s_w3, s_ys, s_yd = (
        sem(n) for n in ("up_a", "silu", "up_b", "hidden", "hidden_high", "hidden_low", "down", "weighed", "summed"))
    s_bo, s_S, s_po, s_xo, s_mo, s_rs, s_n4, s_t4, s_x4f, s_x4h, s_x4, s_pr, s_d, s_w, s_k, s_cw, s_cc, s_tc, s_ct, s_pb, s_xb = (
        sem(n) for n in ("out_biased", "states", "out_proj", "residual", "moments4", "rstd4", "normed4", "turned4", "xT4", "high4", "parts4",
                         "logits", "gap", "gap_tanh", "chain", "shares", "shares_moved", "shares_turned", "shares_kept", "bias_sum", "biased"))
    s_out, s_z, s_tk = sem("written"), sem("zeroed"), sem("tick_zeroed")

    c = Cut(m.work)
    w = B * P
    n4 = c.take(w).rearrange("p (b d) -> p b d", b=B)
    Sx = c.take(w).rearrange("p (b t) -> p b t", b=B)
    g = c.take(w)
    gv = g.rearrange("p (b t) -> p b t", b=B)
    inpN, gN, CN = [m.W3st[:, n * w:(n + 1) * w] for n in range(3)]
    n3 = c.take(N5).rearrange("p (b d) -> p b d", b=HALF)
    x3 = c.take(N5)
    tmp = c.take(N5)
    Cb = c.take(B * (P + 1)).rearrange("p (b t) -> p b t", b=B)
    R = c.take(B * (P + 1)).rearrange("p (b t) -> p b t", b=B)
    x4f = c.take(w)
    x4h, x4l = c.take(w, F16), c.take(w, F16)
    sa = [c.take(N5) for _ in range(2)]
    hb = [c.take(N5) for _ in range(2)]
    hh = [c.take(N5, F16) for _ in range(NC4)]
    hl = [m.W3st[:, 3 * w + N5 // 2 * n:3 * w + N5 // 2 * (n + 1)].bitcast(F16) for n in range(NC4)]
    gT = c.take(N5)
    yw = c.take(N5)
    th = [c.take(B) for _ in range(2)]
    lg = c.take(B * E).rearrange("p (b e) -> p b e", b=B)
    mx8 = c.take(B * E).rearrange("p (b e) -> p b e", b=B)
    ix = c.take(B * E).bitcast(U32).rearrange("p (b e) -> p b e", b=B)
    ixf = c.take(B * 2).rearrange("p (b e) -> p b e", b=B)
    ws = c.take(B * 2).rearrange("p (b e) -> p b e", b=B)
    eq = [c.take(B * E).rearrange("p (b e) -> p b e", b=B) for _ in range(2)]
    cwp = c.take(P)
    cwN = cwp[:, 0:B * E].rearrange("p (b e) -> p b e", b=B)
    cw = c.take(B * E).rearrange("p (b e) -> p b e", b=B)
    cwT = c.take(P)[0:B * E]
    U = m.psum[:, 0:1024]
    bU, bA, bB, bY, bZ = m.ps[0:2], m.ps[2:4], m.ps[4:6], m.ps[6], m.ps[7]
    AT, BT, WinT, WgT, WoT = (m.w5T[:, n, :] for n in range(5))

    def rounds(e, round_):
        round_(0, True, False, False, True)
        round_(1, True, False, True, True)
        with e.Fori(2, NJ - 1) as j:
            round_(j, True, True, True, True)
        round_(NJ - 1, True, True, True, False)
        round_(NJ, False, True, True, False)

    def places(e, j, late, turns, place):
        def turn(n):
            k = (n - LATE) % TURNS
            if not (late if n < LATE else turns):
                return None
            return TURNS * (j - 1) + n - LATE, j - 2 if n < LATE else j - 1, k // E, k % E

        for n in range(TURNS if turns or j == 0 else LATE):
            place(n, turn(n), turn(n - 1))

    NORMED, TURNED, GATED = (LATE + 1, LATE + E), (LATE + 2, LATE + E + 1), (LATE + 3, LATE + E + 2)

    with nc.Block() as block:
        @block.tensor
        def _(e):
            def turned(q):
                e.wait_ge(s_n3, q + 1)
                wait(e, s_g, q)
                for b in range(HALF):
                    last = e.transpose(bZ[:, P * b:P * b + P], n3[:, b, :], m.ident[:, :])
                last.then_inc(s_t3, 1)

            def in_proj(q):
                e.wait_ge(s_x3, q + 1)
                e.matmul(bZ, WinT, x3, start=True, stop=True).then_inc(s_pi, 1)

            def gate_proj(q, h):
                e.wait_ge(s_in, q + 1)
                e.matmul(bZ, WgT, inpN[:, N5 * h:N5 * h + N5], start=True, stop=True).then_inc(s_pg, 1)

            def step(j, t):
                wait(e, s_r, P * j + t)
                if isinstance(t, int) and t == 0:
                    e.wait_ge(s_u, j + 1)
                e.matmul(U[:, bass.ds(B * t, B)], AT, R[:, :, bass.ds(t, 1)].rearrange("p b o -> p (b o)"),
                         start=False, stop=True, skip_group_check=True).then_inc(s_ch, 1)

            def out_proj(p, h):
                if h == 0:
                    e.wait_ge(s_S, p + 1)
                    e.wait_ge(s_g, 2 * p + 4 if not isinstance(p, int) or p < NJ - 1 else 2 * NJ)
                else:
                    e.wait_ge(s_xo, 2 * p + 1)
                for b in range(HALF):
                    last = e.matmul(bZ[:, D * b:D * b + D], Sx[:, HALF * h + b, :], WoT, start=True, stop=True)
                last.then_inc(s_po, 1)

            def start(j, scan, post):
                if scan:
                    wait(e, s_th, P * j)
                    e.wait_ge(s_in, 2 * j + 2)
                    for h in range(2):
                        e.matmul(bU[h], BT, inpN.rearrange("p (b t) -> p t b", b=B)[:, 64 * h:64 * h + 64, :], start=True, stop=True)
                if post:
                    out_proj(j - 1, 0)
                if scan:
                    e.wait_ge(s_cb, j + 1)
                    for h in range(2):
                        last = e.matmul(bU[h], AT, Cb[:, :, 0:P].rearrange("p b t -> p t b")[:, 64 * h:64 * h + 64, :], start=False, stop=True, skip_group_check=True)
                    last.then_inc(s_u, 1)

            def turn4(p, h):
                e.wait_ge(s_n4, 2 * p + h + 1)
                e.wait_ge(s_x4h if h else s_xo, 2 * p + 2 - h)
                for b in range(HALF):
                    last = e.transpose(bZ[:, P * b:P * b + P], n4[:, HALF * h + b, :], m.ident[:, :])
                last.then_inc(s_t4, 1)

            def logits(p):
                e.wait_ge(s_x4f, 2 * p + 2)
                for b in range(B):
                    last = e.matmul(bZ[:, E * b:E * b + E], x4f[:, P * b:P * b + P], m.wr[:, :], start=True, stop=True)
                last.then_inc(s_pr, 1)

            def turn_shares(p):
                e.wait_ge(s_cw, p + 1)
                e.transpose(bZ[:, 0:P], cwp, m.ident[:, :]).then_inc(s_tc, 1)

            def bias_sum(p, h):
                if h:
                    e.wait_ge(s_xb, 2 * p + 1)
                else:
                    e.wait_ge(s_ct, p + 1)
                e.matmul(bZ, cwT, m.b3bd[:, N5 * h:N5 * h + N5], start=True, stop=True).then_inc(s_pb, 1)

            def down(turn, ch):
                g, span, h, x = turn
                if ch == 0:
                    wait(e, s_ys, g)
                for k, (part, W, ready) in enumerate(((hh, m.W3h, s_hh), (hh, m.W3l, None), (hl, m.W3h, s_hl))):
                    if ready:
                        e.wait_ge(ready, 4 * g + ch + 1)
                    for b in range(HALF):
                        last = e.matmul(bY[:, D * b:D * b + D], part[ch][:, P * b:P * b + P], W[:, x, D * ch:D * ch + D],
                                        start=(ch == 0 and k == 0 and b == 0), stop=(ch == NC4 - 1 and k == 2), skip_group_check=True)
                last.then_inc(s_w3, 1)

            def round_(j, scan, late, turns, ahead):
                start(j, scan, turns)
                beside = {}
                if turns:
                    p = j - 1
                    beside = {2: lambda: out_proj(p, 1), 9: lambda: turn4(p, 0), 11: lambda: turn4(p, 1), 13: lambda: logits(p),
                              19: lambda: turn_shares(p), 21: lambda: bias_sum(p, 0), 23: lambda: bias_sum(p, 1)}
                if ahead:
                    for h in range(2):
                        q, n = 2 * (j + 1) + h, STEPS * TURNED[h]
                        beside[n] = (lambda q=q: (wait(e, s_xb, 2 * j) if turns else None, turned(q)))
                        beside[n + 2] = lambda q=q: in_proj(q)
                        beside[n + 5] = lambda q=q, h=h: gate_proj(q, h)

                def place(n, now, before):
                    for s in range(STEPS):
                        if scan:
                            step(j, STEPS * n + s)
                        if STEPS * n + s in beside:
                            beside[STEPS * n + s]()
                        if now is None:
                            continue
                        g, span, h, x = now
                        ch = s // 2
                        f = slice(P * ch, P * ch + P)
                        xh, xl = [v[:, N5 * h:N5 * h + N5] for v in (x4h, x4l)]
                        if s % 2 == 0:
                            if x == 0 and s == 0:
                                e.wait_ge(s_x4, 2 * j - 1 + h)
                            wait(e, s_sa, 4 * g + ch - 1)
                            e.matmul(bA[ch % 2], m.W1h[:, x, f], xh, start=True, stop=False)
                            e.matmul(bA[ch % 2], m.W1h[:, x, f], xl, start=False, stop=False)
                            e.matmul(bA[ch % 2], m.W1l[:, x, f], xh, start=False, stop=True).then_inc(s_a, 1)
                            wait(e, s_h, 4 * g + ch - 1)
                            e.matmul(bB[ch % 2], m.W2h[:, x, f], xh, start=True, stop=False)
                            e.matmul(bB[ch % 2], m.W2h[:, x, f], xl, start=False, stop=False)
                        else:
                            e.matmul(bB[ch % 2], m.W2l[:, x, f], xh, start=False, stop=True).then_inc(s_b, 1)
                            if ch >= DEEP:
                                down(now, ch - DEEP)
                            elif before:
                                down(before, NC4 - DEEP + ch)

                places(e, j, late, turns, place)

            for h in range(2):
                turned(h)
                in_proj(h)
                gate_proj(h, h)
            rounds(e, round_)
            round_(NJ + 1, False, True, False, False)
            for ch in range(NC4 - DEEP, NC4):
                down((TURNS * NJ - 1, NJ - 1, 1, E - 1), ch)

        @block.scalar
        def _(e):
            e.preload_act_table_set("silu_and_others")

            def keep_x(q):
                e.wait_ge(s_t3, q + 1)
                wait(e, s_pi, q)
                e.copy(x3, bZ).then_inc(s_x3, 1)

            def keep_inp(q, h):
                e.wait_ge(s_pi, q + 1)
                e.activation(inpN[:, N5 * h:N5 * h + N5], bZ, ACT.Identity, bias=m.bcol[:, 0:1]).then_inc(s_in, 1)

            def keep_gate(q):
                e.wait_ge(s_pg, q + 1)
                wait(e, s_c, q)
                e.activation(gT, bZ, ACT.Tanh, bias=m.bcol[:, 2:3], scale=0.5).then_inc(s_g, 1)

            def step(j, t, k):
                e.wait_ge(s_ch, P * j + t + 1)
                e.activation(th[k], U[:, bass.ds(B * t, B)], ACT.Tanh).then_inc(s_th, 1)

            def keep4(p, h):
                e.wait_ge(s_t4, 2 * p + h + 1)
                wait(e, s_pr, p)
                wait(e, s_x4, 2 * p)
                e.copy(x4f[:, N5 * h:N5 * h + N5], bZ).then_inc(s_x4f, 1)

            def high4(p, h):
                if h == 0:
                    wait(e, s_b, 4 * (TURNS * (p - 1) + E))
                    e.copy(x4h[:, 0:N5], bZ).then_inc(s_x4h, 1)
                else:
                    wait(e, s_b, 4 * TURNS * p)
                    e.wait_ge(s_x4f, 2 * p + 2)
                    e.copy(x4h[:, N5:2 * N5], x4f[:, N5:2 * N5]).then_inc(s_x4h, 1)

            def high(turn, ch):
                g_ = turn[0]
                e.wait_ge(s_h, 4 * g_ + ch + 1)
                wait(e, s_w3, 4 * g_ + ch - 3)
                e.copy(hh[ch], hb[ch % 2]).then_inc(s_hh, 1)

            def gap(p):
                e.wait_ge(s_d, p + 1)
                e.activation(ws[:, :, 0], ws[:, :, 1], ACT.Tanh, scale=0.5).then_inc(s_w, 1)

            def keep_shares(p):
                e.wait_ge(s_tc, p + 1)
                e.copy(cwT, bZ[0:B * E, 0:P]).then_inc(s_ct, 1)

            def round_(j, scan, late, turns, ahead):
                if scan:
                    e.wait_ge(s_c, 2 * j + 2)
                    wait(e, s_r, P * j)
                    e.copy(g, gN).then_inc(s_gc, 1)
                beside = {}
                if turns:
                    p = j - 1
                    beside = {10: lambda: (keep4(p, 0), high4(p, 0)), 12: lambda: keep4(p, 1), 17: lambda: gap(p), 20: lambda: keep_shares(p),
                              STEPS * LATE + 1: lambda: high4(p, 1)}
                if ahead:
                    for h in range(2):
                        q, n = 2 * (j + 1) + h, STEPS * TURNED[h]
                        beside[n + 1] = lambda q=q: keep_x(q)
                        beside[n + 3] = lambda q=q, h=h: keep_inp(q, h)
                        beside[n + 7] = lambda q=q: keep_gate(q)

                def place(n, now, before):
                    for s in range(STEPS):
                        if scan:
                            step(j, STEPS * n + s, s % 2)
                        if STEPS * n + s in beside:
                            beside[STEPS * n + s]()
                        if s % 2 == 0 and (now if s else before):
                            high(*((now, s // 2 - 1) if s else (before, NC4 - 1)))
                        if now and s % 2 == 0:
                            g_, span, h, x = now
                            ch = s // 2
                            e.wait_ge(s_a, 4 * g_ + ch + 1)
                            wait(e, s_h, 4 * g_ + ch - 1)
                            e.activation(sa[ch % 2], bA[ch % 2], ACT.Silu, bias=m.b12[:, 0, ch, x:x + 1]).then_inc(s_sa, 1)

                places(e, j, late, turns, place)

            for h in range(2):
                keep_x(h)
                keep_inp(h, h)
                keep_gate(h)
            rounds(e, round_)
            round_(NJ + 1, False, True, False, False)
            high((TURNS * NJ - 1,), NC4 - 1)

        @block.gpsimd
        def _(e):
            e.memset(R[:, :, 0:1], 0.0).then_inc(s_z, 1)
            e.memset(Cb[:, :, 0:1], 0.0).then_inc(s_z, 1)
            e.memset(cwp, 0.0).then_inc(s_z, 1)
            tick = m.tick[:, 5:12]
            e.memset(tick, 0.0).then_inc(s_z, 1)
            e.wait_ge(s_z, 4)

            def bear(k):
                e.tensor_tensor(tick[:, k:k + 1], tick[:, 0:1], tick[:, 0:1], ALU.add)

            def gates(q, h, part):
                half = slice(N5 * h, N5 * h + N5)
                if part == 0:
                    e.wait_ge(s_g, q + 1)
                    bear(1)
                    e.tensor_scalar(gN[:, half], gT, 0.5, 0.5, ALU.mult, ALU.add).then_inc(s_gl, 1)
                elif part == 1:
                    e.wait_ge(s_gl, 2 * q + 1)
                    bear(3)
                    e.tensor_tensor(tmp, gN[:, half], inpN[:, half], ALU.mult).then_inc(s_gl, 1)
                else:
                    e.wait_ge(s_gl, 2 * q + 2)
                    bear(5)
                    e.tensor_tensor(CN[:, half], inpN[:, half], tmp, ALU.subtract).then_inc(s_c, 1)

            def low(turn, ch):
                g_ = turn[0]
                e.wait_ge(s_hh, 4 * g_ + ch + 1)
                wait(e, s_w3, 4 * g_ + ch - 3)
                e.tensor_tensor(hl[ch], hb[ch % 2], hh[ch], ALU.subtract).then_inc(s_hl, 1)

            def summed(turn):
                g_, span, h, x = turn
                e.wait_ge(s_ys, g_ + 1)
                e.wait_ge(s_xb, 2 * span + 2)
                wait(e, s_yd, g_)
                bear(2)
                xh = m.X[:, bass.ds(B * span + HALF * h, HALF), :]
                e.tensor_tensor(xh, xh, yw.rearrange("p (b n) -> p b n", b=HALF), ALU.add).then_inc(s_yd, 1)

            def round_(j, scan, late, turns, ahead):
                def power():
                    e.wait_ge(s_mo, MOMENTS * j)
                    e.tensor_tensor(m.rstd4, m.mv4[:, :, 1], m.nhalf[:, 0:B], ALU.pow).then_inc(s_rs, 1)

                def bias():
                    e.wait_ge(s_n3, 2 * j + 2)
                    bear(6)
                    u8 = m.X[:, bass.ds(B * j, B), :]
                    e.tensor_tensor(u8, u8, m.bout[:, :].rearrange("p (o n) -> p o n", o=1).broadcast_to([P, B, D]), ALU.add).then_inc(s_bo, 1)

                def place(n, now, before):
                    if before:
                        low(before, NC4 - 1)
                    if now:
                        low(now, 0)
                    if now:
                        low(now, 1)
                    if n == 0 and turns:
                        power()
                    if before:
                        summed(before)
                    if now:
                        low(now, 2)
                    if n == LATE and scan:
                        bias()
                    for h, first in enumerate(GATED):
                        if ahead and first <= n < first + 3:
                            gates(2 * (j + 1) + h, h, n - first)

                places(e, j, late, turns, place)

            for h in range(2):
                for part in range(3):
                    gates(h, h, part)
            rounds(e, round_)
            round_(NJ + 1, False, True, False, False)
            low((TURNS * NJ - 1,), NC4 - 1)
            summed((TURNS * NJ - 1, NJ - 1, 1, E - 1))

        @block.vector
        def _(e):
            e.wait_ge(s_z, 4)
            e.memset(m.tick[:, 0:5], 0.0).then_inc(s_tk, 1)
            e.wait_ge(s_tk, 1)

            def tick(k=1):
                e.tensor_copy(m.tick[:, k:k + 1], m.tick[:, 0:1])

            def normed(j, q, h, b):
                u = B * j + HALF * h + b
                if b == 0:
                    wait(e, s_t3, q)
                last = e.tensor_scalar(n3[:, b, :], m.X[:, u, :], m.mv[:, u, 0:1], m.rstd[:, bass.ds(u, 1)], ALU.subtract, ALU.mult)
                if b == HALF - 1:
                    last.then_inc(s_n3, 1)

            def step(j, t, k):
                e.wait_ge(s_th, P * j + t + 1)
                if isinstance(t, int) and t == 0:
                    e.wait_ge(s_gc, j + 1)
                e.tensor_tensor(R[:, :, bass.ds(t + 1, 1)].rearrange("p b o -> p (b o)"), th[k],
                                gv[:, :, bass.ds(t, 1)].rearrange("p b o -> p (b o)"), ALU.mult).then_inc(s_r, 1)

            def start(j, scan, post):
                if post:
                    e.wait_ge(s_r, P * j)
                    wait(e, s_po, 2 * (j - 1))
                    wait(e, s_cb, j)
                    e.tensor_tensor(Sx, R[:, :, 1:P + 1], Cb[:, :, 1:P + 1], ALU.add).then_inc(s_S, 1)
                if scan:
                    if post:
                        e.tensor_copy(Cb[:, :, 0:1], Cb[:, :, P:P + 1])
                        e.tensor_copy(R[:, :, 0:1], R[:, :, P:P + 1]).then_inc(s_k2, 1)
                        e.wait_ge(s_k2, j)
                        e.wait_ge(s_S, j)
                    e.wait_ge(s_c, 2 * j + 2)
                    e.tensor_copy(Cb[:, :, 1:P + 1], CN.rearrange("p (b t) -> p b t", b=B)).then_inc(s_cb, 1)

            def weighed(turn):
                g_, span, h, x = turn
                e.wait_ge(s_w3, 4 * g_ + 4)
                wait(e, s_yd, g_)
                e.wait_ge(s_cc, span + 1)
                share = cw[:, HALF * h:HALF * h + HALF, x:x + 1].broadcast_to([P, HALF, D])
                e.tensor_tensor(yw.rearrange("p (b n) -> p b n", b=HALF), bY.rearrange("p (b n) -> p b n", b=HALF), share,
                                ALU.mult).then_inc(s_ys, 1)

            def ending(p, late):
                n = [0]
                iota = m.iota8[:, :].rearrange("p (o n) -> p o n", o=1).broadcast_to([P, B, E])

                def link(ins):
                    ins.then_inc(s_k, 1)
                    n[0] += 1
                    e.wait_ge(s_k, KP * p + n[0])

                def residual(h):
                    if h == 0:
                        e.wait_ge(s_bo, p + 1)
                    e.wait_ge(s_po, 2 * p + h + 1)
                    xh = m.X[:, bass.ds(B * p + HALF * h, HALF), :]
                    e.tensor_tensor(xh, xh, bZ.rearrange("p (b n) -> p b n", b=HALF), ALU.add).then_inc(s_xo, 1)

                def stat(h):
                    e.wait_ge(s_xo, 2 * p + h + 1)
                    tick(2 + h)
                    for b in range(HALF * h, HALF * h + HALF):
                        last = e.bn_stats(m.st4[:, b, :], m.X[:, B * p + b, :])
                    if h:
                        link(last)

                def norm4(h):
                    if h == 0:
                        e.wait_ge(s_rs, p + 1)
                    for b in range(HALF * h, HALF * h + HALF):
                        last = e.tensor_scalar(n4[:, b, :], m.X[:, B * p + b, :], m.mv4[:, b, 0:1], m.rstd4[:, b:b + 1], ALU.subtract, ALU.mult)
                    last.then_inc(s_n4, 1)

                def low4(h):
                    half = slice(N5 * h, N5 * h + N5)
                    e.wait_ge(s_x4h, 2 * p + h + 1)
                    e.wait_ge(s_x4f, 2 * p + h + 1)
                    e.tensor_tensor(x4l[:, half], x4f[:, half], x4h[:, half], ALU.subtract).then_inc(s_x4, 1)

                def best():
                    e.wait_ge(s_pr, p + 1)
                    link(e.tensor_tensor(lg, bZ[:, 0:B * E].rearrange("p (b e) -> p b e", b=B),
                                         m.br[:, :].rearrange("p (o n) -> p o n", o=1).broadcast_to([P, B, E]), ALU.add))
                    tick()
                    for b in range(B):
                        last = e.max(mx8[:, b, :], lg[:, b, :])
                    link(last)

                def which():
                    e.tensor_tensor(ws[:, :, 1], mx8[:, :, 0], mx8[:, :, 1], ALU.subtract).then_inc(s_d, 1)
                    for b in range(B):
                        last = e.max_index(ix[:, b, :], mx8[:, b, :], lg[:, b, :])
                    link(last)

                def match():
                    link(e.tensor_copy(ixf, ix[:, :, 0:2]))
                    for k in range(2):
                        last = e.tensor_tensor(eq[k], iota, ixf[:, :, k:k + 1].broadcast_to([P, B, E]), ALU.is_equal)
                    link(last)

                def shares():
                    e.wait_ge(s_w, p + 1)
                    link(e.tensor_scalar(ws[:, :, 1], ws[:, :, 0], -0.5, 0.5, ALU.mult, ALU.add))
                    link(e.tensor_scalar(ws[:, :, 0], ws[:, :, 0], 0.5, 0.5, ALU.mult, ALU.add))
                    for k in range(2):
                        last = e.tensor_tensor(eq[k], eq[k], ws[:, :, k:k + 1].broadcast_to([P, B, E]), ALU.mult)
                    link(last)
                    wait(e, s_tc, p)
                    wait(e, s_cc, p)
                    e.tensor_tensor(cwN, eq[0], eq[1], ALU.add).then_inc(s_cw, 1)
                    assert n[0] == KP, n[0]

                def biased(h):
                    e.wait_ge(s_pb, 2 * p + h + 1)
                    xh = m.X[:, bass.ds(B * p + HALF * h, HALF), :]
                    e.tensor_tensor(xh, xh, bZ.rearrange("p (b n) -> p b n", b=HALF), ALU.add).then_inc(s_xb, 1)

                def move():
                    e.wait_ge(s_cw, p + 1)
                    wait(e, s_ys, TURNS * p)
                    e.tensor_copy(cw, cwN).then_inc(s_cc, 1)

                return {0: lambda: residual(0), 3: lambda: (residual(1), stat(0)), 4: lambda: stat(1),
                        5: lambda: moments(e, s_mo, MOMENTS * p, m.st4[:, :, :], m.mv4[:, :, 0], m.mv4[:, :, 1]),
                        7: lambda: norm4(0), 8: lambda: norm4(1), 11: lambda: low4(0), 14: best, 15: which, 16: match,
                        18: shares, 22: lambda: biased(0), 24: lambda: biased(1), STEPS * LATE + 5: move,
                        STEPS * LATE + 6: lambda: low4(1)}

            def round_(j, scan, late, turns, ahead):
                start(j, scan, turns)
                beside = ending(j - 1, late) if turns else {}

                def place(n, now, before):
                    for s in range(STEPS):
                        if scan:
                            step(j, STEPS * n + s, s % 2)
                        if STEPS * n + s in beside:
                            beside[STEPS * n + s]()
                        if ahead and n in NORMED and s % 2 == 0:
                            h = NORMED.index(n)
                            normed(j + 1, 2 * (j + 1) + h, h, s // 2)
                        if now and s % 2 == 1:
                            g_, span, h, x = now
                            ch = s // 2
                            e.wait_ge(s_b, 4 * g_ + ch + 1)
                            e.wait_ge(s_sa, 4 * g_ + ch + 1)
                            wait(e, s_hl, 4 * g_ + ch - 1)
                            e.scalar_tensor_tensor(hb[ch % 2], bB[ch % 2], m.b12[:, 1, ch, x:x + 1], sa[ch % 2],
                                                   ALU.add, ALU.mult).then_inc(s_h, 1)
                        if before and s == 2 * DEEP:
                            weighed(before)

                places(e, j, late, turns, place)

            for h in range(2):
                for b in range(HALF):
                    normed(0, h, h, b)
            rounds(e, round_)
            round_(NJ + 1, False, True, False, False)
            weighed((TURNS * NJ - 1, NJ - 1, 1, E - 1))

        @block.sync
        def _(e):
            with e.Fori(0, NJ) as j:
                e.wait_ge(s_yd, 16 * (j + 1))
                e.dma_start(m.out[:, bass.ds(P * j, P), :].rearrange("b p f -> p b f"), m.X[:, bass.ds(B * j, B), :]).then_inc(s_out, 16)
            e.wait_ge(s_out, 16 * NJ)


STAGES = (setup, norm_all, local_attention, latent_attention, ffn, scan_and_experts)


def mixer_moe(nc, arrays, out, stages=STAGES, dump=None):
    with ExitStack() as ctx:
        m = lay_out(nc, ctx)
        m.out = out
        a = Arrays(arrays)
        for stage in stages:
            stage(nc, ctx, m, a)
        if dump:
            dump(nc, ctx, m)


_INS = {"x": "L0_attn_x", "wq": "L0_attn_wq", "wk": "L0_attn_wk", "wv": "L0_attn_wv", "wgq": "L0_attn_wgq",
        "wgk": "L0_attn_wgk", "wgv": "L0_attn_wgv", "r_out_w": "L0_attn_r_out_w",
        "gate_local_w": "L0_attn_gate_local_w", "gate_remote_w": "L0_attn_gate_remote_w", "w_out": "L0_attn_w_out",
        "f_kernel": "L0_ffn_kernel", "f_sin": "L0_ffn_input_scale", "f_sk": "L0_ffn_kernel_scale",
        "f_bias": "L0_ffn_bias", "A": "L1_attn_A", "B": "L1_attn_B", "W_in": "L1_attn_W_in", "b_in": "L1_attn_b_in",
        "W_gate": "L1_attn_W_gate", "b_gate": "L1_attn_b_gate", "W_out": "L1_attn_W_out", "b_out": "L1_attn_b_out",
        "Wr": "L1_ffn_Wr", "br": "L1_ffn_br", "W1": "L1_ffn_W1", "b1": "L1_ffn_b1", "W2": "L1_ffn_W2",
        "b2": "L1_ffn_b2", "W3": "L1_ffn_W3", "b3": "L1_ffn_b3"}


def kernel(**inputs):
    import numpy as _np
    import concourse.bacc as _bacc
    from concourse import mybir as _mybir
    from concourse.bass_utils import run_bass_kernel_spmd as _run

    nc = _bacc.Bacc("TRN2", target_bir_lowering=False, num_devices=1)
    arrays, aps = {}, []
    for short, name in _INS.items():
        v = _np.ascontiguousarray(inputs[name])
        arrays[f"in_{short}"] = v
        aps.append(nc.dram_tensor(f"in_{short}", v.shape, _mybir.dt.from_np(v.dtype), kind="ExternalInput").ap())
    out = nc.dram_tensor("out_0", (B, S, D), _mybir.dt.float32, kind="ExternalOutput").ap()
    mixer_moe(nc, aps, out)
    r = _run(nc, [arrays], core_ids=[0])
    return r.results[0]["out_0"]
```
